# Optimizing a Trainium2 kernel written in Bass

```python
import numpy as np
import jax
import jax.numpy as jnp

def _softmax(x, axis=-1):
    return jax.nn.softmax(x, axis=axis)

def _gelu(x):
    return jax.nn.gelu(x, approximate=True)

def _silu(x):
    return jax.nn.silu(x)

def _sigmoid(x):
    return jax.nn.sigmoid(x)

def _layernorm(x, axis=-1, eps=1e-05):
    m = jnp.mean(x, axis=axis, keepdims=True)
    v = jnp.var(x, axis=axis, keepdims=True)
    return (x - m) / jnp.sqrt(v + eps)

def _scatter_add(tgt, idx, src, axis=0):
    return tgt.at[idx].add(src)

def _segment_sum(src, seg, n):
    return jax.ops.segment_sum(src, seg, n)
kernel_name = 'mk_audio_tower_d2_tok_audfeat256_r4_e3d6ae'

def setup_inputs(seed: int=0):
    np.random.seed(seed)
    _w = jnp.asarray

    def _rec_inputs():
        import jax
        import jax.numpy as jnp
        _rk = jax.random.key(seed)
        x = -0.00197248 + 1.00072 * jax.random.normal(jax.random.fold_in(_rk, 1), (64, 1, 10240), jnp.float32)
        return x
    x = _rec_inputs()

    def _L0_tok_setup():
        import jax, jax.numpy as jnp
        import numpy as np
        B, L = (4, 10240)
        C = 128
        DMLP = 512
        TEMP = 1e-05
        EPS = 1e-05
        FACTOR = 2

        def _conv(x, w, b, stride, pad):
            x = jnp.pad(x, ((0, 0), (0, 0), (pad, pad)), mode='reflect')
            y = jax.lax.conv_general_dilated(x, w, (stride,), 'VALID', dimension_numbers=('NCH', 'OIH', 'NCH'))
            return y + b[None, :, None]

        def _cnorm(x, g, b):
            m = jnp.mean(x, axis=1, keepdims=True)
            v = jnp.var(x, axis=1, keepdims=True, ddof=1)
            return (x - m) * jax.lax.rsqrt(v + EPS) * g[None, :, None] + b[None, :, None]

        def _forward(x, conv0_w, conv0_b, conv1_w, conv1_b, conv2_w, conv2_b, conv3_w, conv3_b, n0_w, n0_b, n1_w, n1_b, n2_w, n2_b, n3_w, n3_b, n4_w, n4_b, mlp_w1, mlp_b1, mlp_w2, mlp_b2, mlp_w3, mlp_b3):
            h = jax.nn.relu(_cnorm(_conv(x, conv0_w, conv0_b, 5, 3), n0_w, n0_b))
            h = jax.nn.relu(_cnorm(_conv(h, conv1_w, conv1_b, 4, 2), n1_w, n1_b))
            h = jax.nn.relu(_cnorm(_conv(h, conv2_w, conv2_b, 2, 1), n2_w, n2_b))
            h = jax.nn.relu(_cnorm(_conv(h, conv3_w, conv3_b, 2, 1), n3_w, n3_b))
            f = jnp.transpose(h, (0, 2, 1))
            T = f.shape[1]
            z = jax.nn.gelu(f @ mlp_w1 + mlp_b1, approximate=False)
            z = jax.nn.gelu(z @ mlp_w2 + mlp_b2, approximate=False)
            imp = jax.nn.sigmoid((z @ mlp_w3 + mlp_b3)[..., 0]) + TEMP
            imp = imp / jnp.sum(imp, axis=1, keepdims=True) * (T / FACTOR)
            Tn = T // FACTOR
            cs = jnp.cumsum(imp, axis=1)
            p = jnp.maximum(cs[:, :, None] - jnp.arange(Tn, dtype=cs.dtype)[None, None, :], 0.0)
            pc = jnp.pad(p, ((0, 0), (0, 0), (0, 1)))
            d = pc[:, :, :-1] - pc[:, :, 1:]
            wmat = d - jnp.pad(d, ((0, 0), (1, 0), (0, 0)))[:, :-1, :]
            pooled = jnp.einsum('btn,btc->bnc', wmat, f)
            out = jnp.transpose(pooled, (0, 2, 1))
            return jax.nn.relu(_cnorm(out, n4_w, n4_b))
        key = jax.random.key(seed)
        ks = jax.random.split(key, 8)

        def w(k, shape, fan_in):
            return jax.random.normal(k, shape, jnp.float32) / np.float32(np.sqrt(fan_in))
        inp = {'x': jax.random.normal(ks[0], (B, 1, L), jnp.float32), 'conv0_w': w(ks[1], (C, 1, 10), 10), 'conv0_b': jnp.zeros(C, jnp.float32), 'conv1_w': w(ks[2], (C, C, 8), C * 8), 'conv1_b': jnp.zeros(C, jnp.float32), 'conv2_w': w(ks[3], (C, C, 4), C * 4), 'conv2_b': jnp.zeros(C, jnp.float32), 'conv3_w': w(ks[4], (C, C, 4), C * 4), 'conv3_b': jnp.zeros(C, jnp.float32), 'mlp_w1': w(ks[5], (C, DMLP), C), 'mlp_b1': jnp.zeros(DMLP, jnp.float32), 'mlp_w2': w(ks[6], (DMLP, DMLP), DMLP), 'mlp_b2': jnp.zeros(DMLP, jnp.float32), 'mlp_w3': w(ks[7], (DMLP, 1), DMLP), 'mlp_b3': jnp.zeros(1, jnp.float32)}
        for i in range(5):
            inp[f'n{i}_w'] = jnp.ones(C, jnp.float32)
            inp[f'n{i}_b'] = jnp.zeros(C, jnp.float32)
        return inp
    _L0_tok_all = _L0_tok_setup()
    _L0_tok_in = {k: v for k, v in _L0_tok_all.items() if k in ('conv0_w', 'conv0_b', 'conv1_w', 'conv1_b', 'conv2_w', 'conv2_b', 'conv3_w', 'conv3_b', 'n0_w', 'n0_b', 'n1_w', 'n1_b', 'n2_w', 'n2_b', 'n3_w', 'n3_b', 'n4_w', 'n4_b', 'mlp_w1', 'mlp_b1', 'mlp_w2', 'mlp_b2', 'mlp_w3', 'mlp_b3')}
    del _L0_tok_all

    def _L0_attn_setup():
        import jax, jax.numpy as jnp
        import numpy as np
        N_HEADS, D_MODEL, D_HEAD = (8, 64, 32)
        BATCH, SEQ = (2, 512)
        INIT_RANGE = 0.02

        def _odd_causal_mask(S):
            i = jnp.arange(S)[:, None]
            j = jnp.arange(S)[None, :]
            allowed = (j < i) & (j % 2 == 1) | (i == j)
            return allowed
        key = jax.random.key(seed)
        ks = jax.random.split(key, 6)
        x = jax.random.normal(ks[0], (BATCH, SEQ, D_MODEL), dtype=jnp.float32)
        W_Q = INIT_RANGE * jax.random.normal(ks[1], (N_HEADS, D_MODEL, D_HEAD), dtype=jnp.float32)
        W_K = INIT_RANGE * jax.random.normal(ks[2], (N_HEADS, D_MODEL, D_HEAD), dtype=jnp.float32)
        W_V = INIT_RANGE * jax.random.normal(ks[3], (N_HEADS, D_MODEL, D_HEAD), dtype=jnp.float32)
        W_O = INIT_RANGE * jax.random.normal(ks[4], (N_HEADS, D_HEAD, D_MODEL), dtype=jnp.float32)
        b_Q = jnp.zeros((N_HEADS, D_HEAD), dtype=jnp.float32)
        b_K = jnp.zeros((N_HEADS, D_HEAD), dtype=jnp.float32)
        b_V = jnp.zeros((N_HEADS, D_HEAD), dtype=jnp.float32)
        b_O = jnp.zeros((D_MODEL,), dtype=jnp.float32)
        return {'normalized_resid_pre': x, 'W_Q': W_Q, 'W_K': W_K, 'W_V': W_V, 'W_O': W_O, 'b_Q': b_Q, 'b_K': b_K, 'b_V': b_V, 'b_O': b_O}
    _L0_attn_all = _L0_attn_setup()
    _L0_attn_in = {k: v for k, v in _L0_attn_all.items() if k in ('W_Q', 'W_K', 'W_V', 'W_O', 'b_Q', 'b_K', 'b_V', 'b_O')}
    del _L0_attn_all

    def _L0_ffn_setup():
        import jax, jax.numpy as jnp
        import numpy as np
        DIM = 64
        HEADS = 8
        NUM_KEYS = 64
        NUM_KV = NUM_KEYS ** 2
        PK_TOPK = 16
        FINAL_TOPK = 16
        DIM_KEY = DIM // 2
        P = 2

        def _pk(x, Wq_pk, pk_keys):
            b, n, _ = x.shape
            q = (x @ Wq_pk).reshape(b, n, P, HEADS, DIM_KEY).transpose(2, 0, 1, 3, 4)
            sim = jnp.einsum('pbnhd,pkhd->pbnhk', q, pk_keys)
            scores, idx = jax.lax.top_k(sim, PK_TOPK)
            idx0 = idx[0]
            idx1 = idx[1] * NUM_KEYS
            index = (idx0[..., :, None] + idx1[..., None, :]).reshape(b, n, HEADS, PK_TOPK * PK_TOPK)
            score = (scores[0][..., :, None] + scores[1][..., None, :]).reshape(b, n, HEADS, PK_TOPK * PK_TOPK)
            final_scores, pk_idx = jax.lax.top_k(score, FINAL_TOPK)
            final_indices = jnp.take_along_axis(index, pk_idx, axis=-1)
            final_scores = jax.nn.softmax(final_scores, axis=-1)
            return (final_scores, final_indices)
        key = jax.random.key(seed)
        ks = jax.random.split(key, 7)
        b, n = (2, 256)
        std = 0.02
        x = jax.random.normal(ks[0], (b, n, DIM), dtype=jnp.float32)
        Wq_pk = jax.random.normal(ks[1], (DIM, P * HEADS * DIM_KEY), dtype=jnp.float32) * std
        pk_keys = jax.random.normal(ks[2], (P, NUM_KEYS, HEADS, DIM_KEY), dtype=jnp.float32) * std
        Wq = jax.random.normal(ks[3], (DIM, HEADS * DIM), dtype=jnp.float32) * std
        keys_table = jax.random.normal(ks[4], (NUM_KV * HEADS, DIM), dtype=jnp.float32) * std
        values_table = jax.random.normal(ks[5], (NUM_KV * HEADS, DIM), dtype=jnp.float32) * std
        Wo = jax.random.normal(ks[6], (DIM * HEADS, DIM), dtype=jnp.float32) * std
        return {'x': x, 'Wq_pk': Wq_pk, 'pk_keys': pk_keys, 'Wq': Wq, 'keys_table': keys_table, 'values_table': values_table, 'Wo': Wo}
    _L0_ffn_all = _L0_ffn_setup()
    _L0_ffn_in = {k: v for k, v in _L0_ffn_all.items() if k in ('Wq_pk', 'pk_keys', 'Wq', 'keys_table', 'values_table', 'Wo')}
    del _L0_ffn_all

    def _L1_attn_setup():
        import jax, jax.numpy as jnp
        import numpy as np
        MAX_ADAPTIVE_LR = 0.1

        def _l2n(z):
            n = jnp.linalg.norm(z, axis=-1, keepdims=True)
            return z / jnp.maximum(n, 1e-12)

        def _mlp(params, z):
            W0, W1, P0, P1 = params
            h = z @ W0 + z @ P0
            h = jax.nn.silu(h)
            return h @ W1 + h @ P1
        key = jax.random.key(seed)
        kx, kf, kp0, kp1 = jax.random.split(key, 4)
        B, T, H, E = (4, 64, 64, 4)
        D = H * E
        x = jax.random.normal(kx, (B, T, H), dtype=jnp.float32)
        W_fused = jax.random.normal(kf, (3 * H + 3, H), dtype=jnp.float32) / np.sqrt(H).astype(np.float32)
        W0 = jnp.zeros((H, D), dtype=jnp.float32)
        W1 = jnp.zeros((D, H), dtype=jnp.float32)
        P0 = jax.random.normal(kp0, (H, D), dtype=jnp.float32)
        P1 = jax.random.normal(kp1, (D, H), dtype=jnp.float32)
        return {'x': x, 'W_fused': W_fused, 'W0': W0, 'W1': W1, 'P0': P0, 'P1': P1}
    _L1_attn_all = _L1_attn_setup()
    _L1_attn_in = {k: v for k, v in _L1_attn_all.items() if k in ('W_fused', 'W0', 'W1', 'P0', 'P1')}
    del _L1_attn_all

    def _L1_ffn_setup():
        import jax, jax.numpy as jnp
        import numpy as np
        E = 8
        K = 2
        D = 64
        H = 128
        DOUT = 64
        EPS = 1e-05
        key = jax.random.key(seed)
        ks = jax.random.split(key, 9)
        s = 0.02
        return {'x': jax.random.normal(ks[0], (4, 2048, D), jnp.float32), 'gamma': 1.0 + 0.05 * jax.random.normal(ks[1], (D,), jnp.float32), 'beta': 0.05 * jax.random.normal(ks[2], (D,), jnp.float32), 'Wr': 0.01 * jax.random.normal(ks[3], (D, E), jnp.float32), 'br': jnp.zeros((E,), jnp.float32), 'W1': s * jax.random.normal(ks[4], (E, D, H), jnp.float32), 'b1': s * jax.random.normal(ks[5], (E, H), jnp.float32), 'W2': s * jax.random.normal(ks[6], (E, H, DOUT), jnp.float32), 'b2': s * jax.random.normal(ks[7], (E, DOUT), jnp.float32)}
    _L1_ffn_all = _L1_ffn_setup()
    _L1_ffn_in = {k: v for k, v in _L1_ffn_all.items() if k in ('gamma', 'beta', 'Wr', 'br', 'W1', 'b1', 'W2', 'b2')}
    del _L1_ffn_all
    return {'x': x, 'L0_tok_conv0_w': _L0_tok_in['conv0_w'], 'L0_tok_conv0_b': _L0_tok_in['conv0_b'], 'L0_tok_conv1_w': _L0_tok_in['conv1_w'], 'L0_tok_conv1_b': _L0_tok_in['conv1_b'], 'L0_tok_conv2_w': _L0_tok_in['conv2_w'], 'L0_tok_conv2_b': _L0_tok_in['conv2_b'], 'L0_tok_conv3_w': _L0_tok_in['conv3_w'], 'L0_tok_conv3_b': _L0_tok_in['conv3_b'], 'L0_tok_n0_w': _L0_tok_in['n0_w'], 'L0_tok_n0_b': _L0_tok_in['n0_b'], 'L0_tok_n1_w': _L0_tok_in['n1_w'], 'L0_tok_n1_b': _L0_tok_in['n1_b'], 'L0_tok_n2_w': _L0_tok_in['n2_w'], 'L0_tok_n2_b': _L0_tok_in['n2_b'], 'L0_tok_n3_w': _L0_tok_in['n3_w'], 'L0_tok_n3_b': _L0_tok_in['n3_b'], 'L0_tok_n4_w': _L0_tok_in['n4_w'], 'L0_tok_n4_b': _L0_tok_in['n4_b'], 'L0_tok_mlp_w1': _L0_tok_in['mlp_w1'], 'L0_tok_mlp_b1': _L0_tok_in['mlp_b1'], 'L0_tok_mlp_w2': _L0_tok_in['mlp_w2'], 'L0_tok_mlp_b2': _L0_tok_in['mlp_b2'], 'L0_tok_mlp_w3': _L0_tok_in['mlp_w3'], 'L0_tok_mlp_b3': _L0_tok_in['mlp_b3'], 'L0_attn_W_Q': _L0_attn_in['W_Q'], 'L0_attn_W_K': _L0_attn_in['W_K'], 'L0_attn_W_V': _L0_attn_in['W_V'], 'L0_attn_W_O': _L0_attn_in['W_O'], 'L0_attn_b_Q': _L0_attn_in['b_Q'], 'L0_attn_b_K': _L0_attn_in['b_K'], 'L0_attn_b_V': _L0_attn_in['b_V'], 'L0_attn_b_O': _L0_attn_in['b_O'], 'L0_ffn_Wq_pk': _L0_ffn_in['Wq_pk'], 'L0_ffn_pk_keys': _L0_ffn_in['pk_keys'], 'L0_ffn_Wq': _L0_ffn_in['Wq'], 'L0_ffn_keys_table': _L0_ffn_in['keys_table'], 'L0_ffn_values_table': _L0_ffn_in['values_table'], 'L0_ffn_Wo': _L0_ffn_in['Wo'], 'L1_attn_W_fused': _L1_attn_in['W_fused'], 'L1_attn_W0': _L1_attn_in['W0'], 'L1_attn_W1': _L1_attn_in['W1'], 'L1_attn_P0': _L1_attn_in['P0'], 'L1_attn_P1': _L1_attn_in['P1'], 'L1_ffn_gamma': _L1_ffn_in['gamma'], 'L1_ffn_beta': _L1_ffn_in['beta'], 'L1_ffn_Wr': _L1_ffn_in['Wr'], 'L1_ffn_br': _L1_ffn_in['br'], 'L1_ffn_W1': _L1_ffn_in['W1'], 'L1_ffn_b1': _L1_ffn_in['b1'], 'L1_ffn_W2': _L1_ffn_in['W2'], 'L1_ffn_b2': _L1_ffn_in['b2']}

def reference(x, L0_tok_conv0_w, L0_tok_conv0_b, L0_tok_conv1_w, L0_tok_conv1_b, L0_tok_conv2_w, L0_tok_conv2_b, L0_tok_conv3_w, L0_tok_conv3_b, L0_tok_n0_w, L0_tok_n0_b, L0_tok_n1_w, L0_tok_n1_b, L0_tok_n2_w, L0_tok_n2_b, L0_tok_n3_w, L0_tok_n3_b, L0_tok_n4_w, L0_tok_n4_b, L0_tok_mlp_w1, L0_tok_mlp_b1, L0_tok_mlp_w2, L0_tok_mlp_b2, L0_tok_mlp_w3, L0_tok_mlp_b3, L0_attn_W_Q, L0_attn_W_K, L0_attn_W_V, L0_attn_W_O, L0_attn_b_Q, L0_attn_b_K, L0_attn_b_V, L0_attn_b_O, L0_ffn_Wq_pk, L0_ffn_pk_keys, L0_ffn_Wq, L0_ffn_keys_table, L0_ffn_values_table, L0_ffn_Wo, L1_attn_W_fused, L1_attn_W0, L1_attn_W1, L1_attn_P0, L1_attn_P1, L1_ffn_gamma, L1_ffn_beta, L1_ffn_Wr, L1_ffn_br, L1_ffn_W1, L1_ffn_b1, L1_ffn_W2, L1_ffn_b2):
    import jax
    import jax.numpy as jnp

    def _L0_tok_ref(x, conv0_w, conv0_b, conv1_w, conv1_b, conv2_w, conv2_b, conv3_w, conv3_b, n0_w, n0_b, n1_w, n1_b, n2_w, n2_b, n3_w, n3_b, n4_w, n4_b, mlp_w1, mlp_b1, mlp_w2, mlp_b2, mlp_w3, mlp_b3):
        import jax, jax.numpy as jnp
        import numpy as np
        B, L = (4, 10240)
        C = 128
        DMLP = 512
        TEMP = 1e-05
        EPS = 1e-05
        FACTOR = 2

        def _conv(x, w, b, stride, pad):
            x = jnp.pad(x, ((0, 0), (0, 0), (pad, pad)), mode='reflect')
            y = jax.lax.conv_general_dilated(x, w, (stride,), 'VALID', dimension_numbers=('NCH', 'OIH', 'NCH'))
            return y + b[None, :, None]

        def _cnorm(x, g, b):
            m = jnp.mean(x, axis=1, keepdims=True)
            v = jnp.var(x, axis=1, keepdims=True, ddof=1)
            return (x - m) * jax.lax.rsqrt(v + EPS) * g[None, :, None] + b[None, :, None]

        def _forward(x, conv0_w, conv0_b, conv1_w, conv1_b, conv2_w, conv2_b, conv3_w, conv3_b, n0_w, n0_b, n1_w, n1_b, n2_w, n2_b, n3_w, n3_b, n4_w, n4_b, mlp_w1, mlp_b1, mlp_w2, mlp_b2, mlp_w3, mlp_b3):
            h = jax.nn.relu(_cnorm(_conv(x, conv0_w, conv0_b, 5, 3), n0_w, n0_b))
            h = jax.nn.relu(_cnorm(_conv(h, conv1_w, conv1_b, 4, 2), n1_w, n1_b))
            h = jax.nn.relu(_cnorm(_conv(h, conv2_w, conv2_b, 2, 1), n2_w, n2_b))
            h = jax.nn.relu(_cnorm(_conv(h, conv3_w, conv3_b, 2, 1), n3_w, n3_b))
            f = jnp.transpose(h, (0, 2, 1))
            T = f.shape[1]
            z = jax.nn.gelu(f @ mlp_w1 + mlp_b1, approximate=False)
            z = jax.nn.gelu(z @ mlp_w2 + mlp_b2, approximate=False)
            imp = jax.nn.sigmoid((z @ mlp_w3 + mlp_b3)[..., 0]) + TEMP
            imp = imp / jnp.sum(imp, axis=1, keepdims=True) * (T / FACTOR)
            Tn = T // FACTOR
            cs = jnp.cumsum(imp, axis=1)
            p = jnp.maximum(cs[:, :, None] - jnp.arange(Tn, dtype=cs.dtype)[None, None, :], 0.0)
            pc = jnp.pad(p, ((0, 0), (0, 0), (0, 1)))
            d = pc[:, :, :-1] - pc[:, :, 1:]
            wmat = d - jnp.pad(d, ((0, 0), (1, 0), (0, 0)))[:, :-1, :]
            pooled = jnp.einsum('btn,btc->bnc', wmat, f)
            out = jnp.transpose(pooled, (0, 2, 1))
            return jax.nn.relu(_cnorm(out, n4_w, n4_b))
        return _forward(x, conv0_w, conv0_b, conv1_w, conv1_b, conv2_w, conv2_b, conv3_w, conv3_b, n0_w, n0_b, n1_w, n1_b, n2_w, n2_b, n3_w, n3_b, n4_w, n4_b, mlp_w1, mlp_b1, mlp_w2, mlp_b2, mlp_w3, mlp_b3)

    def _L0_attn_ref(normalized_resid_pre, W_Q, W_K, W_V, W_O, b_Q, b_K, b_V, b_O):
        import jax, jax.numpy as jnp
        import numpy as np
        N_HEADS, D_MODEL, D_HEAD = (8, 64, 32)
        BATCH, SEQ = (2, 512)
        INIT_RANGE = 0.02

        def _odd_causal_mask(S):
            i = jnp.arange(S)[:, None]
            j = jnp.arange(S)[None, :]
            allowed = (j < i) & (j % 2 == 1) | (i == j)
            return allowed
        x = normalized_resid_pre
        q = jnp.einsum('bsm,hmd->bshd', x, W_Q) + b_Q
        k = jnp.einsum('bsm,hmd->bshd', x, W_K) + b_K
        v = jnp.einsum('bsm,hmd->bshd', x, W_V) + b_V
        scale = 1.0 / jnp.sqrt(jnp.float32(D_HEAD))
        scores = jnp.einsum('bqhd,bkhd->bhqk', q, k) * scale
        allowed = _odd_causal_mask(scores.shape[-1])
        scores = jnp.where(allowed, scores, -jnp.inf)
        pattern = jax.nn.softmax(scores, axis=-1)
        z = jnp.einsum('bkhd,bhqk->bqhd', v, pattern)
        return jnp.einsum('bqhd,hdm->bqm', z, W_O) + b_O

    def _L0_ffn_ref(x, Wq_pk, pk_keys, Wq, keys_table, values_table, Wo):
        import jax, jax.numpy as jnp
        import numpy as np
        DIM = 64
        HEADS = 8
        NUM_KEYS = 64
        NUM_KV = NUM_KEYS ** 2
        PK_TOPK = 16
        FINAL_TOPK = 16
        DIM_KEY = DIM // 2
        P = 2

        def _pk(x, Wq_pk, pk_keys):
            b, n, _ = x.shape
            q = (x @ Wq_pk).reshape(b, n, P, HEADS, DIM_KEY).transpose(2, 0, 1, 3, 4)
            sim = jnp.einsum('pbnhd,pkhd->pbnhk', q, pk_keys)
            scores, idx = jax.lax.top_k(sim, PK_TOPK)
            idx0 = idx[0]
            idx1 = idx[1] * NUM_KEYS
            index = (idx0[..., :, None] + idx1[..., None, :]).reshape(b, n, HEADS, PK_TOPK * PK_TOPK)
            score = (scores[0][..., :, None] + scores[1][..., None, :]).reshape(b, n, HEADS, PK_TOPK * PK_TOPK)
            final_scores, pk_idx = jax.lax.top_k(score, FINAL_TOPK)
            final_indices = jnp.take_along_axis(index, pk_idx, axis=-1)
            final_scores = jax.nn.softmax(final_scores, axis=-1)
            return (final_scores, final_indices)
        b, n, d = x.shape
        q = (x @ Wq).reshape(b, n, HEADS, DIM) * DIM ** (-0.5)
        kv_scores, indices = _pk(x, Wq_pk, pk_keys)
        offsets = jnp.arange(HEADS, dtype=indices.dtype) * NUM_KV
        ind = indices + offsets[None, None, :, None]
        k = jnp.einsum('bnhk,bnhkd->bnhd', kv_scores, keys_table[ind])
        v = jnp.einsum('bnhk,bnhkd->bnhd', kv_scores, values_table[ind])
        sim = jnp.einsum('bihd,bjhd->bhij', q, k)
        neg = -jnp.finfo(sim.dtype).max
        causal = jnp.tril(jnp.ones((n, n), dtype=bool))
        sim = jnp.where(causal, sim, neg)
        attn = jax.nn.softmax(sim, axis=-1)
        out = jnp.einsum('bhij,bjhd->bhid', attn, v)
        out = out.transpose(0, 2, 1, 3).reshape(b, n, HEADS * DIM)
        return out @ Wo

    def _L1_attn_ref(x, W_fused, W0, W1, P0, P1):
        import jax, jax.numpy as jnp
        import numpy as np
        MAX_ADAPTIVE_LR = 0.1

        def _l2n(z):
            n = jnp.linalg.norm(z, axis=-1, keepdims=True)
            return z / jnp.maximum(n, 1e-12)

        def _mlp(params, z):
            W0, W1, P0, P1 = params
            h = z @ W0 + z @ P0
            h = jax.nn.silu(h)
            return h @ W1 + h @ P1
        B, T, H = x.shape
        fp = x @ W_fused.T
        q, k, v, alpha, theta, eta = jnp.split(fp, [H, 2 * H, 3 * H, 3 * H + 1, 3 * H + 2], axis=-1)
        q = _l2n(jax.nn.silu(q))
        k = _l2n(jax.nn.silu(k))
        v = jax.nn.silu(v)
        alpha = jax.nn.sigmoid(alpha)
        theta = jax.nn.sigmoid(theta) * MAX_ADAPTIVE_LR
        eta = jax.nn.sigmoid(eta)
        params0 = (W0, W1, P0, P1)
        bat = lambda p: jnp.broadcast_to(p[None], (B,) + p.shape)
        cur_p = jax.tree_util.tree_map(bat, params0)
        cur_m = jax.tree_util.tree_map(jnp.zeros_like, cur_p)

        def loss_fn(params, kk, vv):
            pred = _mlp(params, kk)
            return jnp.mean((pred - vv) ** 2)

        def step(carry, xs):
            cp, cm = carry
            k_t, v_t, q_t, a_t, th_t, e_t = xs
            g = jax.vmap(jax.grad(loss_fn))(cp, k_t, v_t)
            s = lambda c: c[:, :, None]
            nm = jax.tree_util.tree_map(lambda m, gg: m * s(e_t) - s(th_t) * gg, cm, g)
            np_ = jax.tree_util.tree_map(lambda p, m: p * (1.0 - s(a_t)) + m, cp, nm)
            out_t = jax.vmap(_mlp, in_axes=(0, 0))(np_, q_t)
            new_carry = jax.lax.stop_gradient((np_, nm))
            return (new_carry, out_t)
        tT = lambda a: jnp.swapaxes(a, 0, 1)
        xs = tuple(map(tT, (k, v, q, alpha, theta, eta)))
        _, ys = jax.lax.scan(step, (cur_p, cur_m), xs)
        return jnp.swapaxes(ys, 0, 1)

    def _L1_ffn_ref(x, gamma, beta, Wr, br, W1, b1, W2, b2):
        import jax, jax.numpy as jnp
        import numpy as np
        E = 8
        K = 2
        D = 64
        H = 128
        DOUT = 64
        EPS = 1e-05
        mu = jnp.mean(x, axis=-1, keepdims=True)
        var = jnp.mean(jnp.square(x - mu), axis=-1, keepdims=True)
        xn = (x - mu) * jax.lax.rsqrt(var + EPS) * gamma + beta
        logits = jnp.einsum('bsd,de->bse', xn, Wr) + br
        top_vals, top_idx = jax.lax.top_k(logits, K)
        w = jax.nn.softmax(top_vals, axis=-1)
        w_full = jnp.einsum('bsk,bske->bse', w, jax.nn.one_hot(top_idx, E, dtype=w.dtype))
        y = jnp.zeros(x.shape[:-1] + (DOUT,), x.dtype)
        for e in range(E):
            h = jax.nn.gelu(jnp.einsum('bsd,dh->bsh', xn, W1[e]) + b1[e], approximate=False)
            y_e = jnp.einsum('bsh,hd->bsd', h, W2[e]) + b2[e]
            y = y + y_e * w_full[..., e, None]
        return y
    h = _L0_tok_ref(x, L0_tok_conv0_w, L0_tok_conv0_b, L0_tok_conv1_w, L0_tok_conv1_b, L0_tok_conv2_w, L0_tok_conv2_b, L0_tok_conv3_w, L0_tok_conv3_b, L0_tok_n0_w, L0_tok_n0_b, L0_tok_n1_w, L0_tok_n1_b, L0_tok_n2_w, L0_tok_n2_b, L0_tok_n3_w, L0_tok_n3_b, L0_tok_n4_w, L0_tok_n4_b, L0_tok_mlp_w1, L0_tok_mlp_b1, L0_tok_mlp_w2, L0_tok_mlp_b2, L0_tok_mlp_w3, L0_tok_mlp_b3)
    h = h + _L0_attn_ref(_layernorm(h, axis=-1), L0_attn_W_Q, L0_attn_W_K, L0_attn_W_V, L0_attn_W_O, L0_attn_b_Q, L0_attn_b_K, L0_attn_b_V, L0_attn_b_O)
    h = h + _L0_ffn_ref(_layernorm(h, axis=-1), L0_ffn_Wq_pk, L0_ffn_pk_keys, L0_ffn_Wq, L0_ffn_keys_table, L0_ffn_values_table, L0_ffn_Wo)
    h = h + _L1_attn_ref(_layernorm(h, axis=-1), L1_attn_W_fused, L1_attn_W0, L1_attn_W1, L1_attn_P0, L1_attn_P1)
    h = h + _L1_ffn_ref(_layernorm(h, axis=-1), L1_ffn_gamma, L1_ffn_beta, L1_ffn_Wr, L1_ffn_br, L1_ffn_W1, L1_ffn_b1, L1_ffn_W2, L1_ffn_b2)
    return h

_drawn_inputs = setup_inputs


def setup_inputs(seed=0):
    import zlib

    import numpy as np

    out = dict(_drawn_inputs(seed))
    spreads = {'L0_tok_conv0_b': (0.0, 0.1),
     'L0_tok_conv1_b': (0.0, 0.1),
     'L0_tok_conv2_b': (0.0, 0.1),
     'L0_tok_conv3_b': (0.0, 0.1),
     'L0_tok_n0_w': (1.0, 0.2),
     'L0_tok_n0_b': (0.0, 0.1),
     'L0_tok_n1_w': (1.0, 0.2),
     'L0_tok_n1_b': (0.0, 0.1),
     'L0_tok_n2_w': (1.0, 0.2),
     'L0_tok_n2_b': (0.0, 0.1),
     'L0_tok_n3_w': (1.0, 0.2),
     'L0_tok_n3_b': (0.0, 0.1),
     'L0_tok_n4_w': (1.0, 0.2),
     'L0_tok_n4_b': (0.0, 0.1),
     'L0_tok_mlp_b1': (0.0, 0.358),
     'L0_tok_mlp_b2': (0.0, 0.1),
     'L0_attn_b_Q': (0.0, 0.8),
     'L0_attn_b_K': (0.0, 0.8),
     'L0_attn_b_V': (0.0, 0.1),
     'L0_attn_b_O': (0.0, 0.1),
     'L1_attn_W0': (0.0, 0.279),
     'L1_attn_W1': (0.0, 0.273),
     'L1_ffn_br': (0.0, 0.498)}
    factors = {'L0_attn_W_Q': 8.0,
     'L0_attn_W_K': 8.0,
     'L0_ffn_Wq_pk': 8.0,
     'L0_ffn_pk_keys': 8.0,
     'L0_ffn_Wq': 8.0,
     'L0_ffn_keys_table': 8.0,
     'L0_ffn_values_table': 8.0,
     'L0_ffn_Wo': 8.0,
     'L1_ffn_gamma': 8.0,
     'L1_ffn_beta': 8.0,
     'L1_ffn_Wr': 4.248,
     'L1_ffn_W1': 4.222,
     'L1_ffn_b1': 8.0,
     'L1_ffn_W2': 4.142,
     'L1_ffn_b2': 4.071}
    for name, (base, spread) in spreads.items():
        noise = np.random.default_rng([zlib.crc32(name.encode()), seed]).standard_normal(out[name].shape)
        drawn = base * np.exp(spread * noise) if base else spread * noise
        out[name] = jnp.asarray(drawn.astype(out[name].dtype))
    for name, factor in factors.items():
        out[name] = (out[name] * factor).astype(out[name].dtype)
    return out
```

```python
import concourse.bass as bass
from concourse import mybir
from contextlib import ExitStack

F32 = mybir.dt.float32
U32 = mybir.dt.uint32
ALU = mybir.AluOpType
ACT = mybir.ActivationFunctionType
AX = mybir.AxisListType
EPS = 1e-5

NB = 64
C = 128
D = 64
LEN0, LEN1, LEN2, LEN3 = 2048, 512, 256, 128
DMLP = 512
HEADS, DH = 8, 32
NKEY, NKV, TOPK = 64, 4096, 16
HID = 256
EXPERTS, DFF = 8, 128
BIG = 1.0e30


class Signal:

    def __init__(self, nc, ctx, name, per, by=1, seeded=True):
        self.sem, self.per, self.by = ctx.enter_context(nc.semaphore(name)), per, by
        self.lead = per if seeded else 0

    def seed(self, e):
        e.sem_inc(self.sem, self.lead * self.by)

    def up(self):
        return self.sem, self.by

    def now(self, i, j=None):
        j = self.per - 1 if j is None else j
        return self.sem, (i * self.per + (self.lead + j + 1)) * self.by

    def prev(self, i, j=None):
        j = self.per - 1 if j is None else j
        assert self.lead
        return self.sem, (i * self.per + (j + 1)) * self.by


class Steps:

    def __init__(self, nc, ctx, name):
        self.sem, self.base, self.n = ctx.enter_context(nc.semaphore(name)), 0, 0

    def turn(self, i, per):
        self.base, self.per, self.n0 = i * per, per, self.n

    def end(self):
        assert self.n - self.n0 == self.per, (self.n - self.n0, self.per)

    def up(self):
        self.n += 1
        return self.sem, 1

    def done(self):
        return self.sem, self.base + self.n

    def leave(self, turns):
        self.base = 0
        self.n = self.n0 + turns * self.per


class Core:

    def __init__(self, nc, ctx, ins, out):
        self.nc, self.ctx, self.ins, self.out = nc, ctx, ins, out
        self.gates = {n: ctx.enter_context(nc.semaphore(f"{n}_passed_wait")) for n in
                      ("tensor", "vector", "scalar", "gpsimd", "sync")}
        self.resid = ctx.enter_context(nc.sbuf_tensor("resid", [C, NB * D], F32))
        self.ident = ctx.enter_context(nc.sbuf_tensor("ident", [128, 128], F32))

    def wait(self, name, e, sem, value):
        e.wait_ge(sem, value)
        e.sem_inc(self.gates[name], 1)


def spread(ap, axis, n):
    a = ap.unsqueeze(axis)
    shape = list(a.shape)
    shape[axis] = n
    return a.to_broadcast(shape)


class Stage:

    def __init__(self, k, name):
        self.k, self.nc, self.ctx, self.sems, self.name = k, k.nc, ExitStack(), [], name

    def __enter__(self):
        return self

    def sb(self, name, shape, dt=F32):
        return self.ctx.enter_context(self.nc.sbuf_tensor(f"{self.name}_{name}", shape, dt))

    def ps(self, name, shape):
        return self.ctx.enter_context(self.nc.psum_tensor(f"{self.name}_{name}", shape, F32))

    def sem(self, name):
        s = self.ctx.enter_context(self.nc.semaphore(f"{self.name}_{name}"))
        self.sems.append(s)
        return s

    def sig(self, name, per, by=1, seeded=True):
        s = Signal(self.nc, self.ctx, f"{self.name}_{name}", per, by, seeded)
        self.sems.append(s.sem)
        return s

    def steps(self, name):
        s = Steps(self.nc, self.ctx, f"{self.name}_{name}")
        self.sems.append(s.sem)
        return s

    def block(self):
        self.blk = ExitStack()
        return self.blk.enter_context(self.nc.Block())

    def __exit__(self, *a):
        if a[0] is None:
            self.blk.close()
            for s in self.sems:
                self.nc.sync.sem_clear(s)
            self.nc.all_engine_barrier()
            self.ctx.close()


def make_constants(k):
    nc = k.nc
    with Stage(k, "const") as st:
        made = st.sem("ident_made")
        block = st.block()

        @block.gpsimd
        def _(e):
            e.memset(k.ident[:, :], 0.0).then_inc(made, 1)
            e.wait_ge(made, 1)
            e.affine_select(out=k.ident[:, :], in_=k.ident[:, :], compare_op=ALU.not_equal, fill=1.0,
                            base=0, pattern=[[-1, 128]], channel_multiplier=1).then_inc(made, 1)
            e.wait_ge(made, 2)


def conv_stack(k, feats):
    nc, ins = k.nc, k.ins
    with Stage(k, "conv") as st:
        sb = st.sb
        ps = st.ps
        sig = st.sig
        w0 = sb("w0", [10, C])
        w1, w2, w3 = sb("w1", [C, 8, C]), sb("w2", [C, 4, C]), sb("w3", [C, 4, C])
        s0, ssum = sb("s0", [10, 1]), sb("ssum", [C, 16])
        bias, biasc, gamma, beta = sb("bias", [C, 4]), sb("biasc", [C, 4]), sb("gamma", [C, 5]), sb("beta", [C, 5])
        cent, avg = sb("cent", [C, C]), sb("avg", [C, C])
        xcol = sb("xcol", [10, LEN0])
        h0, h1, h2 = sb("h0", [C, LEN0 + 4]), sb("h1", [C, LEN1 + 2]), sb("h2", [C, LEN2 + 2])
        sq, root, normal = sb("sq", [C, 2, 512]), sb("root", [C, 2, 512]), sb("normal", [C, 2, 512])
        inv = sb("inv", [C, 2, 512])
        epsc = sb("epsc", [C, 1])
        py = ps("py", [C, 4, 512])
        pv = ps("pv", [C, 2, 512])
        pz, pzv = ps("pz", [C, 512]), ps("pzv", [C, 512])
        loaded = st.sem("weights_loaded")
        ready = st.sem("weights_centred")
        bias_mm = st.sem("bias_product")
        own = st.steps("vector_conv_steps")
        xin = sig("x_loaded", 1, 32)
        conv, var = sig("conv_done", 7), sig("variance_done", 7)
        squared, rooted, relued = sig("squared", 7), sig("rooted", 7), sig("relu_done", 7)
        normed, padded = sig("normed", 7), sig("padded", 8)
        width = [512] * 4 + [LEN1, LEN2, LEN3]
        yb = [py[:, q, :] for q in range(4)] + [pz[:, 0:LEN1], pz[:, 0:LEN2], pz[:, 0:LEN3]]
        vb = [pv[:, q % 2, :] for q in range(4)] + [pzv[:, 0:LEN1], pzv[:, 0:LEN2], pzv[:, 0:LEN3]]
        lay = [0, 0, 0, 0, 1, 2, 3]
        block = st.block()

        @block.sync
        def _(e):
            for t, n in ((w0, "conv0"), (w1, "conv1"), (w2, "conv2"), (w3, "conv3"), (bias, "conv_b"),
                         (gamma, "norm_g"), (beta, "norm_b")):
                e.dma_start(t[:], ins[n]).then_inc(loaded, 16)
            xin.seed(e)
            x = ins["x"]
            e.dma_start(xcol[0:5, :], x[0, :, 0:LEN0]).then_inc(xin.sem, 16)
            e.dma_start(xcol[5:10, :], x[0, :, 1:LEN0 + 1]).then_inc(xin.sem, 16)
            with e.Fori(0, NB - 1) as i:
                e.wait_ge(*conv.now(i, 3))
                xi = x[bass.ds(i + 1, 1), :, :].rearrange("o r t -> (o r) t")
                e.dma_start(xcol[0:5, :], xi[:, 0:LEN0]).then_inc(xin.sem, 16)
                e.dma_start(xcol[5:10, :], xi[:, 1:LEN0 + 1]).then_inc(xin.sem, 16)

        @block.tensor
        def _(e):
            conv.seed(e)
            var.seed(e)
            e.wait_ge(ready, 1)
            nc.tensor.matmul(pz[:, 0:4], cent[:, :], bias[:, :], start=True, stop=True).then_inc(bias_mm, 1)
            e.wait_ge(ready, 2)
            with e.Fori(0, NB) as i:
                k.wait("tensor", e, *xin.now(i))
                for q in range(4):
                    k.wait("tensor", e, *normed.prev(i, q))
                    nc.tensor.matmul(yb[q], w0[:, :], xcol[:, q * 512:(q + 1) * 512],
                                     start=True, stop=True).then_inc(*conv.up())

                def variance(q):
                    k.wait("tensor", e, *squared.now(i, q))
                    if 2 <= q < 4:
                        k.wait("tensor", e, *rooted.now(i, q - 2))
                    nc.tensor.matmul(vb[q], avg[:, :], sq[:, q % 2, 0:width[q]], start=True,
                                     stop=True).then_inc(*var.up())
                for q in range(4):
                    variance(q)
                for q, h, w, taps, stride in ((4, h0, w1, 8, 4), (5, h1, w2, 4, 2), (6, h2, w3, 4, 2)):
                    k.wait("tensor", e, *padded.now(i, (3, 5, 7)[q - 4]))
                    k.wait("tensor", e, *relued.now(i, q - 1))
                    for tap in range(taps):
                        src = h[:, tap:tap + stride * (width[q] - 1) + 1:stride]
                        m = nc.tensor.matmul(yb[q], w[:, tap, :], src, start=tap == 0, stop=tap == taps - 1)
                    m.then_inc(*conv.up())
                    variance(q)

        @block.scalar
        def _(e):
            for s in (squared, rooted, relued):
                s.seed(e)
            e.wait_ge(ready, 3)
            with e.Fori(0, NB) as i:
                def square(q):
                    k.wait("scalar", e, *conv.now(i, q))
                    k.wait("scalar", e, *(var.now(i, q - 2) if q >= 2 else var.prev(i, q + 5)))
                    e.activation(sq[:, q % 2, 0:width[q]], yb[q], ACT.Square,
                                 bias=biasc[:, lay[q]:lay[q] + 1]).then_inc(*squared.up())

                def square_root(q):
                    k.wait("scalar", e, *var.now(i, q))
                    k.wait("scalar", e, *(normed.now(i, q - 2) if q >= 2 else normed.prev(i, q + 5)))
                    e.activation(root[:, q % 2, 0:width[q]], vb[q], ACT.Sqrt,
                                 bias=epsc[:, 0:1]).then_inc(*rooted.up())

                def relu(q):
                    k.wait("scalar", e, *normed.now(i, q))
                    if q < 6:
                        if q in (0, 4, 5):
                            k.wait("scalar", e, *conv.prev(i, max(q, 3) + 1))
                        dst = (h0[:, 2 + q * 512:2 + (q + 1) * 512] if q < 4 else
                               h1[:, 1:1 + LEN1] if q == 4 else h2[:, 1:1 + LEN2])
                    else:
                        dst = feats[:, bass.ds(i * LEN3, LEN3)]
                    e.activation(dst, normal[:, q % 2, 0:width[q]], ACT.Relu,
                                 bias=beta[:, lay[q]:lay[q] + 1], scale=gamma[:, lay[q]:lay[q] + 1]
                                 ).then_inc(*relued.up())
                square(0)
                square(1)
                square_root(0)
                square(2)
                square_root(1)
                square(3)
                relu(0)
                square_root(2)
                relu(1)
                square_root(3)
                relu(2)
                relu(3)
                for q in (4, 5, 6):
                    square(q)
                    square_root(q)
                    relu(q)

        @block.gpsimd
        def _(e):
            padded.seed(e)
            with e.Fori(0, NB) as i:
                for q, h, ends in ((3, h0, ((0, 4), (1, 3), (LEN0 + 2, LEN0), (LEN0 + 3, LEN0 - 1))),
                                   (4, h1, ((0, 2), (LEN1 + 1, LEN1 - 1))),
                                   (5, h2, ((0, 2), (LEN2 + 1, LEN2 - 1)))):
                    k.wait("gpsimd", e, *relued.now(i, q))
                    for to, at in ends:
                        e.tensor_copy(h[:, to:to + 1], h[:, at:at + 1]).then_inc(*padded.up())

        @block.vector
        def _(e):
            normed.seed(e)
            v = nc.vector
            v.memset(avg[:, :], 1.0 / (C - 1)).then_inc(*own.up())
            v.memset(epsc[:, :], EPS).then_inc(*own.up())
            v.tensor_scalar(cent[:, :], k.ident[:, :], -1.0 / C, None, ALU.add).then_inc(*own.up())
            e.wait_ge(*own.done())
            e.wait_ge(loaded, 16 * 7)
            v.tensor_reduce(s0[:, :], w0[:, :], axis=AX.X, op=ALU.add).then_inc(ready, 1)
            for t, n, o in ((w1, 8, 0), (w2, 4, 8), (w3, 4, 12)):
                v.tensor_reduce(ssum[:, o:o + n], t[:, :, :], axis=AX.X, op=ALU.add).then_inc(*own.up())
            e.wait_ge(*own.done())
            e.wait_ge(ready, 1)
            v.tensor_scalar(s0[:, :], s0[:, :], -1.0 / C, None, ALU.mult).then_inc(*own.up())
            v.tensor_scalar(ssum[:, :], ssum[:, :], -1.0 / C, None, ALU.mult).then_inc(*own.up())
            e.wait_ge(*own.done())
            v.tensor_scalar(w0[:, :], w0[:, :], s0[:, 0:1], None, ALU.add).then_inc(*own.up())
            for t, n, o in ((w1, 8, 0), (w2, 4, 8), (w3, 4, 12)):
                v.tensor_tensor(t[:, :, :], t[:, :, :], spread(ssum[:, o:o + n], 2, C), ALU.add).then_inc(*own.up())
            e.wait_ge(*own.done())
            e.wait_ge(bias_mm, 1)
            v.tensor_copy(biasc[:, :], pz[:, 0:4]).then_inc(ready, 1)
            e.wait_ge(ready, 2)
            e.sem_inc(ready, 1)
            start = own.n
            with e.Fori(0, NB) as i:
                own.n = start
                own.turn(i, 7)
                for q in range(7):
                    k.wait("vector", e, *rooted.now(i, q))
                    v.reciprocal(inv[:, q % 2, 0:width[q]], root[:, q % 2, 0:width[q]]).then_inc(*own.up())
                    k.wait("vector", e, *(relued.now(i, q - 2) if q >= 2 else relued.prev(i, q + 5)))
                    k.wait("vector", e, *own.done())
                    v.scalar_tensor_tensor(normal[:, q % 2, 0:width[q]], yb[q], biasc[:, lay[q]:lay[q] + 1],
                                           inv[:, q % 2, 0:width[q]], ALU.add, ALU.mult).then_inc(*normed.up())
                own.end()


def importance(k, feats, lrow):
    nc, ins = k.nc, k.ins
    with Stage(k, "imp") as st:
        sb = st.sb
        sig = st.sig
        w1, w2, w3 = sb("mw1", [C, DMLP]), sb("mw2", [C, 4, DMLP]), sb("mw3", [C, 4])
        b1, b2, b3 = sb("mb1", [C, 4]), sb("mb2", [C, 4]), sb("mb3", [1, 1])
        z1, z2 = sb("z1", [C, 4, 512]), sb("z2", [C, 4, 512])
        p1 = st.ps("p1", [C, 4, 512])
        p2 = st.ps("p2", [C, 4, 512])
        loaded = st.sem("mlp_weights_loaded")
        mm1, mm2, mm3 = sig("layer1_done", 4), sig("layer2_done", 4), sig("layer3_done", 1)
        g1, g2, row = sig("gelu1_done", 4), sig("gelu2_done", 4), sig("logits_kept", 1)
        block = st.block()

        @block.sync
        def _(e):
            for t, n in ((w1, "mlp_w1"), (w2, "mlp_w2"), (w3, "mlp_w3"), (b1, "mlp_b1"), (b2, "mlp_b2"), (b3, "mlp_b3")):
                e.dma_start(t[:], ins[n]).then_inc(loaded, 16)

        @block.tensor
        def _(e):
            for s in (mm1, mm2, mm3):
                s.seed(e)
            e.wait_ge(loaded, 96)
            with e.Fori(0, NB // 4) as i:
                for m in range(4):
                    if m == 0:
                        k.wait("tensor", e, *row.prev(i))
                    k.wait("tensor", e, *g1.prev(i, m))
                    nc.tensor.matmul(p1[:, m, :], w1[:, m * C:(m + 1) * C], feats[:, bass.ds(i * 512, 512)],
                                     start=True, stop=True).then_inc(*mm1.up())
                for m in range(4):
                    k.wait("tensor", e, *g2.prev(i, m))
                    for c in range(4):
                        if m == 0:
                            k.wait("tensor", e, *g1.now(i, c))
                        x = nc.tensor.matmul(p2[:, m, :], w2[:, c, m * C:(m + 1) * C], z1[:, c, :],
                                             start=c == 0, stop=c == 3)
                    x.then_inc(*mm2.up())
                for c in range(4):
                    k.wait("tensor", e, *g2.now(i, c))
                    x = nc.tensor.matmul(p1[0:1, 0, :], w3[:, c:c + 1], z2[:, c, :], start=c == 0, stop=c == 3)
                x.then_inc(*mm3.up())

        @block.scalar
        def _(e):
            for s in (g1, g2, row):
                s.seed(e)
            e.wait_ge(loaded, 96)
            with e.Fori(0, NB // 4) as i:
                for m in range(4):
                    k.wait("scalar", e, *mm1.now(i, m))
                    k.wait("scalar", e, *mm2.prev(i))
                    e.activation(z1[:, m, :], p1[:, m, :], ACT.Gelu, bias=b1[:, m:m + 1]).then_inc(*g1.up())
                for m in range(4):
                    k.wait("scalar", e, *mm2.now(i, m))
                    k.wait("scalar", e, *mm3.prev(i))
                    e.activation(z2[:, m, :], p2[:, m, :], ACT.Gelu, bias=b2[:, m:m + 1]).then_inc(*g2.up())
                k.wait("scalar", e, *mm3.now(i))
                e.activation(lrow[:, bass.ds(i * 512, 512)], p1[0:1, 0, :], ACT.Identity,
                             bias=b3[:, 0:1]).then_inc(*row.up())


def pool_frames(k, feats, lrow):
    nc, ins = k.nc, k.ins
    G, NG = 8, NB // 8
    with Stage(k, "pool") as st:
        sb = st.sb
        ps = st.ps
        sig = st.sig
        imp, cs = sb("imp", [NB, C]), sb("cs", [NB, C + 1])
        zero, tot = sb("zero", [NB, C]), sb("tot", [NB, 1])
        cst, csp = sb("cst", [C, NB]), sb("csp", [C, NB])
        step = sb("step", [C, D + 1])
        pa, pb = sb("pa", [C, G, D + 1]), sb("pb", [C, G, D + 1])
        da, db, wm = sb("da", [C, G, D]), sb("db", [C, G, D]), sb("wm", [C, G, D])
        avg = sb("avgp", [C, C])
        gamma, beta = sb("gammap", [C, 5]), sb("betap", [C, 5])
        fg, fm, ft = sb("fg", [C, G * C]), sb("fm", [C, G]), sb("ft", [C, G, C])
        sq, root, inv, normal = sb("sqp", [C, 512]), sb("rootp", [C, 512]), sb("invp", [C, 512]), sb("normp", [C, 512])
        epsc = sb("epscp", [C, 1])
        pt = ps("pt", [C, G, C])
        po, pv, pc = ps("po", [C, 512]), ps("pvp", [C, 512]), ps("pc", [C, 2, NB])
        scratch = nc.dram_tensor("logit_rows", (NB, C), F32, kind="Internal").ap()
        moved = st.sem("logits_moved")
        act0 = st.sem("sigmoid_done")
        tr0 = st.sem("sums_transposed")
        vec0 = st.sem("sums_done")
        iot = st.sem("steps_made")
        own = st.steps("vector_pool_steps")
        grp, ftd, mm, var = sig("group_copied", 1), sig("frames_transposed", 1), sig("pooled", 1), sig("pool_variance", 1)
        sqd, rtd, rel = sig("pool_squared", 1), sig("pool_rooted", 1), sig("pool_relu", 1)
        cen, wts, nrm = sig("frames_centred", 1), sig("weights_made", 1), sig("pool_normed", 1)
        block = st.block()

        @block.sync
        def _(e):
            e.dma_start(scratch.rearrange("b t -> (b t)").rearrange("(o n) -> o n", o=1), lrow[:, :]).then_inc(moved, 16)
            e.wait_ge(moved, 16)
            e.dma_start(imp[:, :], scratch).then_inc(moved, 16)
            e.dma_start(gamma[:, :], ins["norm_g"]).then_inc(moved, 16)
            e.dma_start(beta[:, :], ins["norm_b"]).then_inc(moved, 16)

        @block.gpsimd
        def _(e):
            e.iota(step[:, :], [[-1, D + 1]], base=0, channel_multiplier=0,
                   allow_small_or_imprecise_dtypes=True).then_inc(iot, 1)
            e.wait_ge(iot, 1)
            e.memset(step[:, D:D + 1], -BIG).then_inc(iot, 1)
            e.memset(avg[:, :], 1.0 / (C - 1)).then_inc(iot, 1)
            e.memset(epsc[:, :], EPS).then_inc(iot, 1)
            e.memset(zero[:, :], 0.0).then_inc(iot, 1)
            e.memset(cs[:, 0:1], 0.0).then_inc(iot, 1)

        @block.scalar
        def _(e):
            for s in (grp, sqd, rtd, rel):
                s.seed(e)
            e.wait_ge(moved, 64)
            e.wait_ge(iot, 6)
            e.activation(imp[:, :], imp[:, :], ACT.Sigmoid).then_inc(act0, 1)
            with e.Fori(0, NG) as i:
                k.wait("scalar", e, *ftd.prev(i))
                e.activation(fg[:, :], feats[:, bass.ds(i * G * C, G * C)], ACT.Copy).then_inc(*grp.up())
                k.wait("scalar", e, *mm.now(i))
                k.wait("scalar", e, *var.prev(i))
                e.activation(sq[:, :], po[:, :], ACT.Square).then_inc(*sqd.up())
                k.wait("scalar", e, *var.now(i))
                k.wait("scalar", e, *nrm.prev(i))
                e.activation(root[:, :], pv[:, :], ACT.Sqrt, bias=epsc[:, 0:1]).then_inc(*rtd.up())
                k.wait("scalar", e, *nrm.now(i))
                e.activation(k.resid[:, bass.ds(i * G * D, G * D)], normal[:, :], ACT.Relu,
                             bias=beta[:, 4:5], scale=gamma[:, 4:5]).then_inc(*rel.up())

        @block.tensor
        def _(e):
            for s in (ftd, mm, var):
                s.seed(e)
            e.wait_ge(vec0, 1)
            nc.tensor.transpose(pc[:, 0, :], cs[:, 1:C + 1], k.ident[0:NB, 0:NB]).then_inc(tr0, 1)
            nc.tensor.transpose(pc[:, 1, :], cs[:, 0:C], k.ident[0:NB, 0:NB]).then_inc(tr0, 1)
            with e.Fori(0, NG) as i:
                k.wait("tensor", e, *grp.now(i))
                k.wait("tensor", e, *cen.prev(i))
                for g in range(G):
                    m = nc.tensor.transpose(pt[:, g, :], fg[:, g * C:(g + 1) * C], k.ident[:, :])
                m.then_inc(*ftd.up())
                k.wait("tensor", e, *cen.now(i))
                k.wait("tensor", e, *wts.now(i))
                k.wait("tensor", e, *nrm.prev(i))
                for g in range(G):
                    m = nc.tensor.matmul(po[:, g * D:(g + 1) * D], ft[:, g, :], wm[:, g, :], start=True, stop=True)
                m.then_inc(*mm.up())
                k.wait("tensor", e, *sqd.now(i))
                k.wait("tensor", e, *rtd.prev(i))
                nc.tensor.matmul(pv[:, :], avg[:, :], sq[:, :], start=True, stop=True).then_inc(*var.up())

        @block.vector
        def _(e):
            v = nc.vector
            for s in (cen, wts, nrm):
                s.seed(e)
            e.wait_ge(act0, 1)
            v.tensor_scalar(imp[:, :], imp[:, :], 1e-5, None, ALU.add).then_inc(*own.up())
            e.wait_ge(*own.done())
            v.tensor_reduce(tot[:, :], imp[:, :], axis=AX.X, op=ALU.add).then_inc(*own.up())
            e.wait_ge(*own.done())
            v.reciprocal(tot[:, :], tot[:, :]).then_inc(*own.up())
            e.wait_ge(*own.done())
            v.tensor_scalar(imp[:, :], imp[:, :], tot[:, 0:1], float(D), ALU.mult, ALU.mult).then_inc(*own.up())
            e.wait_ge(*own.done())
            v.tensor_tensor_scan(cs[:, 1:C + 1], imp[:, :], zero[:, :], 0.0, ALU.add, ALU.add).then_inc(vec0, 1)
            e.wait_ge(tr0, 2)
            v.tensor_copy(cst[:, :], pc[:, 0, :]).then_inc(*own.up())
            v.tensor_copy(csp[:, :], pc[:, 1, :]).then_inc(*own.up())
            e.wait_ge(*own.done())
            base = own.n
            with e.Fori(0, NG) as i:
                own.n = base
                own.turn(i, PER_POOL)
                for p, s in ((pa, cst), (pb, csp)):
                    v.tensor_tensor(p[:, :, :], spread(step[:, :], 1, G),
                                    spread(s[:, bass.ds(i * G, G)], 2, D + 1), ALU.add).then_inc(*own.up())
                k.wait("vector", e, *own.done())
                for p in (pa, pb):
                    v.tensor_scalar(p[:, :, :], p[:, :, :], 0.0, None, ALU.max).then_inc(*own.up())
                k.wait("vector", e, *own.done())
                for p, d in ((pa, da), (pb, db)):
                    v.tensor_tensor(d[:, :, :], p[:, :, 0:D], p[:, :, 1:D + 1], ALU.subtract).then_inc(*own.up())
                k.wait("vector", e, *own.done())
                k.wait("vector", e, *mm.prev(i))
                v.tensor_tensor(wm[:, :, :], da[:, :, :], db[:, :, :], ALU.subtract).then_inc(*wts.up())
                k.wait("vector", e, *ftd.now(i))
                for g2 in range(2):
                    v.tensor_reduce(fm[:, 4 * g2:4 * g2 + 4], pt[:, 4 * g2:4 * g2 + 4, :], axis=AX.X, op=ALU.add).then_inc(*own.up())
                k.wait("vector", e, *own.done())
                v.tensor_scalar(fm[:, :], fm[:, :], 1.0 / C, None, ALU.mult).then_inc(*own.up())
                k.wait("vector", e, *own.done())
                v.tensor_tensor(ft[:, 0:4, :], pt[:, 0:4, :], spread(fm[:, 0:4], 2, C), ALU.subtract).then_inc(*own.up())
                v.tensor_tensor(ft[:, 4:8, :], pt[:, 4:8, :], spread(fm[:, 4:8], 2, C), ALU.subtract).then_inc(*cen.up())
                k.wait("vector", e, *rtd.now(i))
                v.reciprocal(inv[:, :], root[:, :]).then_inc(*own.up())
                k.wait("vector", e, *own.done())
                k.wait("vector", e, *rel.prev(i))
                v.tensor_tensor(normal[:, :], po[:, :], inv[:, :], ALU.mult).then_inc(*nrm.up())
                own.end()


PER_POOL = 11


def norm_transpose(k, name, xt, affine=None):
    G, NG = 8, NB // 8
    nc = k.nc
    with Stage(k, name) as st:
        mean, dev, sq = st.sb("mean", [C, G]), st.sb("dev", [C, G, D]), st.sb("sq", [C, G, D])
        ss, root, inv, xn = st.sb("ss", [C, G]), st.sb("root", [C, G]), st.sb("inv", [C, G]), st.sb("xn", [C, G, D])
        epsc = st.sb("epsc", [C, 1])
        gb = st.sb("gb", [D, 2])
        pt = st.ps("pt", [D, G, C])
        loaded = st.sem("affine_loaded")
        const = st.sem("norm_constants")
        own = st.steps("vector_norm_steps")
        devd, sqd, var = st.sig("deviations", 1), st.sig("squares", 1), st.sig("variances", 1)
        rtd, nrm, trd, kept = st.sig("roots", 1), st.sig("normed", 1), st.sig("transposed", 1), st.sig("kept", 1)
        block = st.block()

        @block.sync
        def _(e):
            if affine:
                e.dma_start(gb[:, :], k.ins[affine]).then_inc(loaded, 16)

        @block.vector
        def _(e):
            v = nc.vector
            for s in (devd, var, nrm):
                s.seed(e)
            v.memset(xt[D:D + 1, :], 1.0).then_inc(const, 1)
            v.memset(epsc[:, :], EPS).then_inc(const, 1)
            with e.Fori(0, NG) as i:
                own.n = 0
                own.turn(i, 3)
                x = k.resid[:, bass.ds(i * G * D, G * D)].rearrange("p (g d) -> p g d", g=G)
                v.tensor_reduce(mean[:, :], x, axis=AX.X, op=ALU.add).then_inc(*own.up())
                k.wait("vector", e, *own.done())
                v.tensor_scalar(mean[:, :], mean[:, :], 1.0 / D, None, ALU.mult).then_inc(*own.up())
                k.wait("vector", e, *own.done())
                v.tensor_tensor(dev[:, :, :], x, spread(mean[:, :], 2, D), ALU.subtract).then_inc(*devd.up())
                k.wait("vector", e, *sqd.now(i))
                v.tensor_reduce(ss[:, :], sq[:, :, :], axis=AX.X, op=ALU.add).then_inc(*var.up())
                k.wait("vector", e, *rtd.now(i))
                v.reciprocal(inv[:, :], root[:, :]).then_inc(*own.up())
                k.wait("vector", e, *own.done())
                k.wait("vector", e, *trd.prev(i))
                v.tensor_tensor(xn[:, :, :], dev[:, :, :], spread(inv[:, :], 2, D), ALU.mult).then_inc(*nrm.up())
                own.end()

        @block.scalar
        def _(e):
            for s in (sqd, rtd, kept):
                s.seed(e)
            e.wait_ge(const, 2)
            if affine:
                e.wait_ge(loaded, 16)
            with e.Fori(0, NG) as i:
                k.wait("scalar", e, *devd.now(i))
                e.activation(sq[:, :, :], dev[:, :, :], ACT.Square).then_inc(*sqd.up())
                k.wait("scalar", e, *var.now(i))
                e.activation(root[:, :], ss[:, :], ACT.Sqrt, bias=epsc[:, 0:1], scale=1.0 / D).then_inc(*rtd.up())
                k.wait("scalar", e, *trd.now(i))
                dst = xt[0:D, bass.ds(i * G * C, G * C)].rearrange("p (g c) -> p g c", g=G)
                if affine:
                    e.activation(dst, pt[:, :, :], ACT.Identity, bias=gb[:, 1:2], scale=gb[:, 0:1]).then_inc(*kept.up())
                else:
                    e.activation(dst, pt[:, :, :], ACT.Copy).then_inc(*kept.up())

        @block.tensor
        def _(e):
            trd.seed(e)
            with e.Fori(0, NG) as i:
                k.wait("tensor", e, *nrm.now(i))
                k.wait("tensor", e, *kept.prev(i))
                for g in range(G):
                    m = nc.tensor.transpose(pt[:, g, :], xn[:, g, :], k.ident[:, :])
                m.then_inc(*trd.up())


def odd_attention(k, xt):
    nc = k.nc
    DA = DH + 1
    with Stage(k, "oddattn") as st:
        wq, wk, wv = st.sb("wq", [D + 1, HEADS * DH]), st.sb("wk", [D + 1, HEADS * DH]), st.sb("wv", [D + 1, HEADS * DH])
        wo, bo, ones = st.sb("wo", [128, 2, D]), st.sb("bo", [1, D]), st.sb("ones", [1, C])
        mask = st.sb("mask", [C, C])
        xb = st.sb("xb", [D + 1, C])
        qz, kt, va = st.sb("qz", [128, 2, 4, C]), st.sb("kt", [128, 2, C]), st.sb("va", [C, HEADS, DA])
        s, mx, p, pt_ = st.sb("s", [C, HEADS, C]), st.sb("mx", [C, HEADS]), st.sb("p", [C, HEADS, C]), st.sb("pt_", [C, HEADS, C])
        rz, zn, zt = st.sb("rz", [C, HEADS]), st.sb("zn", [C, HEADS, DH]), st.sb("zt", [128, 2, C])
        pqk, pvo, pS = st.ps("pqk", [128, 4, C]), st.ps("pvo", [C, 512]), st.ps("pS", [C, HEADS, C])
        pT, pz, pzt = st.ps("pT", [C, HEADS, C]), st.ps("pz", [C, 512]), st.ps("pzt", [128, 512])
        loaded, const = st.sem("attn_weights_loaded"), st.sem("attn_constants")
        own = st.steps("vector_attn_steps")
        xc, qkv, qkk, vk = st.sig("x_copied", 1), st.sig("qkv_done", 1), st.sig("qk_kept", 5), st.sig("v_kept", 1)
        sc, sh, ex, tr = st.sig("scores_done", 1), st.sig("scores_shifted", 1), st.sig("exps_done", 1), st.sig("probs_transposed", 1)
        ta, tb, zd, zn_s = st.sig("probs_kept_low", 1), st.sig("probs_kept_high", 1), st.sig("mixed", 1), st.sig("mix_normed", 1)
        ztd, ztk, od, rd = st.sig("mix_transposed", 1), st.sig("mix_kept", 1), st.sig("out_done", 1), st.sig("resid_done", 1)
        block = st.block()

        @block.sync
        def _(e):
            for t, n in ((wq, "a_wq"), (wk, "a_wk"), (wv, "a_wv"), (wo, "a_wo"), (bo, "a_bo")):
                e.dma_start(t[:], k.ins[n]).then_inc(loaded, 16)

        @block.gpsimd
        def _(e):
            e.memset(mask[:, :], 0.0).then_inc(const, 1)
            e.memset(qz[:, :, :, :], 0.0).then_inc(const, 1)
            e.memset(va[:, :, :], 1.0).then_inc(const, 1)
            e.memset(ones[:, :], 1.0).then_inc(const, 1)
            e.wait_ge(const, 4)
            e.affine_select(out=mask[:, :], in_=mask[:, :], compare_op=ALU.is_ge, fill=-BIG, base=0,
                            pattern=[[-1, C]], channel_multiplier=1).then_inc(const, 1)
            e.wait_ge(const, 5)
            e.affine_select(out=mask[:, 0:C:2], in_=mask[:, 0:C:2], compare_op=ALU.is_equal, fill=-BIG, base=0,
                            pattern=[[-2, C // 2]], channel_multiplier=1).then_inc(const, 1)

        @block.vector
        def _(e):
            v = nc.vector
            for g in (xc, vk, sh, tb, zn_s, rd):
                g.seed(e)
            e.wait_ge(const, 6)
            with e.Fori(0, NB) as i:
                own.n = 0
                own.turn(i, 3)
                k.wait("vector", e, *qkv.prev(i))
                v.tensor_copy(xb[:, :], xt[0:D + 1, bass.ds(i * C, C)]).then_inc(*xc.up())
                k.wait("vector", e, *qkv.now(i))
                k.wait("vector", e, *zd.prev(i))
                v.tensor_copy(va[:, :, 0:DH], pvo[:, 0:HEADS * DH].rearrange("p (h d) -> p h d", h=HEADS)).then_inc(*vk.up())
                k.wait("vector", e, *sc.now(i))
                k.wait("vector", e, *ex.prev(i))
                v.scalar_tensor_tensor(s[:, :, :], pS[:, :, :], float(DH) ** -0.5, spread(mask[:, :], 1, HEADS),
                                       ALU.mult, ALU.add).then_inc(*own.up())
                k.wait("vector", e, *own.done())
                v.tensor_reduce(mx[:, :], s[:, :, :], axis=AX.X, op=ALU.max).then_inc(*own.up())
                k.wait("vector", e, *own.done())
                v.tensor_tensor(s[:, :, :], s[:, :, :], spread(mx[:, :], 2, C), ALU.subtract).then_inc(*sh.up())
                k.wait("vector", e, *tr.now(i))
                k.wait("vector", e, *zd.prev(i))
                v.tensor_copy(pt_[:, 4:8, :], pT[:, 4:8, :]).then_inc(*tb.up())
                k.wait("vector", e, *zd.now(i))
                z = pz[:, 0:HEADS * DA].rearrange("p (h d) -> p h d", h=HEADS)
                v.reciprocal(rz[:, :], z[:, :, DH]).then_inc(*own.up())
                k.wait("vector", e, *own.done())
                k.wait("vector", e, *ztd.prev(i))
                v.tensor_tensor(zn[:, :, :], z[:, :, 0:DH], spread(rz[:, :], 2, DH), ALU.mult).then_inc(*zn_s.up())
                k.wait("vector", e, *od.now(i))
                r = k.resid[:, bass.ds(i * D, D)]
                v.tensor_tensor(r, r, pvo[:, 256:256 + D], ALU.add).then_inc(*rd.up())
                own.end()

        @block.scalar
        def _(e):
            for g in (qkk, ex, ta, ztk):
                g.seed(e)
            e.wait_ge(const, 6)
            with e.Fori(0, NB) as i:
                k.wait("scalar", e, *qkv.now(i))
                k.wait("scalar", e, *sc.prev(i))
                for j in range(4):
                    r = slice(32 * j, 32 * j + 32)
                    e.activation(qz[r, :, j, :], pqk[r, 0:2, :], ACT.Copy).then_inc(*qkk.up())
                e.activation(kt[:, :, :], pqk[:, 2:4, :], ACT.Copy).then_inc(*qkk.up())
                k.wait("scalar", e, *sh.now(i))
                k.wait("scalar", e, *tr.prev(i))
                e.activation(p[:, :, :], s[:, :, :], ACT.Exp).then_inc(*ex.up())
                k.wait("scalar", e, *tr.now(i))
                k.wait("scalar", e, *zd.prev(i))
                e.activation(pt_[:, 0:4, :], pT[:, 0:4, :], ACT.Copy).then_inc(*ta.up())
                k.wait("scalar", e, *ztd.now(i))
                k.wait("scalar", e, *od.prev(i))
                e.activation(zt[:, :, :], pzt[:, 0:256].rearrange("p (a c) -> p a c", a=2), ACT.Copy).then_inc(*ztk.up())

        @block.tensor
        def _(e):
            t = nc.tensor
            for g in (qkv, sc, tr, zd, ztd, od):
                g.seed(e)
            e.wait_ge(loaded, 80)
            e.wait_ge(const, 6)
            with e.Fori(0, NB) as i:
                k.wait("tensor", e, *xc.now(i))
                k.wait("tensor", e, *qkk.prev(i))
                k.wait("tensor", e, *rd.prev(i))
                for n, w in ((0, wq), (2, wk)):
                    for g in range(2):
                        t.matmul(pqk[:, n + g, :], w[:, g * 128:(g + 1) * 128], xb[:, :], start=True, stop=True)
                t.matmul(pvo[:, 0:256], xb[:, :], wv[:, :], start=True, stop=True).then_inc(*qkv.up())
                k.wait("tensor", e, *qkk.now(i))
                k.wait("tensor", e, *sh.prev(i))
                for h in range(HEADS):
                    m = t.matmul(pS[:, h, :], qz[:, h // 4, h % 4, :], kt[:, h // 4, :], start=True, stop=True)
                m.then_inc(*sc.up())
                k.wait("tensor", e, *ex.now(i))
                for h in range(HEADS):
                    m = t.transpose(pT[:, h, :], p[:, h, :], k.ident[:, :])
                m.then_inc(*tr.up())
                k.wait("tensor", e, *ta.now(i))
                k.wait("tensor", e, *tb.now(i))
                k.wait("tensor", e, *vk.now(i))
                for h in range(HEADS):
                    m = t.matmul(pz[:, h * DA:(h + 1) * DA], pt_[:, h, :], va[:, h, :], start=True, stop=True)
                m.then_inc(*zd.up())
                k.wait("tensor", e, *zn_s.now(i))
                zf = zn[:, :, :].rearrange("p h d -> p (h d)")
                for g in range(2):
                    m = t.transpose(pzt[:, g * C:(g + 1) * C], zf[:, g * 128:(g + 1) * 128], k.ident[:, :])
                m.then_inc(*ztd.up())
                k.wait("tensor", e, *ztk.now(i))
                for g in range(2):
                    t.matmul(pvo[:, 256:256 + D], zt[:, g, :], wo[:, g, :], start=g == 0, stop=False)
                t.matmul(pvo[:, 256:256 + D], ones[:, :], bo[:, :], start=False, stop=True).then_inc(*od.up())


RUNS = ((0, 1, 16), (1, 1, 8), (2, 1, 5), (3, 1, 4), (4, 1, 3), (5, 3, 2), (8, 8, 1))
NCAND = sum(n * m for _, n, m in RUNS)
RING = 4


def key_memory(k, xt):
    nc = k.nc
    DV = D + 1
    with Stage(k, "pkm") as st:
        wpk, keys = st.sb("wpk", [32, 16, D]), st.sb("keys", [32, 16, NKEY])
        wsim = st.sb("wsim", [D, 16, NKEY])
        wq, wo = st.sb("wq", [D, HEADS * D]), st.sb("wo", [128, 4, D])
        mask = st.sb("mask", [C, C])
        hoff, iot = st.sb("hoff", [C, HEADS, TOPK]), st.sb("iot", [C, NCAND])
        xb = st.sb("xb", [D, C])
        sim, rest = st.sb("sim", [C, 16, NKEY]), st.sb("rest", [C, 16, NKEY])
        val, idx = st.sb("val", [C, 16, TOPK]), st.sb("idx", [C, 16, TOPK], U32)
        idf = st.sb("idf", [C, 16, TOPK])
        cand, crest, cidx = st.sb("cand", [C, HEADS, NCAND]), st.sb("crest", [C, HEADS, NCAND]), st.sb("cidx", [C, HEADS, NCAND])
        best, pos, posf = st.sb("best", [C, HEADS, TOPK]), st.sb("pos", [C, HEADS, TOPK], U32), st.sb("posf", [C, HEADS, TOPK])
        hit = st.sb("hit", [C, 4, TOPK, NCAND])
        rowf, row = st.sb("rowf", [C, HEADS, TOPK]), st.sb("row", [C, HEADS * TOPK], U32)
        shifted, wnew, wcur = st.sb("shifted", [C, HEADS, TOPK]), st.sb("wnew", [C, HEADS, TOPK]), st.sb("wcur", [C, HEADS, TOPK])
        tot, rtot = st.sb("tot", [C, HEADS]), st.sb("rtot", [C, HEADS])
        ring = [[st.sb(f"ring{r}", [C, TOPK, 2 * D])] for r in range(RING)]
        ring = [r[0] for r in ring]
        kk, vv = st.sb("kk", [C, HEADS, D]), st.sb("vv", [C, HEADS, DV])
        qz, kt = st.sb("qz", [128, HEADS, C]), st.sb("kt", [128, 4, C])
        s, mx, p, pt_ = st.sb("s", [C, HEADS, C]), st.sb("mx", [C, HEADS]), st.sb("p", [C, HEADS, C]), st.sb("pt_", [C, HEADS, C])
        rz, zn, zt = st.sb("rz", [C, HEADS]), st.sb("zn", [C, HEADS, D]), st.sb("zt", [128, 4, C])
        pq, psim, pk = st.ps("pq", [128, 4, C]), st.ps("psim", [128, 16, NKEY]), st.ps("pk", [128, 4, C])
        pS, pT = st.ps("pS", [C, HEADS, C]), st.ps("pT", [C, HEADS, C])
        loaded, const, prep = st.sem("weights_loaded"), st.sem("constants"), st.sem("key_product")
        own = st.steps("vector_steps")
        xc, simd, simk = st.sig("x_copied", 1), st.sig("similarities_done", 1), st.sig("similarities_kept", 1)
        wsh, wex = st.sig("best_shifted", 1), st.sig("best_exps", 1)
        rows = st.sig("rows_chosen", 1)
        got = [st.sig(f"rows_gathered{r}", 2, 256, seeded=False) for r in range(RING)]
        used = st.sig("rows_used", HEADS)
        qd, qk = st.sig("q_done", 1), st.sig("q_kept", 2)
        kd, kkept = st.sig("k_transposed", 1), st.sig("k_kept", 1)
        sc, sh, ex, tr = st.sig("scores_done", 1), st.sig("scores_shifted", 1), st.sig("exps_done", 1), st.sig("probs_transposed", 1)
        ta, tb, zd, zns = st.sig("probs_kept_low", 1), st.sig("probs_kept_high", 1), st.sig("mixed", 1), st.sig("mix_normed", 1)
        ztd, ztk, od, rd = st.sig("mix_transposed", 1), st.sig("mix_kept", 1), st.sig("out_done", 1), st.sig("resid_done", 1)
        block = st.block()

        @block.sync
        def _(e):
            for t, n in ((wpk, "k_wpk"), (keys, "k_keys"), (wq, "k_wq"), (wo, "k_wo")):
                e.dma_start(t[:], k.ins[n]).then_inc(loaded, 16)

        @block.gpsimd
        def _(e):
            e.memset(mask[:, :], 0.0).then_inc(const, 1)
            e.memset(qz[:, :, :], 0.0).then_inc(const, 1)
            e.memset(vv[:, :, :], 1.0).then_inc(const, 1)
            e.iota(hoff[:, :, :], [[NKV, HEADS], [0, TOPK]], base=0, channel_multiplier=0,
                   allow_small_or_imprecise_dtypes=True).then_inc(const, 1)
            e.iota(iot[:, :], [[1, NCAND]], base=0, channel_multiplier=0,
                   allow_small_or_imprecise_dtypes=True).then_inc(const, 1)
            e.wait_ge(const, 5)
            e.affine_select(out=mask[:, :], in_=mask[:, :], compare_op=ALU.is_ge, fill=-BIG, base=0,
                            pattern=[[-1, C]], channel_multiplier=1).then_inc(const, 1)
            with e.Fori(0, NB) as i:
                k.wait("gpsimd", e, *rows.now(i))
                for h in range(HEADS):
                    k.wait("gpsimd", e, *(used.now(i, h - RING) if h >= RING else used.prev(i, h + HEADS - RING)))
                    for j in range(TOPK):
                        e.indirect_dma_start(ring[h % RING][:, j, :], None, k.ins["k_table"],
                                             bass.IndirectOffsetOnAxis(ap=row[:, h * TOPK + j:h * TOPK + j + 1], axis=0)
                                             ).then_inc(got[h % RING].sem, 16)

        @block.vector
        def _(e):
            v = nc.vector
            for g in (xc, wsh, rows, used, kkept, sh, tb, zns, rd):
                g.seed(e)
            e.wait_ge(prep, 1)
            v.tensor_copy(wsim[:, :, :], psim[0:D, :, :]).then_inc(prep, 1)
            e.wait_ge(const, 6)

            def settle():
                k.wait("vector", e, *own.done())

            def top16(vals, spots, x, y, n, m):
                for a in range(n):
                    v.max(vals[:, a, 0:8], x[:, a, :]).then_inc(*own.up())
                settle()
                for a in range(n):
                    v.max_index(spots[:, a, 0:8], vals[:, a, 0:8], x[:, a, :]).then_inc(*own.up())
                    v.match_replace(y[:, a, :], vals[:, a, 0:8], x[:, a, :], -BIG).then_inc(*own.up())
                settle()
                for a in range(n):
                    v.max(vals[:, a, 8:16], y[:, a, :]).then_inc(*own.up())
                settle()
                for a in range(n):
                    v.max_index(spots[:, a, 8:16], vals[:, a, 8:16], y[:, a, :]).then_inc(*own.up())

            def search(i):
                k.wait("vector", e, *simd.prev(i))
                v.tensor_copy(xb[:, :], xt[0:D, bass.ds(i * C, C)]).then_inc(*xc.up())
                k.wait("vector", e, *simk.now(i))
                top16(val, idx, sim, rest, 16, NKEY)
                settle()
                v.tensor_copy(idf[:, :, :], idx[:, :, :]).then_inc(*own.up())
                settle()
                v.scalar_tensor_tensor(idf[:, HEADS:, :], idf[:, HEADS:, :], float(NKEY), hoff[:, :, :],
                                       ALU.mult, ALU.add).then_inc(*own.up())
                settle()
                o = 0
                for a, n, m in RUNS:
                    for to, at in ((cand, val), (cidx, idf)):
                        v.tensor_tensor(to[:, :, o:o + n * m].rearrange("p h (a b) -> p h a b", a=n),
                                        spread(at[:, 0:HEADS, a:a + n], 3, m),
                                        spread(at[:, HEADS:, 0:m], 2, n), ALU.add).then_inc(*own.up())
                    o += n * m
                settle()
                top16(best, pos, cand, crest, HEADS, NCAND)
                settle()
                k.wait("vector", e, *wex.prev(i))
                v.tensor_tensor(shifted[:, :, :], best[:, :, :], spread(best[:, :, 0], 2, TOPK), ALU.subtract).then_inc(*wsh.up())
                v.tensor_copy(posf[:, :, :], pos[:, :, :]).then_inc(*own.up())
                settle()
                for a in (0, 4):
                    v.tensor_tensor(hit[:, :, :, :], spread(posf[:, a:a + 4, :], 3, NCAND),
                                    spread(spread(iot[:, :], 1, TOPK), 1, 4), ALU.is_equal).then_inc(*own.up())
                    settle()
                    v.tensor_tensor(hit[:, :, :, :], hit[:, :, :, :], spread(cidx[:, a:a + 4, :], 2, TOPK), ALU.mult).then_inc(*own.up())
                    settle()
                    v.tensor_reduce(rowf[:, a:a + 4, :], hit[:, :, :, :], axis=AX.X, op=ALU.add).then_inc(*own.up())
                    settle()
                k.wait("vector", e, *wex.now(i))
                v.tensor_reduce(tot[:, :], wnew[:, :, :], axis=AX.X, op=ALU.add).then_inc(*own.up())
                settle()
                v.reciprocal(rtot[:, :], tot[:, :]).then_inc(*own.up())
                settle()
                v.tensor_tensor(wnew[:, :, :], wnew[:, :, :], spread(rtot[:, :], 2, TOPK), ALU.mult).then_inc(*own.up())
                settle()

            def choose():
                v.tensor_copy(row[:, :], rowf[:, :, :].rearrange("p h j -> p (h j)")).then_inc(*rows.up())

            def mix(i, h):
                r = ring[h % RING]
                k.wait("vector", e, *got[h % RING].now(i, h // RING))
                if h == HEADS - 1 and k.more:
                    choose()
                v.tensor_tensor(r[:, :, :], r[:, :, :], spread(wcur[:, h, :], 2, 2 * D), ALU.mult).then_inc(*own.up())
                settle()
                if h == 0:
                    k.wait("vector", e, *kd.prev(i))
                    k.wait("vector", e, *zd.prev(i))
                v.tensor_reduce(kk[:, h, :], r[:, :, 0:D].rearrange("p j d -> p d j"), axis=AX.X, op=ALU.add).then_inc(*own.up())
                v.tensor_reduce(vv[:, h, 0:D], r[:, :, D:].rearrange("p j d -> p d j"), axis=AX.X, op=ALU.add).then_inc(*used.up())

            def attend(i):
                k.wait("vector", e, *kd.now(i))
                v.tensor_copy(kt[:, :, :], pk[:, :, :]).then_inc(*kkept.up())
                k.wait("vector", e, *sc.now(i))
                v.tensor_tensor(s[:, :, :], pS[:, :, :], spread(mask[:, :], 1, HEADS), ALU.add).then_inc(*own.up())
                settle()
                v.tensor_reduce(mx[:, :], s[:, :, :], axis=AX.X, op=ALU.max).then_inc(*own.up())
                settle()
                v.tensor_tensor(s[:, :, :], s[:, :, :], spread(mx[:, :], 2, C), ALU.subtract).then_inc(*sh.up())
                k.wait("vector", e, *tr.now(i))
                v.tensor_copy(pt_[:, 4:8, :], pT[:, 4:8, :]).then_inc(*tb.up())
                k.wait("vector", e, *zd.now(i))
                z = [pS[:, 4 * a:4 * a + 4, :].rearrange("p h c -> p (h c)")[:, 0:4 * DV].rearrange("p (h d) -> p h d", h=4)
                     for a in range(2)]
                for a in range(2):
                    v.reciprocal(rz[:, 4 * a:4 * a + 4], z[a][:, :, D]).then_inc(*own.up())
                settle()
                v.tensor_tensor(zn[:, 0:4, :], z[0][:, :, 0:D], spread(rz[:, 0:4], 2, D), ALU.mult).then_inc(*own.up())
                v.tensor_tensor(zn[:, 4:8, :], z[1][:, :, 0:D], spread(rz[:, 4:8], 2, D), ALU.mult).then_inc(*zns.up())
                k.wait("vector", e, *od.now(i))
                r = k.resid[:, bass.ds(i * D, D)]
                v.tensor_tensor(r, r, pk[:, 0, 0:D], ALU.add).then_inc(*rd.up())

            def turn(i, more):
                k.more = more
                if more:
                    search(i + 1)
                for h in range(HEADS):
                    mix(i, h)
                if more:
                    v.tensor_copy(wcur[:, :, :], wnew[:, :, :]).then_inc(*own.up())
                attend(i)

            search(0)
            choose()
            v.tensor_copy(wcur[:, :, :], wnew[:, :, :]).then_inc(*own.up())
            own.turn(0, 0)
            first = own.n
            with e.Fori(0, NB - 1) as i:
                own.n = first
                own.turn(i, PER_PKM)
                turn(i, True)
                own.end()
            own.leave(NB - 1)
            turn(NB - 1, False)

        @block.scalar
        def _(e):
            for g in (simk, wex, qk, ex, ta, ztk):
                g.seed(e)
            e.wait_ge(const, 6)

            def search(i):
                k.wait("scalar", e, *simd.now(i))
                k.wait("scalar", e, *wsh.prev(i))
                e.activation(sim[:, :, :], psim[:, :, :], ACT.Copy).then_inc(*simk.up())
                k.wait("scalar", e, *wsh.now(i))
                e.activation(wnew[:, :, :], shifted[:, :, :], ACT.Exp).then_inc(*wex.up())

            def attend(i):
                k.wait("scalar", e, *qd.now(i))
                e.activation(qz[0:D, 0:HEADS:2, :], pq[0:D, :, :], ACT.Copy, scale=float(D) ** -0.5).then_inc(*qk.up())
                e.activation(qz[D:, 1:HEADS:2, :], pq[D:, :, :], ACT.Copy, scale=float(D) ** -0.5).then_inc(*qk.up())
                k.wait("scalar", e, *sh.now(i))
                k.wait("scalar", e, *tr.prev(i))
                e.activation(p[:, :, :], s[:, :, :], ACT.Exp).then_inc(*ex.up())
                k.wait("scalar", e, *tr.now(i))
                k.wait("scalar", e, *zd.prev(i))
                e.activation(pt_[:, 0:4, :], pT[:, 0:4, :], ACT.Copy).then_inc(*ta.up())
                k.wait("scalar", e, *ztd.now(i))
                e.activation(zt[:, :, :], pq[:, :, :], ACT.Copy).then_inc(*ztk.up())
            search(0)
            with e.Fori(0, NB - 1) as i:
                search(i + 1)
                attend(i)
            attend(NB - 1)

        @block.tensor
        def _(e):
            t = nc.tensor
            for g in (simd, qd, kd, sc, tr, zd, ztd, od):
                g.seed(e)
            e.wait_ge(loaded, 64)
            for n in range(16):
                m = t.matmul(psim[0:D, n, :], wpk[:, n, :], keys[:, n, :], start=True, stop=True)
            m.then_inc(prep, 1)
            e.wait_ge(prep, 2)
            e.wait_ge(const, 6)

            def search(i):
                k.wait("tensor", e, *xc.now(i))
                k.wait("tensor", e, *simk.prev(i))
                w = wsim[:, :, :].rearrange("p n k -> p (n k)")
                o = psim[:, :, :].rearrange("p n k -> p (n k)")
                for a in range(2):
                    m = t.matmul(o[:, a * 512:(a + 1) * 512], xb[:, :], w[:, a * 512:(a + 1) * 512], start=True, stop=True)
                m.then_inc(*simd.up())

            def attend(i):
                k.wait("tensor", e, *ztk.prev(i))
                for a in range(4):
                    m = t.matmul(pq[:, a, :], wq[:, a * 128:(a + 1) * 128], xt[0:D, bass.ds(i * C, C)], start=True, stop=True)
                m.then_inc(*qd.up())
                k.wait("tensor", e, *used.now(i))
                k.wait("tensor", e, *rd.prev(i))
                kf = kk[:, :, :].rearrange("p h d -> p (h d)")
                for a in range(4):
                    m = t.transpose(pk[:, a, :], kf[:, a * 128:(a + 1) * 128], k.ident[:, :])
                m.then_inc(*kd.up())
                k.wait("tensor", e, *kkept.now(i))
                k.wait("tensor", e, *qk.now(i))
                for h in range(HEADS):
                    m = t.matmul(pS[:, h, :], qz[:, h, :], kt[:, h // 2, :], start=True, stop=True)
                m.then_inc(*sc.up())
                k.wait("tensor", e, *ex.now(i))
                for h in range(HEADS):
                    m = t.transpose(pT[:, h, :], p[:, h, :], k.ident[:, :])
                m.then_inc(*tr.up())
                k.wait("tensor", e, *ta.now(i))
                k.wait("tensor", e, *tb.now(i))
                for h in range(HEADS):
                    o = pS[:, 4 * (h // 4):4 * (h // 4) + 4, :].rearrange("p h c -> p (h c)")
                    m = t.matmul(o[:, (h % 4) * DV:(h % 4 + 1) * DV], pt_[:, h, :], vv[:, h, :], start=True, stop=True)
                m.then_inc(*zd.up())
                k.wait("tensor", e, *zns.now(i))
                zf = zn[:, :, :].rearrange("p h d -> p (h d)")
                for a in range(4):
                    m = t.transpose(pq[:, a, :], zf[:, a * 128:(a + 1) * 128], k.ident[:, :])
                m.then_inc(*ztd.up())
                k.wait("tensor", e, *ztk.now(i))
                for a in range(4):
                    m = t.matmul(pk[:, 0, 0:D], zt[:, a, :], wo[:, a, :], start=a == 0, stop=a == 3)
                m.then_inc(*od.up())
            search(0)
            with e.Fori(0, NB - 1) as i:
                search(i + 1)
                attend(i)
            attend(NB - 1)


PER_PKM = 168


SC = 16
LR = 0.1
GATES = 3


def gated_features(k, xt, fp, gates):
    nc = k.nc
    W = 3 * D + GATES
    with Stage(k, "gated") as st:
        wf, xb = st.sb("wf", [D, W]), st.sb("xb", [D, 2 * C])
        pf = st.ps("pf", [C, 2, W])
        sq, n2 = st.sb("sq", [C, NB, D]), st.sb("n2", [C, 2, NB])
        loaded = st.sem("weights_loaded")
        own, aown = st.steps("vector_steps"), st.steps("scalar_steps")
        xc, fd, fk = st.sig("x_copied", 1), st.sig("features_done", 1), st.sig("features_kept", 1)
        block = st.block()

        @block.sync
        def _(e):
            e.dma_start(wf[:, :], k.ins["t_wf"]).then_inc(loaded, 16)

        @block.tensor
        def _(e):
            fd.seed(e)
            e.wait_ge(loaded, 16)
            with e.Fori(0, NB // 2) as i:
                k.wait("tensor", e, *xc.now(i))
                k.wait("tensor", e, *fk.prev(i))
                for g in range(2):
                    m = nc.tensor.matmul(pf[:, g, :], xb[:, g * C:(g + 1) * C], wf[:, :], start=True, stop=True)
                m.then_inc(*fd.up())

        @block.scalar
        def _(e):
            fk.seed(e)
            with e.Fori(0, NB // 2) as i:
                k.wait("scalar", e, *fd.now(i))
                e.activation(fp[:, bass.ds(2 * i, 2), :], pf[:, :, :], ACT.Copy).then_inc(*fk.up())
            e.wait_ge(*fk.now(NB // 2 - 1))
            e.activation(fp[:, :, 0:3 * D], fp[:, :, 0:3 * D], ACT.Silu).then_inc(*aown.up())
            e.activation(gates[:, :, :], fp[:, :, 3 * D:], ACT.Sigmoid).then_inc(*aown.up())
            e.wait_ge(own.sem, NORM_AT)
            e.activation(n2[:, :, :], n2[:, :, :], ACT.Sqrt).then_inc(*aown.up())

        @block.vector
        def _(e):
            v = nc.vector
            xc.seed(e)
            with e.Fori(0, NB // 2) as i:
                k.wait("vector", e, *fd.prev(i))
                v.tensor_copy(xb[:, :], xt[0:D, bass.ds(i * 2 * C, 2 * C)]).then_inc(*xc.up())
            e.wait_ge(aown.sem, 2)
            for a in range(2):
                x = fp[:, :, a * D:(a + 1) * D]
                v.tensor_tensor(sq[:, :, :], x, x, ALU.mult).then_inc(*own.up())
                e.wait_ge(*own.done())
                v.tensor_reduce(n2[:, a, :], sq[:, :, :], axis=AX.X, op=ALU.add).then_inc(*own.up())
                e.wait_ge(*own.done())
            assert own.n == NORM_AT
            v.tensor_scalar(gates[:, :, 1], gates[:, :, 1], LR, None, ALU.mult).then_inc(*own.up())
            e.wait_ge(aown.sem, 3)
            v.tensor_scalar(n2[:, :, :], n2[:, :, :], 1e-12, None, ALU.max).then_inc(*own.up())
            e.wait_ge(*own.done())
            v.reciprocal(n2[:, :, :], n2[:, :, :]).then_inc(*own.up())
            e.wait_ge(*own.done())
            for a in range(2):
                x = fp[:, :, a * D:(a + 1) * D]
                v.tensor_tensor(x, x, spread(n2[:, a, :], 2, D), ALU.mult).then_inc(*own.up())
            e.wait_ge(*own.done())


NORM_AT = 4


def load_sum(k, e, v, a, b, loaded, own):
    e.wait_ge(*loaded)
    v.tensor_tensor(a, a, b, ALU.add).then_inc(*own.up())
    e.wait_ge(*own.done())


def scan_weights(k, fp, gates, dram, ccol):
    nc = k.nc
    with Stage(k, "weights") as st:
        a0, a1 = st.sb("a0", [D, HID]), st.sb("a1", [D, HID])
        ones, zero, one = st.sb("ones", [C, C]), st.sb("zero", [C, C]), st.sb("one", [1, 1])
        qk, gt = st.sb("qk", [C, 2, D]), st.sb("gt", [C, GATES])
        qkt = st.sb("qkt", [D, 2, C])
        diag, own_g = st.sb("diag", [C, 2, C]), st.sb("own_g", [C, C])
        m2, oma, u, cr = st.sb("m2", [C, C]), st.sb("oma", [C, C]), st.sb("u", [C, C + 1]), st.sb("cr", [C, C + 1])
        cc, uq, w1, wr = st.sb("cc", [C, 2]), st.sb("uq", [C, C]), st.sb("w1", [C, C]), st.sb("wr", [C, 2, C])
        kq = st.sb("kq", [C, 2, HID])
        pt, pb, pg = st.ps("pt", [D, 2, C]), st.ps("pb", [C, 2, C]), st.ps("pg", [C, 2, C])
        pa, pc, pw = st.ps("pa", [C, 2, HID]), st.ps("pc", [C, 2]), st.ps("pw", [C, 2, C])
        loaded, const = st.sem("weights_loaded"), st.sem("constants")
        own = st.steps("vector_steps")
        xc, trd, trk, dg = st.sig("qk_copied", 1), st.sig("qk_transposed", 1), st.sig("qk_kept", 1), st.sig("diagonals", 1)
        bd, sd, gd, wd = st.sig("rows_spread", 1), st.sig("scanned", 1), st.sig("grams_done", 1), st.sig("weighted", 4)
        cd, cck, wtd, wtk = st.sig("c_turned", 1), st.sig("c_kept", 2), st.sig("weights_turned", 1), st.sig("weights_kept", 1)
        kak, stored = st.sig("first_terms_kept", 2), st.sig("stored", 6, 16)
        vdone = st.sem("v_stored")
        block = st.block()

        @block.sync
        def _(e):
            e.dma_start(a0[:, :], k.ins["t_w0"]).then_inc(loaded, 16)
            e.dma_start(a1[:, :], k.ins["t_p0"]).then_inc(loaded, 16)
            e.dma_start(dram["v"].rearrange("b t d -> t b d"), fp[:, :, 2 * D:3 * D]).then_inc(vdone, 16)
            stored.seed(e)
            with e.Fori(0, NB) as i:
                def row(t):
                    return t[bass.ds(i, 1)]
                k.wait("sync", e, *kak.now(i))
                e.dma_start(row(dram["ka"]).rearrange("o t h -> (o t) h"), kq[:, 0, :]).then_inc(*stored.up())
                e.dma_start(row(dram["qa"]).rearrange("o t h -> (o t) h"), kq[:, 1, :]).then_inc(*stored.up())
                k.wait("sync", e, *wtk.now(i))
                e.dma_start(row(dram["w"]).rearrange("o t h -> (o t) h"), wr[:, :, :].rearrange("p a s -> p (a s)")).then_inc(*stored.up())
                e.dma_start(row(dram["uq"])[:, :, 0, :].rearrange("o s t -> (o s) t"), uq[:, :]).then_inc(*stored.up())
                e.dma_start(row(dram["uq"])[:, :, 1, :].rearrange("o s t -> (o s) t"), u[:, 1:C + 1]).then_inc(*stored.up())
                e.dma_start(row(dram["c"]), cr[0:1, :]).then_inc(*stored.up())
            e.wait_ge(*stored.now(NB - 1))
            e.wait_ge(vdone, 16)

        @block.gpsimd
        def _(e):
            e.memset(ones[:, :], 1.0).then_inc(const, 1)
            e.memset(zero[:, :], 0.0).then_inc(const, 1)
            e.memset(one[:, :], 1.0).then_inc(const, 1)
            e.memset(u[:, 0:1], 0.0).then_inc(const, 1)
            e.memset(cr[:, 0:1], 1.0).then_inc(const, 1)

        @block.vector
        def _(e):
            v = nc.vector
            for s in (xc, dg, sd, wd, cck):
                s.seed(e)
            load_sum(k, e, v, a0[:, :], a1[:, :], (loaded, 32), own)
            e.sem_inc(const, 1)
            e.wait_ge(const, 6)
            first = own.n
            with e.Fori(0, NB) as i:
                own.n = first
                own.turn(i, 4)
                k.wait("vector", e, *bd.prev(i))
                v.tensor_copy(gt[:, :], gates[:, bass.ds(i, 1), :].rearrange("p o g -> p (o g)")).then_inc(*own.up())
                v.tensor_copy(qk[:, :, :], fp[:, bass.ds(i, 1), 0:2 * D].rearrange("p o (a d) -> p (o a) d", a=2)).then_inc(*xc.up())
                k.wait("vector", e, *own.done())
                v.tensor_scalar(own_g[:, :], k.ident[:, :], gt[:, 1:2], -2.0, ALU.mult, ALU.mult).then_inc(*own.up())
                v.tensor_scalar(diag[:, 0, :], k.ident[:, :], gt[:, 2:3], None, ALU.mult).then_inc(*own.up())
                v.tensor_scalar(diag[:, 1, :], k.ident[:, :], gt[:, 0:1], None, ALU.mult).then_inc(*dg.up())
                k.wait("vector", e, *own.done())
                k.wait("vector", e, *bd.now(i))
                v.tensor_scalar(oma[:, :], pb[:, 1, :], -1.0, 1.0, ALU.mult, ALU.add).then_inc(*own.up())
                v.tensor_tensor_scan(m2[:, :], pb[:, 0, :], own_g[:, :], 0.0, ALU.mult, ALU.add).then_inc(*sd.up())
                k.wait("vector", e, *own.done())
                k.wait("vector", e, *sd.now(i))
                k.wait("vector", e, *stored.prev(i))
                v.tensor_tensor_scan(u[:, 1:C + 1], oma[:, :], m2[:, :], 0.0, ALU.mult, ALU.add).then_inc(*wd.up())
                v.tensor_tensor_scan(cr[:, 1:C + 1], oma[:, :], zero[:, :], 1.0, ALU.mult, ALU.add).then_inc(*wd.up())
                k.wait("vector", e, *wd.now(i, 1))
                k.wait("vector", e, *gd.now(i))
                v.tensor_tensor(uq[:, :], pg[:, 0, :], u[:, 1:C + 1], ALU.mult).then_inc(*wd.up())
                v.tensor_tensor(w1[:, :], pg[:, 1, :], u[:, 0:C], ALU.mult).then_inc(*wd.up())
                k.wait("vector", e, *cd.now(i))
                k.wait("vector", e, *kak.prev(i))
                v.tensor_copy(cc[:, :], pc[:, :]).then_inc(*cck.up())
                v.tensor_copy(ccol[:, bass.ds(i, 1)], pc[:, 1:2]).then_inc(*cck.up())
                own.end()
            e.wait_ge(*cck.now(NB - 1))

        @block.scalar
        def _(e):
            for s in (trk, wtk, kak):
                s.seed(e)
            with e.Fori(0, NB) as i:
                k.wait("scalar", e, *trd.now(i))
                k.wait("scalar", e, *gd.prev(i))
                e.activation(qkt[:, :, :], pt[:, :, :], ACT.Copy).then_inc(*trk.up())
                k.wait("scalar", e, *cck.now(i))
                k.wait("scalar", e, *stored.prev(i))
                for a in range(2):
                    e.activation(kq[:, a, :], pa[:, a, :], ACT.Copy, scale=cc[:, a:a + 1]).then_inc(*kak.up())
                k.wait("scalar", e, *wtd.now(i))
                e.activation(wr[:, :, :], pw[:, :, :], ACT.Copy).then_inc(*wtk.up())

        @block.tensor
        def _(e):
            t = nc.tensor
            for s in (trd, bd, gd, cd, wtd):
                s.seed(e)
            e.wait_ge(const, 6)
            with e.Fori(0, NB) as i:
                k.wait("tensor", e, *xc.now(i))
                k.wait("tensor", e, *trk.prev(i))
                for a in range(2):
                    m = t.transpose(pt[:, a, :], qk[:, a, :], k.ident[:, :])
                m.then_inc(*trd.up())
                k.wait("tensor", e, *dg.now(i))
                k.wait("tensor", e, *sd.prev(i))
                t.matmul(pb[:, :, :], ones[:, :], diag[:, :, :], start=True, stop=True).then_inc(*bd.up())
                k.wait("tensor", e, *trk.now(i))
                k.wait("tensor", e, *wd.prev(i))
                k.wait("tensor", e, *kak.prev(i))
                t.matmul(pa[:, 0, :], qkt[:, 1, :], a0[:, :], start=True, stop=True)
                t.matmul(pa[:, 1, :], qkt[:, 0, :], a0[:, :], start=True, stop=True)
                t.matmul(pg[:, :, :], qkt[:, 1, :], qkt[:, :, :], start=True, stop=True).then_inc(*gd.up())
                k.wait("tensor", e, *wd.now(i, 1))
                k.wait("tensor", e, *cck.prev(i))
                t.matmul(pc[:, 0:1], cr[0:1, 0:C], one[:, :], start=True, stop=True)
                t.matmul(pc[:, 1:2], cr[0:1, 1:C + 1], one[:, :], start=True, stop=True).then_inc(*cd.up())
                k.wait("tensor", e, *wd.now(i))
                k.wait("tensor", e, *wtk.prev(i))
                t.transpose(pw[:, 0, :], w1[:, :], k.ident[:, :])
                t.transpose(pw[:, 1, :], u[:, 0:C], k.ident[:, :]).then_inc(*wtd.up())


def scan(k, dram):
    nc = k.nc
    HH, DD = HID // 2, D // 2
    with Stage(k, "scan") as st:
        hh, gg, ee = st.sb("hh", [128, C, HH]), st.sb("gg", [128, C, HH]), st.sb("ee", [128, C, DD])
        wc, ka, vc = st.sb("wc", [128, SC, 2, C]), st.sb("ka", [128, SC, HH]), st.sb("vc", [128, SC, DD])
        cp = st.sb("cp", [128, C + 1])
        tmp, part = st.sb("tmp", [128, SC * HH]), st.sb("part", [128, C // SC, HH])
        acc, pre, sg, h, ds = [st.sb(n, [128, HH]) for n in ("acc", "pre", "sg", "h", "ds")]
        gr, w = st.sb("gr", [128, C]), st.sb("w", [128, C])
        er, eacc = st.sb("er", [128, DD]), st.sb("eacc", [128, DD])
        ht, et = st.sb("ht", [128, 128]), st.sb("et", [DD, 128])
        b0, c0 = st.sb("b0", [128, 2, D]), st.sb("c0", [DD, 2, HID])
        b1 = tmp[:, 0:2 * D].rearrange("p (a d) -> p a d", a=2)
        c1 = tmp[0:DD, 2 * D:2 * D + 2 * HID].rearrange("p (a h) -> p a h", a=2)
        pair = st.sb("pair", [128, 128])
        pht, ppb, pgr, pet, pdb = st.ps("pht", [128, 128]), st.ps("ppb", [128, DD]), st.ps("pgr", [128, 2, 512]), st.ps("pet", [DD, 128]), st.ps("pdb", [128, HH])
        loaded, cleared, const = st.sem("weights_loaded"), st.sem("cleared"), st.sem("constants")
        chunk, over, kept = st.sem("chunk_loaded"), st.sem("chunk_over"), st.sem("histories_stored")
        own = st.steps("vector_steps")
        pr, sgd, hd = st.sig("pre_done", 1), st.sig("sigmoid_done", 1), st.sig("hidden_done", 1)
        htd, htk, pbd = st.sig("hidden_turned", 1), st.sig("hidden_kept", 1), st.sig("first_prediction_done", 1)
        grd, prd = st.sig("gram_halves", 2), st.sig("gram_sums", 2)
        ed, etd, etk, dbd = st.sig("error_done", 1), st.sig("error_turned", 1), st.sig("error_kept", 1), st.sig("first_backward_done", 1)
        gdone = st.sig("gradient_done", 1)
        block = st.block()

        @block.sync
        def _(e):
            for t, n in ((b0, "t_w1"), (b1, "t_p1"), (c0, "t_w1t"), (c1, "t_p1t")):
                e.dma_start(t[:, :, :], k.ins[n]).then_inc(loaded, 16)
            for a in range(2):
                e.dma_start(cp[64 * a:64 * a + 64, :], dram["c"]).then_inc(loaded, 16)
            for c in range(C // SC):
                s = slice(c * SC, (c + 1) * SC)
                if c:
                    e.wait_ge(over, c)
                for a in range(2):
                    r = slice(64 * a, 64 * a + 64)
                    e.dma_start(wc[r, :, :, :].rearrange("p t a s -> p t (a s)"), dram["w"][:, s, :]).then_inc(chunk, 16)
                    e.dma_start(ka[r, :, :], dram["ka"][:, s, a * HH:(a + 1) * HH]).then_inc(chunk, 16)
                    e.dma_start(vc[r, :, :], dram["v"][:, s, a * DD:(a + 1) * DD]).then_inc(chunk, 16)
            e.wait_ge(over, C // SC)
            for a in range(2):
                r = slice(64 * a, 64 * a + 64)
                e.dma_start(dram["g"][:, :, a * HH:(a + 1) * HH], gg[r, :, :]).then_inc(kept, 16)
                e.dma_start(dram["h"][:, :, a * HH:(a + 1) * HH], hh[r, :, :]).then_inc(kept, 16)
                e.dma_start(dram["e"][:, :, a * DD:(a + 1) * DD], ee[r, :, :]).then_inc(kept, 16)
            e.wait_ge(kept, 96)

        @block.gpsimd
        def _(e):
            e.memset(gg[:, :, :], 0.0).then_inc(cleared, 1)
            e.memset(ee[:, :, :], 0.0).then_inc(cleared, 1)
            e.memset(hh[:, :, :], 0.0).then_inc(cleared, 1)
            e.memset(gr[:, :], 0.0).then_inc(cleared, 1)

        @block.vector
        def _(e):
            v = nc.vector
            for s in (pr, hd, grd, ed, gdone):
                s.seed(e)

            def settle():
                k.wait("vector", e, *own.done())
            for a in range(2):
                for b in range(2):
                    v.tensor_copy(pair[64 * a:64 * a + 64, 64 * b:64 * b + 64],
                                  k.ident[64 * a:64 * a + 64, 64 * a:64 * a + 64]).then_inc(const, 1)
            e.wait_ge(loaded, 96)
            v.tensor_tensor(b0[:, :, :], b0[:, :, :], b1[:, :, :], ALU.add).then_inc(const, 1)
            v.tensor_tensor(c0[:, :, :], c0[:, :, :], c1[:, :, :], ALU.add).then_inc(const, 1)
            e.wait_ge(const, 6)
            e.wait_ge(cleared, 4)

            def mix_rows(rows, coef, n, width, out):
                step = SC * HH // width
                cuts = [(o, min(step, n - o)) for o in range(0, n, step)]
                for b, (o, m) in enumerate(cuts):
                    t = tmp[:, 0:m * width].rearrange("p (s w) -> p s w", s=m)
                    v.tensor_tensor(t, rows[:, o:o + m, :], spread(coef[:, o:o + m], 2, width), ALU.mult).then_inc(*own.up())
                    settle()
                    to = out if len(cuts) == 1 else part[:, b, 0:width]
                    v.tensor_reduce(to, t.rearrange("p s w -> p w s"), axis=AX.X, op=ALU.add).then_inc(*own.up())
                    settle()
                if len(cuts) > 1:
                    v.tensor_reduce(out, part[:, 0:len(cuts), 0:width].rearrange("p b w -> p w b"),
                                    axis=AX.X, op=ALU.add).then_inc(*own.up())
                    settle()

            def dots(rows, vec, n, width, out, signal):
                step = SC * HH // width
                for o in range(0, n, step):
                    m = min(step, n - o)
                    t = tmp[:, 0:m * width].rearrange("p (s w) -> p s w", s=m)
                    v.tensor_tensor(t, rows[:, o:o + m, :], spread(vec, 1, m), ALU.mult).then_inc(*own.up())
                    settle()
                    v.tensor_reduce(out[:, o:o + m], t, axis=AX.X, op=ALU.add).then_inc(
                        *(signal.up() if o + m >= n else own.up()))
                    if o + m < n:
                        settle()

            for c in range(C // SC):
                n = SC * (c + 1)
                e.wait_ge(chunk, 96 * (c + 1))
                if c:
                    own.leave(SC)
                first = own.n
                with e.Fori(0, SC) as it:
                    i = it + c * SC
                    own.n = first
                    own.turn(it, scan_steps(c))
                    u_row = wc[:, bass.ds(it, 1), 1, 0:n].rearrange("p o s -> p (o s)")
                    w_row = wc[:, bass.ds(it, 1), 0, 0:n].rearrange("p o s -> p (o s)")
                    one = lambda t, j: t[:, bass.ds(j, 1), :].rearrange("p o w -> p (o w)")
                    mix_rows(gg, w_row, n, HH, acc[:, :])
                    v.tensor_tensor(pre[:, :], acc[:, :], one(ka, it), ALU.add).then_inc(*pr.up())
                    k.wait("vector", e, *sgd.now(i))
                    k.wait("vector", e, *pr.now(i))
                    v.tensor_tensor(h[:, :], pre[:, :], sg[:, :], ALU.mult).then_inc(*hd.up())
                    k.wait("vector", e, *hd.now(i))
                    v.tensor_tensor(ds[:, :], h[:, :], sg[:, :], ALU.mult).then_inc(*own.up())
                    settle()
                    v.tensor_tensor(ds[:, :], h[:, :], ds[:, :], ALU.subtract).then_inc(*own.up())
                    settle()
                    v.tensor_tensor(ds[:, :], ds[:, :], sg[:, :], ALU.add).then_inc(*own.up())
                    dots(hh, h[:, :], n, HH, gr, grd)
                    k.wait("vector", e, *prd.now(i, 0))
                    v.tensor_tensor(w[:, 0:n], pgr[:, 0, 0:n], u_row, ALU.mult).then_inc(*own.up())
                    settle()
                    mix_rows(ee, w, n, DD, eacc[:, :])
                    k.wait("vector", e, *pbd.now(i))
                    v.scalar_tensor_tensor(eacc[:, :], ppb[:, :], cp[:, bass.ds(i, 1)], eacc[:, :], ALU.mult, ALU.add).then_inc(*own.up())
                    settle()
                    v.tensor_tensor(eacc[:, :], eacc[:, :], one(vc, it), ALU.subtract).then_inc(*own.up())
                    settle()
                    v.tensor_scalar(er[:, :], eacc[:, :], 2.0 / D, None, ALU.mult).then_inc(*ed.up())
                    k.wait("vector", e, *ed.now(i))
                    dots(ee, er[:, :], n, DD, gr, grd)
                    k.wait("vector", e, *prd.now(i, 1))
                    v.tensor_tensor(w[:, 0:n], pgr[:, 1, 0:n], u_row, ALU.mult).then_inc(*own.up())
                    settle()
                    mix_rows(hh, w, n, HH, acc[:, :])
                    k.wait("vector", e, *dbd.now(i))
                    v.scalar_tensor_tensor(acc[:, :], pdb[:, :], cp[:, bass.ds(i, 1)], acc[:, :], ALU.mult, ALU.add).then_inc(*own.up())
                    settle()
                    v.tensor_copy(one(hh, i), h[:, :]).then_inc(*own.up())
                    v.tensor_copy(one(ee, i), er[:, :]).then_inc(*own.up())
                    v.tensor_tensor(one(gg, i), acc[:, :], ds[:, :], ALU.mult).then_inc(*gdone.up())
                    k.wait("vector", e, *gdone.now(i))
                    own.end()
                e.sem_inc(over, 1)

        @block.scalar
        def _(e):
            for s in (sgd, htk, etk):
                s.seed(e)
            with e.Fori(0, C) as i:
                k.wait("scalar", e, *pr.now(i))
                e.activation(sg[:, :], pre[:, :], ACT.Sigmoid).then_inc(*sgd.up())
                k.wait("scalar", e, *htd.now(i))
                e.activation(ht[:, :], pht[:, :], ACT.Copy).then_inc(*htk.up())
                k.wait("scalar", e, *etd.now(i))
                e.activation(et[:, :], pet[:, :], ACT.Copy).then_inc(*etk.up())

        @block.tensor
        def _(e):
            t = nc.tensor
            for s in (htd, pbd, prd, etd, dbd):
                s.seed(e)
            e.wait_ge(const, 6)
            with e.Fori(0, C) as i:
                k.wait("tensor", e, *hd.now(i))
                t.transpose(pht[:, :], h[:, :], k.ident[:, :]).then_inc(*htd.up())
                k.wait("tensor", e, *htk.now(i))
                for to in range(2):
                    for a in range(2):
                        m = t.matmul(ppb[64 * to:64 * to + 64, :], ht[:, 64 * a:64 * a + 64],
                                     b0[:, a, DD * to:DD * to + DD], start=a == 0, stop=a == 1)
                m.then_inc(*pbd.up())
                k.wait("tensor", e, *grd.now(i, 0))
                t.matmul(pgr[:, 0, 0:C], pair[:, :], gr[:, :], start=True, stop=True).then_inc(*prd.up())
                k.wait("tensor", e, *ed.now(i))
                t.transpose(pet[:, :], er[:, :], k.ident[:, :]).then_inc(*etd.up())
                k.wait("tensor", e, *etk.now(i))
                for to in range(2):
                    for a in range(2):
                        m = t.matmul(pdb[64 * to:64 * to + 64, :], et[:, 64 * a:64 * a + 64],
                                     c0[:, a, HH * to:HH * to + HH], start=a == 0, stop=a == 1)
                m.then_inc(*dbd.up())
                k.wait("tensor", e, *grd.now(i, 1))
                t.matmul(pgr[:, 1, 0:C], pair[:, :], gr[:, :], start=True, stop=True).then_inc(*prd.up())


def scan_steps(c):
    n = SC * (c + 1)
    wide, thin = c + 1, (n + 63) // 64
    mix = lambda m: 2 * m + (m > 1)
    return 2 * mix(wide) + mix(thin) + (2 * wide - 1) + (2 * thin - 1) + 10


def scan_outputs(k, dram, ccol):
    nc = k.nc
    with Stage(k, "answers") as st:
        gb, hb, eb = st.sb("gb", [C, HID]), st.sb("hb", [C, HID]), st.sb("eb", [C, D])
        uq, qa = st.sb("uq", [C, 2, C]), st.sb("qa", [C, HID])
        pre, hq, tt, w = st.sb("pre", [C, HID]), st.sb("hq", [C, HID]), st.sb("tt", [128, 4, C]), st.sb("w", [C, C])
        y = st.sb("y", [C, D])
        b0, b1 = st.sb("b0", [128, 2, D]), st.sb("b1", [128, 2, D])
        pp, ptt, pg, po = st.ps("pp", [C, HID]), st.ps("ptt", [128, 4, C]), st.ps("pg", [C, C]), st.ps("po", [C, 2, D])
        pb = st.ps("pb", [C, D])
        loaded = st.sem("weights_loaded")
        own = st.steps("vector_steps")
        ld = st.sig("batch_loaded", 5, 16)
        ppd, prd, hqd = st.sig("history_term", 1), st.sig("pre_done", 1), st.sig("hidden_done", 1)
        trd, trk, gd, wd = st.sig("turned", 1), st.sig("turned_kept", 1), st.sig("gram_done", 1), st.sig("weighted", 1)
        od, rd = st.sig("out_done", 1), st.sig("resid_done", 1)
        block = st.block()

        @block.sync
        def _(e):
            for t, n in ((b0, "t_w1"), (b1, "t_p1")):
                e.dma_start(t[:], k.ins[n]).then_inc(loaded, 16)
            ld.seed(e)
            with e.Fori(0, NB) as i:
                k.wait("sync", e, *rd.prev(i))
                for t, n in ((gb, "g"), (hb, "h"), (eb, "e"), (qa, "qa")):
                    e.dma_start(t[:, :], dram[n][bass.ds(i, 1), :, :].rearrange("o s w -> (o s) w")).then_inc(*ld.up())
                e.dma_start(uq[:, :, :], dram["uq"][bass.ds(i, 1), :, :, :].rearrange("o s a t -> (o s) a t")).then_inc(*ld.up())

        @block.tensor
        def _(e):
            t = nc.tensor
            for s in (ppd, trd, gd, od):
                s.seed(e)
            e.wait_ge(own.sem, 1)
            with e.Fori(0, NB) as i:
                k.wait("tensor", e, *ld.now(i))
                t.matmul(pp[:, :], uq[:, 0, :], gb[:, :], start=True, stop=True).then_inc(*ppd.up())
                k.wait("tensor", e, *hqd.now(i))
                for a, x in enumerate((hb, hb, hq, hq)):
                    m = t.transpose(ptt[:, a, :], x[:, (a % 2) * 128:(a % 2 + 1) * 128], k.ident[:, :])
                m.then_inc(*trd.up())
                k.wait("tensor", e, *trk.now(i))
                for a in range(2):
                    m = t.matmul(pg[:, :], tt[:, a, :], tt[:, 2 + a, :], start=a == 0, stop=a == 1)
                m.then_inc(*gd.up())
                for a in range(2):
                    t.matmul(pb[:, :], tt[:, 2 + a, :], b0[:, a, :], start=a == 0, stop=a == 1)
                k.wait("tensor", e, *wd.now(i))
                t.matmul(po[:, 0, :], w[:, :], eb[:, :], start=True, stop=True).then_inc(*od.up())

        @block.scalar
        def _(e):
            for s in (hqd, trk):
                s.seed(e)
            with e.Fori(0, NB) as i:
                k.wait("scalar", e, *prd.now(i))
                e.activation(hq[:, :], pre[:, :], ACT.Silu).then_inc(*hqd.up())
                k.wait("scalar", e, *trd.now(i))
                e.activation(tt[:, :, :], ptt[:, :, :], ACT.Copy).then_inc(*trk.up())

        @block.vector
        def _(e):
            v = nc.vector
            for s in (prd, wd, rd):
                s.seed(e)
            load_sum(k, e, v, b0[:, :, :], b1[:, :, :], (loaded, 32), own)
            first = own.n
            with e.Fori(0, NB) as i:
                own.n = first
                own.turn(i, 1)
                k.wait("vector", e, *ppd.now(i))
                v.tensor_tensor(pre[:, :], pp[:, :], qa[:, :], ALU.add).then_inc(*prd.up())
                k.wait("vector", e, *gd.now(i))
                v.tensor_tensor(w[:, :], pg[:, :], uq[:, 1, :], ALU.mult).then_inc(*wd.up())
                k.wait("vector", e, *od.now(i))
                r = k.resid[:, bass.ds(i * D, D)]
                v.scalar_tensor_tensor(y[:, :], pb[:, :], ccol[:, bass.ds(i, 1)], r, ALU.mult, ALU.add).then_inc(*own.up())
                k.wait("vector", e, *own.done())
                v.tensor_tensor(r, y[:, :], po[:, 0, :], ALU.add).then_inc(*rd.up())
                own.end()


def experts(k, xt):
    nc = k.nc
    G, NG = 4, NB // 4
    with Stage(k, "experts") as st:
        wr, w1, w2 = st.sb("wr", [D + 1, EXPERTS]), st.sb("w1", [D + 1, EXPERTS, DFF]), st.sb("w2", [DFF, EXPERTS, D])
        b2 = st.sb("b2", [C, EXPERTS, D])
        iot = st.sb("iot", [C, EXPERTS])
        xs = st.sb("xs", [D + 1, G * C])
        lg, top, place, pf = st.sb("lg", [C, G, 8]), st.sb("top", [C, G, 8]), st.sb("place", [C, G, 8], U32), st.sb("pf", [C, G, 8])
        gap, e2, share = st.sb("gap", [C, G]), st.sb("e2", [C, G]), st.sb("share", [C, G, 2])
        one_hot, wf = st.sb("one_hot", [C, G, 2, 8]), st.sb("wf", [C, G, 8])
        hb = st.sb("hb", [DFF, 2, G * C])
        prod, y = st.sb("prod", [C, 2, EXPERTS, D]), st.sb("y", [C, G, D])
        py, ph, pl = st.ps("py", [C, G, EXPERTS * D]), st.ps("ph", [DFF, 2, G * C]), st.ps("pl", [C, G, 8])
        loaded, const = st.sem("weights_loaded"), st.sem("constants")
        own = st.steps("vector_steps")
        xc, ld, gp, ex2 = st.sig("x_copied", 1), st.sig("logits_done", 1), st.sig("gap_done", 1), st.sig("gap_exp", 1)
        lk = st.sig("logits_kept", 1)
        hd, gl, rd = st.sig("hidden_done", EXPERTS), st.sig("gelu_done", EXPERTS), st.sig("resid_done", 1)
        yu = st.sig("answers_used", G)
        used = st.sig("hidden_used", EXPERTS)
        block = st.block()

        @block.sync
        def _(e):
            for t, n in ((wr, "m_wr"), (w1, "m_w1"), (w2, "m_w2")):
                e.dma_start(t[:], k.ins[n]).then_inc(loaded, 16)
            e.dma_start(b2[:, :, :].rearrange("p x d -> p (x d)"), k.ins["m_b2"].to_broadcast([C, EXPERTS * D])).then_inc(loaded, 16)

        @block.gpsimd
        def _(e):
            e.iota(iot[:, :], [[1, EXPERTS]], base=0, channel_multiplier=0,
                   allow_small_or_imprecise_dtypes=True).then_inc(const, 1)

        @block.tensor
        def _(e):
            t = nc.tensor
            for s in (ld, hd, used):
                s.seed(e)
            e.wait_ge(loaded, 64)
            e.wait_ge(const, 1)
            with e.Fori(0, NG) as i:
                k.wait("tensor", e, *xc.now(i))
                k.wait("tensor", e, *lk.prev(i))
                for g in range(G):
                    m = t.matmul(pl[:, g, :], xs[:, g * C:(g + 1) * C], wr[:, :], start=True, stop=True)
                m.then_inc(*ld.up())

                def hidden(x):
                    k.wait("tensor", e, *(gl.now(i, x - 2) if x >= 2 else gl.prev(i, x + EXPERTS - 2)))
                    t.matmul(ph[:, x % 2, :], w1[:, x, :], xs[:, :], start=True, stop=True).then_inc(*hd.up())
                hidden(0)
                for g in range(G):
                    k.wait("tensor", e, *yu.prev(i, g))
                for x in range(EXPERTS):
                    if x + 1 < EXPERTS:
                        hidden(x + 1)
                    k.wait("tensor", e, *gl.now(i, x))
                    for g in range(G):
                        m = t.matmul(py[:, g, x * D:(x + 1) * D], hb[:, x % 2, g * C:(g + 1) * C], w2[:, x, :],
                                     start=True, stop=True)
                    m.then_inc(*used.up())

        @block.scalar
        def _(e):
            for s in (ex2, gl):
                s.seed(e)
            with e.Fori(0, NG) as i:
                for x in range(EXPERTS):
                    k.wait("scalar", e, *hd.now(i, x))
                    k.wait("scalar", e, *(used.now(i, x - 2) if x >= 2 else used.prev(i, x + EXPERTS - 2)))
                    e.activation(hb[:, x % 2, :], ph[:, x % 2, :], ACT.Gelu).then_inc(*gl.up())
                k.wait("scalar", e, *gp.now(i))
                e.activation(e2[:, :], gap[:, :], ACT.Exp).then_inc(*ex2.up())

        @block.vector
        def _(e):
            v = nc.vector
            for s in (xc, lk, gp, yu, rd):
                s.seed(e)
            e.wait_ge(const, 1)
            e.wait_ge(loaded, 64)

            def settle():
                k.wait("vector", e, *own.done())
            with e.Fori(0, NG) as i:
                own.n = 0
                own.turn(i, PER_EXPERTS)
                k.wait("vector", e, *used.prev(i))
                v.tensor_copy(xs[:, :], xt[:, bass.ds(i * G * C, G * C)]).then_inc(*xc.up())
                k.wait("vector", e, *ld.now(i))
                v.tensor_copy(lg[:, :, :], pl[:, :, :]).then_inc(*lk.up())
                k.wait("vector", e, *lk.now(i))
                for g in range(G):
                    v.max(top[:, g, :], lg[:, g, :]).then_inc(*own.up())
                settle()
                for g in range(G):
                    v.max_index(place[:, g, :], top[:, g, :], lg[:, g, :]).then_inc(*own.up())
                v.tensor_tensor(gap[:, :], top[:, :, 1], top[:, :, 0], ALU.subtract).then_inc(*gp.up())
                settle()
                v.tensor_copy(pf[:, :, :], place[:, :, :]).then_inc(*own.up())
                settle()
                v.tensor_tensor(one_hot[:, :, :, :], spread(pf[:, :, 0:2], 3, 8),
                                spread(spread(iot[:, :], 1, 2), 1, G), ALU.is_equal).then_inc(*own.up())
                k.wait("vector", e, *ex2.now(i))
                v.tensor_scalar(share[:, :, 0], e2[:, :], 1.0, None, ALU.add).then_inc(*own.up())
                settle()
                v.reciprocal(share[:, :, 0], share[:, :, 0]).then_inc(*own.up())
                settle()
                v.tensor_tensor(share[:, :, 1], share[:, :, 0], e2[:, :], ALU.mult).then_inc(*own.up())
                settle()
                v.tensor_tensor(one_hot[:, :, :, :], one_hot[:, :, :, :], spread(share[:, :, :], 3, 8), ALU.mult).then_inc(*own.up())
                settle()
                v.tensor_tensor(wf[:, :, :], one_hot[:, :, 0, :], one_hot[:, :, 1, :], ALU.add).then_inc(*own.up())
                settle()
                k.wait("vector", e, *used.now(i))
                for g in range(G):
                    v.tensor_tensor(prod[:, g % 2, :, :], py[:, g, :].rearrange("p (x d) -> p x d", x=EXPERTS),
                                    b2[:, :, :], ALU.add).then_inc(*yu.up())
                    k.wait("vector", e, *yu.now(i, g))
                    v.tensor_tensor(prod[:, g % 2, :, :], prod[:, g % 2, :, :], spread(wf[:, g, :], 2, D), ALU.mult).then_inc(*own.up())
                    settle()
                    v.tensor_reduce(y[:, g, :], prod[:, g % 2, :, :].rearrange("p x d -> p d x"), axis=AX.X, op=ALU.add).then_inc(*own.up())
                settle()
                r = k.resid[:, bass.ds(i * G * D, G * D)]
                v.tensor_tensor(r, r, y[:, :, :].rearrange("p g d -> p (g d)"), ALU.add).then_inc(*rd.up())
                own.end()


PER_EXPERTS = 23


def store(k):
    nc = k.nc
    with Stage(k, "store") as st:
        stored = st.sem("out_stored")
        block = st.block()

        @block.sync
        def _(e):
            e.dma_start(k.out.rearrange("b s d -> s b d"), k.resid[:, :].rearrange("s (b d) -> s b d", b=NB)).then_inc(stored, 16)
            e.wait_ge(stored, 16)


def build(nc, ins, out):
    with ExitStack() as ctx:
        k = Core(nc, ctx, ins, out)
        make_constants(k)
        with ExitStack() as t:
            feats = t.enter_context(nc.sbuf_tensor("feats", [C, NB * LEN3], F32))
            lrow = t.enter_context(nc.sbuf_tensor("lrow", [1, NB * LEN3], F32))
            conv_stack(k, feats)
            importance(k, feats, lrow)
            pool_frames(k, feats, lrow)
        with ExitStack() as t:
            xt = t.enter_context(nc.sbuf_tensor("xt", [D + 1, NB * C], F32))
            norm_transpose(k, "norm1", xt)
            odd_attention(k, xt)
        with ExitStack() as t:
            xt = t.enter_context(nc.sbuf_tensor("xt2", [D + 1, NB * C], F32))
            norm_transpose(k, "norm2", xt)
            key_memory(k, xt)
        ccol = ctx.enter_context(nc.sbuf_tensor("ccol", [C, NB], F32))
        shapes = {"v": (NB, C, D), "ka": (NB, C, HID), "qa": (NB, C, HID), "w": (NB, C, 2 * C), "uq": (NB, C, 2, C),
                  "c": (NB, C + 1), "g": (NB, C, HID), "h": (NB, C, HID), "e": (NB, C, D)}
        dram = {n: nc.dram_tensor(f"history_{n}", s, F32, kind="Internal").ap() for n, s in shapes.items()}
        with ExitStack() as t:
            fp = t.enter_context(nc.sbuf_tensor("fp", [C, NB, 3 * D + GATES], F32))
            gates = t.enter_context(nc.sbuf_tensor("gates", [C, NB, GATES], F32))
            with ExitStack() as u:
                xt = u.enter_context(nc.sbuf_tensor("xt3", [D + 1, NB * C], F32))
                norm_transpose(k, "norm3", xt)
                gated_features(k, xt, fp, gates)
            scan_weights(k, fp, gates, dram, ccol)
        scan(k, dram)
        scan_outputs(k, dram, ccol)
        with ExitStack() as t:
            xt = t.enter_context(nc.sbuf_tensor("xt4", [D + 1, NB * C], F32))
            norm_transpose(k, "norm4", xt, "m_affine")
            experts(k, xt)
        store(k)


def laid_out(a):
    import numpy as np
    t = lambda n: np.asarray(a["L0_tok_" + n])
    x = np.pad(np.asarray(a["x"])[:, 0, :], ((0, 0), (3, 4)), mode="reflect")
    o = {"x": x[:, :5 * (LEN0 + 1)].reshape(NB, LEN0 + 1, 5).transpose(0, 2, 1)}
    o["conv0"] = t("conv0_w")[:, 0, :].T
    for n in (1, 2, 3):
        o[f"conv{n}"] = t(f"conv{n}_w").transpose(1, 2, 0)
    o["conv_b"] = np.stack([t(f"conv{n}_b") for n in range(4)], 1)
    o["norm_g"] = np.stack([t(f"n{n}_w") for n in range(5)], 1)
    o["norm_b"] = np.stack([t(f"n{n}_b") for n in range(5)], 1)
    o["mlp_w1"] = t("mlp_w1")
    o["mlp_w2"] = t("mlp_w2").reshape(4, C, DMLP).transpose(1, 0, 2)
    o["mlp_w3"] = t("mlp_w3").reshape(4, C).T
    o["mlp_b1"] = t("mlp_b1").reshape(4, C).T
    o["mlp_b2"] = t("mlp_b2").reshape(4, C).T
    o["mlp_b3"] = t("mlp_b3").reshape(1, 1)
    b = lambda n: np.asarray(a["L0_attn_" + n])
    for n in "QKV":
        w = b("W_" + n).transpose(1, 0, 2).reshape(D, HEADS * DH)
        o["a_w" + n.lower()] = np.concatenate([w, b("b_" + n).reshape(1, -1)], 0)
    o["a_wo"] = b("W_O").reshape(2, 128, D).transpose(1, 0, 2)
    o["a_bo"] = b("b_O").reshape(1, D)
    f = lambda n: np.asarray(a["L0_ffn_" + n])
    o["k_wpk"] = f("Wq_pk").T.reshape(16, 32, D).transpose(1, 0, 2)
    o["k_keys"] = f("pk_keys").transpose(3, 0, 2, 1).reshape(32, 16, NKEY)
    o["k_wq"] = f("Wq")
    o["k_wo"] = f("Wo").reshape(4, 128, D).transpose(1, 0, 2)
    o["k_table"] = np.concatenate([f("keys_table"), f("values_table")], 1)
    g = lambda n: np.asarray(a["L1_attn_" + n])
    o["t_wf"] = g("W_fused").T
    o["t_w0"], o["t_p0"] = g("W0"), g("P0")
    for n, w in (("w1", g("W1")), ("p1", g("P1"))):
        o["t_" + n] = w.reshape(2, 128, D).transpose(1, 0, 2)
        o["t_" + n + "t"] = w.T.reshape(2, D // 2, HID).transpose(1, 0, 2)
    h = lambda n: np.asarray(a["L1_ffn_" + n])
    o["m_affine"] = np.stack([h("gamma"), h("beta")], 1)
    o["m_wr"] = np.concatenate([h("Wr"), h("br").reshape(1, EXPERTS)], 0)
    o["m_w1"] = np.concatenate([h("W1").transpose(1, 0, 2), h("b1").reshape(1, EXPERTS, DFF)], 0)
    o["m_w2"] = h("W2").transpose(1, 0, 2)
    o["m_b2"] = h("b2").reshape(1, EXPERTS * D)
    return {n: np.ascontiguousarray(v) for n, v in o.items()}


def kernel(**inputs):
    import concourse.bacc as _bacc
    from concourse import mybir as _mybir
    from concourse.bass_utils import run_bass_kernel_spmd as _run

    nc = _bacc.Bacc("TRN2", target_bir_lowering=False, num_devices=1)
    arrays = laid_out(inputs)
    ins = {n: nc.dram_tensor(n, v.shape, _mybir.dt.from_np(v.dtype), kind="ExternalInput").ap()
           for n, v in arrays.items()}
    out = nc.dram_tensor("out", (NB, C, D), _mybir.dt.float32, kind="ExternalOutput").ap()
    build(nc, ins, out)
    r = _run(nc, [arrays], core_ids=[0])
    return r.results[0]["out"]
```

```python
import concourse.bass as bass
from concourse import mybir
from contextlib import ExitStack

F32 = mybir.dt.float32
U32 = mybir.dt.uint32
ALU = mybir.AluOpType
ACT = mybir.ActivationFunctionType
AX = mybir.AxisListType
EPS = 1e-5

NB = 64
C = 128
D = 64
LEN0, LEN1, LEN2, LEN3 = 2048, 512, 256, 128
DMLP = 512
HEADS, DH = 8, 32
NKEY, NKV, TOPK = 64, 4096, 16
HID = 256
EXPERTS, DFF = 8, 128
BIG = 1.0e30


class Signal:

    def __init__(self, nc, ctx, name, per, by=1, seeded=True):
        self.sem, self.per, self.by = ctx.enter_context(nc.semaphore(name)), per, by
        self.lead = per if seeded else 0

    def seed(self, e):
        e.sem_inc(self.sem, self.lead * self.by)

    def up(self):
        return self.sem, self.by

    def now(self, i, j=None):
        j = self.per - 1 if j is None else j
        return self.sem, (i * self.per + (self.lead + j + 1)) * self.by

    def prev(self, i, j=None):
        j = self.per - 1 if j is None else j
        assert self.lead
        return self.sem, (i * self.per + (j + 1)) * self.by


class Steps:

    def __init__(self, nc, ctx, name):
        self.sem, self.base, self.n = ctx.enter_context(nc.semaphore(name)), 0, 0

    def turn(self, i, per):
        self.base, self.per, self.n0 = i * per, per, self.n

    def end(self):
        assert self.n - self.n0 == self.per, (self.n - self.n0, self.per)

    def up(self):
        self.n += 1
        return self.sem, 1

    def done(self):
        return self.sem, self.base + self.n

    def leave(self, turns):
        self.base = 0
        self.n = self.n0 + turns * self.per


class Core:

    def __init__(self, nc, ctx, ins, out):
        self.nc, self.ctx, self.ins, self.out = nc, ctx, ins, out
        self.gates = {n: ctx.enter_context(nc.semaphore(f"{n}_passed_wait")) for n in
                      ("tensor", "vector", "scalar", "gpsimd", "sync")}
        self.resid = ctx.enter_context(nc.sbuf_tensor("resid", [C, NB * D], F32))
        self.ident = ctx.enter_context(nc.sbuf_tensor("ident", [128, 128], F32))

    def wait(self, name, e, sem, value):
        e.wait_ge(sem, value)
        e.sem_inc(self.gates[name], 1)


def spread(ap, axis, n):
    a = ap.unsqueeze(axis)
    shape = list(a.shape)
    shape[axis] = n
    return a.to_broadcast(shape)


class Stage:

    def __init__(self, k, name):
        self.k, self.nc, self.ctx, self.sems, self.name = k, k.nc, ExitStack(), [], name

    def __enter__(self):
        return self

    def sb(self, name, shape, dt=F32):
        return self.ctx.enter_context(self.nc.sbuf_tensor(f"{self.name}_{name}", shape, dt))

    def ps(self, name, shape):
        return self.ctx.enter_context(self.nc.psum_tensor(f"{self.name}_{name}", shape, F32))

    def sem(self, name):
        s = self.ctx.enter_context(self.nc.semaphore(f"{self.name}_{name}"))
        self.sems.append(s)
        return s

    def sig(self, name, per, by=1, seeded=True):
        s = Signal(self.nc, self.ctx, f"{self.name}_{name}", per, by, seeded)
        self.sems.append(s.sem)
        return s

    def steps(self, name):
        s = Steps(self.nc, self.ctx, f"{self.name}_{name}")
        self.sems.append(s.sem)
        return s

    def block(self):
        self.blk = ExitStack()
        return self.blk.enter_context(self.nc.Block())

    def __exit__(self, *a):
        if a[0] is None:
            self.blk.close()
            for s in self.sems:
                self.nc.sync.sem_clear(s)
            self.nc.all_engine_barrier()
            self.ctx.close()


def make_constants(k):
    nc = k.nc
    with Stage(k, "const") as st:
        made = st.sem("ident_made")
        block = st.block()

        @block.gpsimd
        def _(e):
            e.memset(k.ident[:, :], 0.0).then_inc(made, 1)
            e.wait_ge(made, 1)
            e.affine_select(out=k.ident[:, :], in_=k.ident[:, :], compare_op=ALU.not_equal, fill=1.0,
                            base=0, pattern=[[-1, 128]], channel_multiplier=1).then_inc(made, 1)
            e.wait_ge(made, 2)


def conv_stack(k, feats):
    nc, ins = k.nc, k.ins
    with Stage(k, "conv") as st:
        sb = st.sb
        ps = st.ps
        sig = st.sig
        w0 = sb("w0", [10, C])
        w1, w2, w3 = sb("w1", [C, 8, C]), sb("w2", [C, 4, C]), sb("w3", [C, 4, C])
        s0, ssum = sb("s0", [10, 1]), sb("ssum", [C, 16])
        bias, biasc, gamma, beta = sb("bias", [C, 4]), sb("biasc", [C, 4]), sb("gamma", [C, 5]), sb("beta", [C, 5])
        cent, avg = sb("cent", [C, C]), sb("avg", [C, C])
        xcol = sb("xcol", [10, LEN0])
        h0, h1, h2 = sb("h0", [C, LEN0 + 4]), sb("h1", [C, LEN1 + 2]), sb("h2", [C, LEN2 + 2])
        sq, normal, inv = sb("sq", [C, 7, 512]), sb("normal", [C, 7, 512]), sb("inv", [C, 7, 512])
        root, epsc = sb("root", [C, 7, 512]), sb("epsc", [C, 1])
        py = ps("py", [C, 4, 512])
        pv = ps("pv", [C, 2, 512])
        pz, pzv = ps("pz", [C, 512]), ps("pzv", [C, 512])
        loaded = st.sem("weights_loaded")
        ready = st.sem("weights_centred")
        bias_mm = st.sem("bias_product")
        setup = st.steps("vector_setup_steps")
        xin = sig("x_loaded", 1, 32, seeded=False)
        conv, var = sig("conv_done", 7), sig("variance_done", 7)
        squared, rooted, inverted = sig("squared", 7), sig("roots_done", 7), sig("inverted", 7)
        normed, relued, padded = sig("normed", 7), sig("relu_done", 7), sig("padded", 8)
        width = [512, 512, LEN1, 512, LEN2, 512, LEN3]
        layer = [0, 0, 1, 0, 2, 0, 3]
        chunks = {0: 0, 1: 1, 3: 2, 5: 3}
        yb = [py[:, chunks[s], :] if s in chunks else pz[:, 0:width[s]] for s in range(7)]
        vb = [pv[:, chunks[s] % 2, :] if s in chunks else pzv[:, 0:width[s]] for s in range(7)]

        def before(s, i, slot):
            return s.prev(i, 6) if slot == 2 else s.now(i, slot - 2)

        def empty(e, slot, *signals):
            for s in signals:
                if slot:
                    e.wait_ge(*s.prev(0, slot - 1))
                e.sem_inc(s.sem, 1)
        block = st.block()

        @block.sync
        def _(e):
            for t, n in ((w0, "conv0"), (w1, "conv1"), (w2, "conv2"), (w3, "conv3"), (bias, "conv_b"),
                         (gamma, "norm_g"), (beta, "norm_b")):
                e.dma_start(t[:], ins[n]).then_inc(loaded, 16)
            x = ins["x"]

            def load(xi):
                e.dma_start(xcol[0:5, :], xi[:, 0:LEN0]).then_inc(xin.sem, 16)
                e.dma_start(xcol[5:10, :], xi[:, 1:LEN0 + 1]).then_inc(xin.sem, 16)
            load(x[0, :, :])
            with e.Fori(0, NB - 1) as i:
                e.wait_ge(*conv.prev(i, 5))
                load(x[bass.ds(i + 1, 1), :, :].rearrange("o r t -> (o r) t"))
            e.wait_ge(*conv.now(NB - 2, 5))
            load(x[NB - 1, :, :])

        @block.tensor
        def _(e):
            t = nc.tensor

            def chunk(slot):
                q = chunks[slot]
                t.matmul(yb[slot], w0[:, :], xcol[:, q * 512:(q + 1) * 512], start=True, stop=True).then_inc(*conv.up())

            def sum_squares(slot):
                t.matmul(vb[slot], avg[:, :], sq[:, slot, 0:width[slot]], start=True, stop=True).then_inc(*var.up())
            e.wait_ge(ready, 1)
            t.matmul(pz[:, 0:4], cent[:, :], bias[:, :], start=True, stop=True).then_inc(bias_mm, 1)
            e.wait_ge(ready, 2)
            e.wait_ge(xin.sem, 32)
            for slot in range(7):
                if slot in chunks:
                    chunk(slot)
                else:
                    empty(e, slot, conv)
            for slot in range(7):
                if slot in chunks:
                    e.wait_ge(*squared.prev(0, slot))
                    if chunks[slot] >= 2:
                        e.wait_ge(*rooted.prev(0, {3: 0, 5: 1}[slot]))
                    sum_squares(slot)
                else:
                    empty(e, slot, var)
            with e.Fori(0, NB) as i:
                def convolve(slot, h, w, taps, stride, ends):
                    k.wait("tensor", e, *ends)
                    k.wait("tensor", e, *before(normed, i, slot))
                    for tap in range(taps):
                        src = h[:, tap:tap + stride * (width[slot] - 1) + 1:stride]
                        m = t.matmul(yb[slot], w[:, tap, :], src, start=tap == 0, stop=tap == taps - 1)
                    m.then_inc(*conv.up())

                def next_chunk(slot):
                    k.wait("tensor", e, *normed.prev(i, slot))
                    chunk(slot)

                def variance(slot):
                    k.wait("tensor", e, *squared.now(i, slot))
                    k.wait("tensor", e, *(rooted.prev(i, {0: 3, 1: 5}[slot]) if slot in (0, 1) else
                                          rooted.now(i, {3: 0, 5: 1}[slot]) if slot in (3, 5) else
                                          before(rooted, i, slot)))
                    sum_squares(slot)
                k.wait("tensor", e, *xin.now(i + 1))
                next_chunk(0)
                next_chunk(1)
                variance(0)
                variance(1)
                convolve(2, h0, w1, 8, 4, padded.prev(i, 7))
                next_chunk(3)
                variance(2)
                variance(3)
                convolve(4, h1, w2, 4, 2, padded.now(i, 1))
                next_chunk(5)
                variance(4)
                variance(5)
                convolve(6, h2, w3, 4, 2, padded.now(i, 3))
                variance(6)

        @block.scalar
        def _(e):
            def square(slot):
                e.activation(sq[:, slot, 0:width[slot]], yb[slot], ACT.Square,
                             bias=biasc[:, layer[slot]:layer[slot] + 1]).then_inc(*squared.up())

            def square_root(slot):
                e.activation(root[:, slot, 0:width[slot]], vb[slot], ACT.Sqrt, bias=epsc[:, 0:1]).then_inc(*rooted.up())

            def relu_to(slot, dst):
                n = layer[slot]
                e.activation(dst, normal[:, slot, 0:width[slot]], ACT.Relu,
                             bias=beta[:, n:n + 1], scale=gamma[:, n:n + 1]).then_inc(*relued.up())
            h0_part = lambda slot: h0[:, 2 + chunks[slot] * 512:2 + (chunks[slot] + 1) * 512]
            e.wait_ge(ready, 3)
            for slot in range(7):
                if slot in chunks:
                    e.wait_ge(*conv.prev(0, slot))
                    square(slot)
                else:
                    empty(e, slot, squared)
            for slot in range(7):
                if slot in chunks:
                    e.wait_ge(*var.prev(0, slot))
                    square_root(slot)
                else:
                    empty(e, slot, rooted)
            for slot in range(7):
                if slot in chunks:
                    e.wait_ge(*normed.prev(0, slot))
                    relu_to(slot, h0_part(slot))
                else:
                    empty(e, slot, relued)
            with e.Fori(0, NB) as i:
                def squares(slot):
                    k.wait("scalar", e, *conv.now(i, slot))
                    k.wait("scalar", e, *var.prev(i, slot))
                    square(slot)

                def roots(slot):
                    k.wait("scalar", e, *var.now(i, slot))
                    k.wait("scalar", e, *inverted.prev(i, slot))
                    square_root(slot)

                def relu(slot):
                    k.wait("scalar", e, *normed.now(i, slot))
                    if slot in (2, 4):
                        k.wait("scalar", e, *conv.prev(i, slot + 2))
                    elif slot in chunks:
                        k.wait("scalar", e, *conv.now(i, 2))
                    relu_to(slot, h1[:, 1:1 + LEN1] if slot == 2 else h2[:, 1:1 + LEN2] if slot == 4 else
                            feats[:, bass.ds(i * LEN3, LEN3)] if slot == 6 else h0_part(slot))
                squares(0)
                squares(1)
                roots(0)
                roots(1)
                squares(2)
                squares(3)
                roots(2)
                relu(0)
                relu(1)
                roots(3)
                relu(2)
                squares(4)
                squares(5)
                roots(4)
                roots(5)
                relu(3)
                relu(4)
                squares(6)
                roots(6)
                relu(5)
                relu(6)

        @block.gpsimd
        def _(e):
            def reflect(h, ends):
                for to, at in ends:
                    e.tensor_copy(h[:, to:to + 1], h[:, at:at + 1]).then_inc(*padded.up())

            ends0 = ((0, 4), (1, 3), (LEN0 + 2, LEN0), (LEN0 + 3, LEN0 - 1))
            e.sem_inc(padded.sem, 4)
            e.wait_ge(*relued.prev(0, 5))
            reflect(h0, ends0)
            with e.Fori(0, NB) as i:
                k.wait("gpsimd", e, *relued.now(i, 2))
                reflect(h1, ((0, 2), (LEN1 + 1, LEN1 - 1)))
                k.wait("gpsimd", e, *relued.now(i, 4))
                reflect(h2, ((0, 2), (LEN2 + 1, LEN2 - 1)))
                k.wait("gpsimd", e, *relued.now(i, 5))
                reflect(h0, ends0)

        @block.vector
        def _(e):
            v = nc.vector
            v.memset(avg[:, :], 1.0 / (C - 1)).then_inc(*setup.up())
            v.memset(epsc[:, :], EPS).then_inc(*setup.up())
            v.tensor_scalar(cent[:, :], k.ident[:, :], -1.0 / C, None, ALU.add).then_inc(*setup.up())
            e.wait_ge(*setup.done())
            e.wait_ge(loaded, 16 * 7)
            v.tensor_reduce(s0[:, :], w0[:, :], axis=AX.X, op=ALU.add).then_inc(ready, 1)
            for t, n, o in ((w1, 8, 0), (w2, 4, 8), (w3, 4, 12)):
                v.tensor_reduce(ssum[:, o:o + n], t[:, :, :], axis=AX.X, op=ALU.add).then_inc(*setup.up())
            e.wait_ge(*setup.done())
            e.wait_ge(ready, 1)
            v.tensor_scalar(s0[:, :], s0[:, :], -1.0 / C, None, ALU.mult).then_inc(*setup.up())
            v.tensor_scalar(ssum[:, :], ssum[:, :], -1.0 / C, None, ALU.mult).then_inc(*setup.up())
            e.wait_ge(*setup.done())
            v.tensor_scalar(w0[:, :], w0[:, :], s0[:, 0:1], None, ALU.add).then_inc(*setup.up())
            for t, n, o in ((w1, 8, 0), (w2, 4, 8), (w3, 4, 12)):
                v.tensor_tensor(t[:, :, :], t[:, :, :], spread(ssum[:, o:o + n], 2, C), ALU.add).then_inc(*setup.up())
            e.wait_ge(*setup.done())
            e.wait_ge(bias_mm, 1)
            v.tensor_copy(biasc[:, :], pz[:, 0:4]).then_inc(ready, 1)
            e.wait_ge(ready, 2)
            e.sem_inc(ready, 1)

            def invert(slot):
                v.reciprocal(inv[:, slot, 0:width[slot]], root[:, slot, 0:width[slot]]).then_inc(*inverted.up())

            def normalise(slot):
                v.scalar_tensor_tensor(normal[:, slot, 0:width[slot]], yb[slot], biasc[:, layer[slot]:layer[slot] + 1],
                                       inv[:, slot, 0:width[slot]], ALU.add, ALU.mult).then_inc(*normed.up())
            for slot in range(7):
                if slot in chunks:
                    e.wait_ge(*rooted.prev(0, slot))
                    invert(slot)
                    e.wait_ge(*inverted.prev(0, slot))
                    normalise(slot)
                else:
                    empty(e, slot, inverted, normed)
            with e.Fori(0, NB) as i:
                for slot in range(7):
                    k.wait("vector", e, *rooted.now(i, slot))
                    invert(slot)
                    k.wait("vector", e, *inverted.now(i, slot))
                    k.wait("vector", e, *relued.prev(i, slot))
                    normalise(slot)


def importance(k, feats, lrow):
    nc, ins = k.nc, k.ins
    with Stage(k, "imp") as st:
        sb = st.sb
        sig = st.sig
        w1, w2, w3 = sb("mw1", [C, DMLP]), sb("mw2", [C, 4, DMLP]), sb("mw3", [C, 4])
        b1, b2, b3 = sb("mb1", [C, 4]), sb("mb2", [C, 4]), sb("mb3", [1, 1])
        z1, z2 = sb("z1", [C, 4, 512]), sb("z2", [C, 4, 512])
        p1 = st.ps("p1", [C, 4, 512])
        p2 = st.ps("p2", [C, 4, 512])
        loaded = st.sem("mlp_weights_loaded")
        mm1, mm2, mm3 = sig("layer1_done", 4), sig("layer2_done", 4), sig("layer3_done", 1)
        g1, g2, row = sig("gelu1_done", 4), sig("gelu2_done", 4), sig("logits_kept", 1)
        block = st.block()

        @block.sync
        def _(e):
            for t, n in ((w1, "mlp_w1"), (w2, "mlp_w2"), (w3, "mlp_w3"), (b1, "mlp_b1"), (b2, "mlp_b2"), (b3, "mlp_b3")):
                e.dma_start(t[:], ins[n]).then_inc(loaded, 16)

        @block.tensor
        def _(e):
            for s in (mm1, mm2, mm3):
                s.seed(e)
            e.wait_ge(loaded, 96)
            with e.Fori(0, NB // 4) as i:
                for m in range(4):
                    if m == 0:
                        k.wait("tensor", e, *row.prev(i))
                    k.wait("tensor", e, *g1.prev(i, m))
                    nc.tensor.matmul(p1[:, m, :], w1[:, m * C:(m + 1) * C], feats[:, bass.ds(i * 512, 512)],
                                     start=True, stop=True).then_inc(*mm1.up())
                for m in range(4):
                    k.wait("tensor", e, *g2.prev(i, m))
                    for c in range(4):
                        if m == 0:
                            k.wait("tensor", e, *g1.now(i, c))
                        x = nc.tensor.matmul(p2[:, m, :], w2[:, c, m * C:(m + 1) * C], z1[:, c, :],
                                             start=c == 0, stop=c == 3)
                    x.then_inc(*mm2.up())
                for c in range(4):
                    k.wait("tensor", e, *g2.now(i, c))
                    x = nc.tensor.matmul(p1[0:1, 0, :], w3[:, c:c + 1], z2[:, c, :], start=c == 0, stop=c == 3)
                x.then_inc(*mm3.up())

        @block.scalar
        def _(e):
            for s in (g1, g2, row):
                s.seed(e)
            e.wait_ge(loaded, 96)
            with e.Fori(0, NB // 4) as i:
                for m in range(4):
                    k.wait("scalar", e, *mm1.now(i, m))
                    k.wait("scalar", e, *mm2.prev(i))
                    e.activation(z1[:, m, :], p1[:, m, :], ACT.Gelu, bias=b1[:, m:m + 1]).then_inc(*g1.up())
                for m in range(4):
                    k.wait("scalar", e, *mm2.now(i, m))
                    k.wait("scalar", e, *mm3.prev(i))
                    e.activation(z2[:, m, :], p2[:, m, :], ACT.Gelu, bias=b2[:, m:m + 1]).then_inc(*g2.up())
                k.wait("scalar", e, *mm3.now(i))
                e.activation(lrow[:, bass.ds(i * 512, 512)], p1[0:1, 0, :], ACT.Identity,
                             bias=b3[:, 0:1]).then_inc(*row.up())


def pool_frames(k, feats, lrow):
    nc, ins = k.nc, k.ins
    G, NG = 8, NB // 8
    with Stage(k, "pool") as st:
        sb = st.sb
        ps = st.ps
        sig = st.sig
        imp, cs = sb("imp", [NB, C]), sb("cs", [NB, C + 1])
        zero, tot = sb("zero", [NB, C]), sb("tot", [NB, 1])
        cst, csp = sb("cst", [C, NB]), sb("csp", [C, NB])
        step = sb("step", [C, D + 1])
        pa, pb = sb("pa", [C, G, D + 1]), sb("pb", [C, G, D + 1])
        da, db, wm = sb("da", [C, G, D]), sb("db", [C, G, D]), sb("wm", [C, G, D])
        avg = sb("avgp", [C, C])
        gamma, beta = sb("gammap", [C, 5]), sb("betap", [C, 5])
        fg, fm, ft = sb("fg", [C, G * C]), sb("fm", [C, G]), sb("ft", [C, G, C])
        sq, root, inv, normal = sb("sqp", [C, 512]), sb("rootp", [C, 512]), sb("invp", [C, 512]), sb("normp", [C, 512])
        epsc = sb("epscp", [C, 1])
        pt = ps("pt", [C, G, C])
        po, pv, pc = ps("po", [C, 512]), ps("pvp", [C, 512]), ps("pc", [C, 2, NB])
        scratch = nc.dram_tensor("logit_rows", (NB, C), F32, kind="Internal").ap()
        moved = st.sem("logits_moved")
        act0 = st.sem("sigmoid_done")
        tr0 = st.sem("sums_transposed")
        vec0 = st.sem("sums_done")
        iot = st.sem("steps_made")
        own = st.steps("vector_pool_steps")
        grp, ftd, mm, var = sig("group_copied", 1), sig("frames_transposed", 1), sig("pooled", 1), sig("pool_variance", 1)
        sqd, rtd, rel = sig("pool_squared", 1), sig("pool_rooted", 1), sig("pool_relu", 1)
        cen, wts, nrm = sig("frames_centred", 1), sig("weights_made", 1), sig("pool_normed", 1)
        block = st.block()

        @block.sync
        def _(e):
            e.dma_start(scratch.rearrange("b t -> (b t)").rearrange("(o n) -> o n", o=1), lrow[:, :]).then_inc(moved, 16)
            e.wait_ge(moved, 16)
            e.dma_start(imp[:, :], scratch).then_inc(moved, 16)
            e.dma_start(gamma[:, :], ins["norm_g"]).then_inc(moved, 16)
            e.dma_start(beta[:, :], ins["norm_b"]).then_inc(moved, 16)

        @block.gpsimd
        def _(e):
            e.iota(step[:, :], [[-1, D + 1]], base=0, channel_multiplier=0,
                   allow_small_or_imprecise_dtypes=True).then_inc(iot, 1)
            e.wait_ge(iot, 1)
            e.memset(step[:, D:D + 1], -BIG).then_inc(iot, 1)
            e.memset(avg[:, :], 1.0 / (C - 1)).then_inc(iot, 1)
            e.memset(epsc[:, :], EPS).then_inc(iot, 1)
            e.memset(zero[:, :], 0.0).then_inc(iot, 1)
            e.memset(cs[:, 0:1], 0.0).then_inc(iot, 1)

        @block.scalar
        def _(e):
            for s in (grp, sqd, rtd, rel):
                s.seed(e)
            e.wait_ge(moved, 64)
            e.wait_ge(iot, 6)
            e.activation(imp[:, :], imp[:, :], ACT.Sigmoid).then_inc(act0, 1)
            with e.Fori(0, NG) as i:
                k.wait("scalar", e, *ftd.prev(i))
                e.activation(fg[:, :], feats[:, bass.ds(i * G * C, G * C)], ACT.Copy).then_inc(*grp.up())
                k.wait("scalar", e, *mm.now(i))
                k.wait("scalar", e, *var.prev(i))
                e.activation(sq[:, :], po[:, :], ACT.Square).then_inc(*sqd.up())
                k.wait("scalar", e, *var.now(i))
                k.wait("scalar", e, *nrm.prev(i))
                e.activation(root[:, :], pv[:, :], ACT.Sqrt, bias=epsc[:, 0:1]).then_inc(*rtd.up())
                k.wait("scalar", e, *nrm.now(i))
                e.activation(k.resid[:, bass.ds(i * G * D, G * D)], normal[:, :], ACT.Relu,
                             bias=beta[:, 4:5], scale=gamma[:, 4:5]).then_inc(*rel.up())

        @block.tensor
        def _(e):
            for s in (ftd, mm, var):
                s.seed(e)
            e.wait_ge(vec0, 1)
            nc.tensor.transpose(pc[:, 0, :], cs[:, 1:C + 1], k.ident[0:NB, 0:NB]).then_inc(tr0, 1)
            nc.tensor.transpose(pc[:, 1, :], cs[:, 0:C], k.ident[0:NB, 0:NB]).then_inc(tr0, 1)
            with e.Fori(0, NG) as i:
                k.wait("tensor", e, *grp.now(i))
                k.wait("tensor", e, *cen.prev(i))
                for g in range(G):
                    m = nc.tensor.transpose(pt[:, g, :], fg[:, g * C:(g + 1) * C], k.ident[:, :])
                m.then_inc(*ftd.up())
                k.wait("tensor", e, *cen.now(i))
                k.wait("tensor", e, *wts.now(i))
                k.wait("tensor", e, *nrm.prev(i))
                for g in range(G):
                    m = nc.tensor.matmul(po[:, g * D:(g + 1) * D], ft[:, g, :], wm[:, g, :], start=True, stop=True)
                m.then_inc(*mm.up())
                k.wait("tensor", e, *sqd.now(i))
                k.wait("tensor", e, *rtd.prev(i))
                nc.tensor.matmul(pv[:, :], avg[:, :], sq[:, :], start=True, stop=True).then_inc(*var.up())

        @block.vector
        def _(e):
            v = nc.vector
            for s in (cen, wts, nrm):
                s.seed(e)
            e.wait_ge(act0, 1)
            v.tensor_scalar(imp[:, :], imp[:, :], 1e-5, None, ALU.add).then_inc(*own.up())
            e.wait_ge(*own.done())
            v.tensor_reduce(tot[:, :], imp[:, :], axis=AX.X, op=ALU.add).then_inc(*own.up())
            e.wait_ge(*own.done())
            v.reciprocal(tot[:, :], tot[:, :]).then_inc(*own.up())
            e.wait_ge(*own.done())
            v.tensor_scalar(imp[:, :], imp[:, :], tot[:, 0:1], float(D), ALU.mult, ALU.mult).then_inc(*own.up())
            e.wait_ge(*own.done())
            v.tensor_tensor_scan(cs[:, 1:C + 1], imp[:, :], zero[:, :], 0.0, ALU.add, ALU.add).then_inc(vec0, 1)
            e.wait_ge(tr0, 2)
            v.tensor_copy(cst[:, :], pc[:, 0, :]).then_inc(*own.up())
            v.tensor_copy(csp[:, :], pc[:, 1, :]).then_inc(*own.up())
            e.wait_ge(*own.done())
            base = own.n
            with e.Fori(0, NG) as i:
                own.n = base
                own.turn(i, PER_POOL)
                for p, s in ((pa, cst), (pb, csp)):
                    v.tensor_tensor(p[:, :, :], spread(step[:, :], 1, G),
                                    spread(s[:, bass.ds(i * G, G)], 2, D + 1), ALU.add).then_inc(*own.up())
                k.wait("vector", e, *own.done())
                for p in (pa, pb):
                    v.tensor_scalar(p[:, :, :], p[:, :, :], 0.0, None, ALU.max).then_inc(*own.up())
                k.wait("vector", e, *own.done())
                for p, d in ((pa, da), (pb, db)):
                    v.tensor_tensor(d[:, :, :], p[:, :, 0:D], p[:, :, 1:D + 1], ALU.subtract).then_inc(*own.up())
                k.wait("vector", e, *own.done())
                k.wait("vector", e, *mm.prev(i))
                v.tensor_tensor(wm[:, :, :], da[:, :, :], db[:, :, :], ALU.subtract).then_inc(*wts.up())
                k.wait("vector", e, *ftd.now(i))
                for g2 in range(2):
                    v.tensor_reduce(fm[:, 4 * g2:4 * g2 + 4], pt[:, 4 * g2:4 * g2 + 4, :], axis=AX.X, op=ALU.add).then_inc(*own.up())
                k.wait("vector", e, *own.done())
                v.tensor_scalar(fm[:, :], fm[:, :], 1.0 / C, None, ALU.mult).then_inc(*own.up())
                k.wait("vector", e, *own.done())
                v.tensor_tensor(ft[:, 0:4, :], pt[:, 0:4, :], spread(fm[:, 0:4], 2, C), ALU.subtract).then_inc(*own.up())
                v.tensor_tensor(ft[:, 4:8, :], pt[:, 4:8, :], spread(fm[:, 4:8], 2, C), ALU.subtract).then_inc(*cen.up())
                k.wait("vector", e, *rtd.now(i))
                v.reciprocal(inv[:, :], root[:, :]).then_inc(*own.up())
                k.wait("vector", e, *own.done())
                k.wait("vector", e, *rel.prev(i))
                v.tensor_tensor(normal[:, :], po[:, :], inv[:, :], ALU.mult).then_inc(*nrm.up())
                own.end()


PER_POOL = 11


def norm_transpose(k, name, xt, affine=None):
    G, NG = 8, NB // 8
    nc = k.nc
    with Stage(k, name) as st:
        mean, dev, sq = st.sb("mean", [C, G]), st.sb("dev", [C, G, D]), st.sb("sq", [C, G, D])
        ss, root, inv, xn = st.sb("ss", [C, G]), st.sb("root", [C, G]), st.sb("inv", [C, G]), st.sb("xn", [C, G, D])
        epsc = st.sb("epsc", [C, 1])
        gb = st.sb("gb", [D, 2])
        pt = st.ps("pt", [D, G, C])
        loaded = st.sem("affine_loaded")
        const = st.sem("norm_constants")
        own = st.steps("vector_norm_steps")
        devd, sqd, var = st.sig("deviations", 1), st.sig("squares", 1), st.sig("variances", 1)
        rtd, nrm, trd, kept = st.sig("roots", 1), st.sig("normed", 1), st.sig("transposed", 1), st.sig("kept", 1)
        block = st.block()

        @block.sync
        def _(e):
            if affine:
                e.dma_start(gb[:, :], k.ins[affine]).then_inc(loaded, 16)

        @block.vector
        def _(e):
            v = nc.vector
            for s in (devd, var, nrm):
                s.seed(e)
            v.memset(xt[D:D + 1, :], 1.0).then_inc(const, 1)
            v.memset(epsc[:, :], EPS).then_inc(const, 1)
            with e.Fori(0, NG) as i:
                own.n = 0
                own.turn(i, 3)
                x = k.resid[:, bass.ds(i * G * D, G * D)].rearrange("p (g d) -> p g d", g=G)
                v.tensor_reduce(mean[:, :], x, axis=AX.X, op=ALU.add).then_inc(*own.up())
                k.wait("vector", e, *own.done())
                v.tensor_scalar(mean[:, :], mean[:, :], 1.0 / D, None, ALU.mult).then_inc(*own.up())
                k.wait("vector", e, *own.done())
                v.tensor_tensor(dev[:, :, :], x, spread(mean[:, :], 2, D), ALU.subtract).then_inc(*devd.up())
                k.wait("vector", e, *sqd.now(i))
                v.tensor_reduce(ss[:, :], sq[:, :, :], axis=AX.X, op=ALU.add).then_inc(*var.up())
                k.wait("vector", e, *rtd.now(i))
                v.reciprocal(inv[:, :], root[:, :]).then_inc(*own.up())
                k.wait("vector", e, *own.done())
                k.wait("vector", e, *trd.prev(i))
                v.tensor_tensor(xn[:, :, :], dev[:, :, :], spread(inv[:, :], 2, D), ALU.mult).then_inc(*nrm.up())
                own.end()

        @block.scalar
        def _(e):
            for s in (sqd, rtd, kept):
                s.seed(e)
            e.wait_ge(const, 2)
            if affine:
                e.wait_ge(loaded, 16)
            with e.Fori(0, NG) as i:
                k.wait("scalar", e, *devd.now(i))
                e.activation(sq[:, :, :], dev[:, :, :], ACT.Square).then_inc(*sqd.up())
                k.wait("scalar", e, *var.now(i))
                e.activation(root[:, :], ss[:, :], ACT.Sqrt, bias=epsc[:, 0:1], scale=1.0 / D).then_inc(*rtd.up())
                k.wait("scalar", e, *trd.now(i))
                dst = xt[0:D, bass.ds(i * G * C, G * C)].rearrange("p (g c) -> p g c", g=G)
                if affine:
                    e.activation(dst, pt[:, :, :], ACT.Identity, bias=gb[:, 1:2], scale=gb[:, 0:1]).then_inc(*kept.up())
                else:
                    e.activation(dst, pt[:, :, :], ACT.Copy).then_inc(*kept.up())

        @block.tensor
        def _(e):
            trd.seed(e)
            with e.Fori(0, NG) as i:
                k.wait("tensor", e, *nrm.now(i))
                k.wait("tensor", e, *kept.prev(i))
                for g in range(G):
                    m = nc.tensor.transpose(pt[:, g, :], xn[:, g, :], k.ident[:, :])
                m.then_inc(*trd.up())


def odd_attention(k, xt):
    nc = k.nc
    DA = DH + 1
    with Stage(k, "oddattn") as st:
        wq, wk, wv = st.sb("wq", [D + 1, HEADS * DH]), st.sb("wk", [D + 1, HEADS * DH]), st.sb("wv", [D + 1, HEADS * DH])
        wo, bo, ones = st.sb("wo", [128, 2, D]), st.sb("bo", [1, D]), st.sb("ones", [1, C])
        mask = st.sb("mask", [C, C])
        xb = st.sb("xb", [D + 1, C])
        qz, kt, va = st.sb("qz", [128, 2, 4, C]), st.sb("kt", [128, 2, C]), st.sb("va", [C, HEADS, DA])
        s, mx, p, pt_ = st.sb("s", [C, HEADS, C]), st.sb("mx", [C, HEADS]), st.sb("p", [C, HEADS, C]), st.sb("pt_", [C, HEADS, C])
        rz, zn, zt = st.sb("rz", [C, HEADS]), st.sb("zn", [C, HEADS, DH]), st.sb("zt", [128, 2, C])
        pqk, pv, pS = st.ps("pqk", [128, 4, C]), st.ps("pv", [C, 512]), st.ps("pS", [C, HEADS, C])
        pT, pz, pzt = st.ps("pT", [C, HEADS, C]), st.ps("pz", [C, 512]), st.ps("pzt", [128, 512])
        loaded, const = st.sem("attn_weights_loaded"), st.sem("attn_constants")
        xc, qkv, qkk, vk = st.sig("x_copied", 1), st.sig("qkv_done", 1), st.sig("qk_kept", 5), st.sig("v_kept", 1)
        sc, masked, maxed = st.sig("scores_done", 1), st.sig("scores_masked", 1), st.sig("row_maxima", 1)
        sh, ex = st.sig("scores_shifted", 1), st.sig("exps_done", 1)
        tr, ta, tb, zd = (st.sig("probs_transposed", 1), st.sig("probs_kept_low", 1), st.sig("probs_kept_high", 1),
                          st.sig("mixed", 1))
        inverted, zn_s, ztd = st.sig("sums_inverted", 1), st.sig("mix_normed", 1), st.sig("mix_transposed", 1)
        ztk, od, rd = st.sig("mix_kept", 1), st.sig("out_done", 1), st.sig("resid_done", 1)
        block = st.block()

        @block.sync
        def _(e):
            for t, n in ((wq, "a_wq"), (wk, "a_wk"), (wv, "a_wv"), (wo, "a_wo"), (bo, "a_bo")):
                e.dma_start(t[:], k.ins[n]).then_inc(loaded, 16)

        @block.gpsimd
        def _(e):
            e.memset(mask[:, :], 0.0).then_inc(const, 1)
            e.memset(qz[:, :, :, :], 0.0).then_inc(const, 1)
            e.memset(va[:, :, :], 1.0).then_inc(const, 1)
            e.memset(ones[:, :], 1.0).then_inc(const, 1)
            e.wait_ge(const, 4)
            e.affine_select(out=mask[:, :], in_=mask[:, :], compare_op=ALU.is_ge, fill=-BIG, base=0,
                            pattern=[[-1, C]], channel_multiplier=1).then_inc(const, 1)
            e.wait_ge(const, 5)
            e.affine_select(out=mask[:, 0:C:2], in_=mask[:, 0:C:2], compare_op=ALU.is_equal, fill=-BIG, base=0,
                            pattern=[[-2, C // 2]], channel_multiplier=1).then_inc(const, 1)

        @block.vector
        def _(e):
            v = nc.vector
            for g in (tb, inverted, zn_s, rd):
                g.seed(e)
            e.wait_ge(const, 6)

            def copy_x(b):
                v.tensor_copy(xb[:, :], xt[0:D + 1, bass.ds(b * C, C)]).then_inc(*xc.up())

            def keep_v():
                v.tensor_copy(va[:, :, 0:DH], pv[:, 0:HEADS * DH].rearrange("p (h d) -> p h d", h=HEADS)).then_inc(*vk.up())

            def mask_scores():
                v.scalar_tensor_tensor(s[:, :, :], pS[:, :, :], float(DH) ** -0.5, spread(mask[:, :], 1, HEADS),
                                       ALU.mult, ALU.add).then_inc(*masked.up())

            def shift_scores(masked_now, maxed_now):
                k.wait("vector", e, *masked_now)
                v.tensor_reduce(mx[:, :], s[:, :, :], axis=AX.X, op=ALU.max).then_inc(*maxed.up())
                k.wait("vector", e, *maxed_now)
                v.tensor_tensor(s[:, :, :], s[:, :, :], spread(mx[:, :], 2, C), ALU.subtract).then_inc(*sh.up())

            def turn(i, more):
                if more:
                    k.wait("vector", e, *qkv.prev(i))
                    copy_x(i + 1)
                k.wait("vector", e, *tr.now(i))
                k.wait("vector", e, *zd.prev(i))
                v.tensor_copy(pt_[:, 4:8, :], pT[:, 4:8, :]).then_inc(*tb.up())
                if more:
                    k.wait("vector", e, *sc.now(i))
                    k.wait("vector", e, *ex.prev(i))
                    mask_scores()
                k.wait("vector", e, *zd.now(i))
                z = pz[:, 0:HEADS * DA].rearrange("p (h d) -> p h d", h=HEADS)
                v.reciprocal(rz[:, :], z[:, :, DH]).then_inc(*inverted.up())
                k.wait("vector", e, *inverted.now(i))
                k.wait("vector", e, *ztd.prev(i))
                v.tensor_tensor(zn[:, :, :], z[:, :, 0:DH], spread(rz[:, :], 2, DH), ALU.mult).then_inc(*zn_s.up())
                if more:
                    shift_scores(masked.now(i), maxed.now(i))
                    k.wait("vector", e, *qkv.now(i))
                    keep_v()
                k.wait("vector", e, *od.now(i))
                r = k.resid[:, bass.ds(i * D, D)]
                v.tensor_tensor(r, r, pzt[:, 256:256 + D], ALU.add).then_inc(*rd.up())
            copy_x(0)
            e.wait_ge(*qkv.prev(0))
            keep_v()
            e.wait_ge(*sc.prev(0))
            mask_scores()
            shift_scores(masked.prev(0), maxed.prev(0))
            with e.Fori(0, NB - 1) as i:
                turn(i, True)
            turn(NB - 1, False)

        @block.scalar
        def _(e):
            for g in (ta, ztk):
                g.seed(e)
            e.wait_ge(const, 6)

            def keep_qk():
                for j in range(4):
                    r = slice(32 * j, 32 * j + 32)
                    e.activation(qz[r, :, j, :], pqk[r, 0:2, :], ACT.Copy).then_inc(*qkk.up())
                e.activation(kt[:, :, :], pqk[:, 2:4, :], ACT.Copy).then_inc(*qkk.up())

            def exps():
                e.activation(p[:, :, :], s[:, :, :], ACT.Exp).then_inc(*ex.up())

            def turn(i, more):
                if more:
                    k.wait("scalar", e, *qkv.now(i))
                    k.wait("scalar", e, *sc.prev(i))
                    keep_qk()
                k.wait("scalar", e, *tr.now(i))
                k.wait("scalar", e, *zd.prev(i))
                e.activation(pt_[:, 0:4, :], pT[:, 0:4, :], ACT.Copy).then_inc(*ta.up())
                k.wait("scalar", e, *ztd.now(i))
                k.wait("scalar", e, *od.prev(i))
                e.activation(zt[:, :, :], pzt[:, 0:256].rearrange("p (a c) -> p a c", a=2), ACT.Copy).then_inc(*ztk.up())
                if more:
                    k.wait("scalar", e, *sh.now(i))
                    exps()
            e.wait_ge(*qkv.prev(0))
            keep_qk()
            e.wait_ge(*sh.prev(0))
            exps()
            with e.Fori(0, NB - 1) as i:
                turn(i, True)
            turn(NB - 1, False)

        @block.tensor
        def _(e):
            t = nc.tensor
            for g in (tr, zd, ztd, od):
                g.seed(e)
            e.wait_ge(loaded, 80)
            e.wait_ge(const, 6)

            def project():
                for n, w in ((0, wq), (2, wk)):
                    for g in range(2):
                        t.matmul(pqk[:, n + g, :], w[:, g * 128:(g + 1) * 128], xb[:, :], start=True, stop=True)
                t.matmul(pv[:, 0:256], xb[:, :], wv[:, :], start=True, stop=True).then_inc(*qkv.up())

            def scores():
                for h in range(HEADS):
                    m = t.matmul(pS[:, h, :], qz[:, h // 4, h % 4, :], kt[:, h // 4, :], start=True, stop=True)
                m.then_inc(*sc.up())

            def turn(i, more):
                if more:
                    k.wait("tensor", e, *xc.now(i))
                    k.wait("tensor", e, *qkk.prev(i))
                    k.wait("tensor", e, *vk.prev(i))
                    project()
                k.wait("tensor", e, *ex.prev(i))
                k.wait("tensor", e, *ta.prev(i))
                k.wait("tensor", e, *tb.prev(i))
                for h in range(HEADS):
                    m = t.transpose(pT[:, h, :], p[:, h, :], k.ident[:, :])
                m.then_inc(*tr.up())
                if more:
                    k.wait("tensor", e, *qkk.now(i))
                    k.wait("tensor", e, *masked.prev(i))
                    scores()
                k.wait("tensor", e, *ta.now(i))
                k.wait("tensor", e, *tb.now(i))
                k.wait("tensor", e, *vk.prev(i))
                k.wait("tensor", e, *zn_s.prev(i))
                for h in range(HEADS):
                    m = t.matmul(pz[:, h * DA:(h + 1) * DA], pt_[:, h, :], va[:, h, :], start=True, stop=True)
                m.then_inc(*zd.up())
                k.wait("tensor", e, *zn_s.now(i))
                k.wait("tensor", e, *rd.prev(i))
                zf = zn[:, :, :].rearrange("p h d -> p (h d)")
                for g in range(2):
                    m = t.transpose(pzt[:, g * C:(g + 1) * C], zf[:, g * 128:(g + 1) * 128], k.ident[:, :])
                m.then_inc(*ztd.up())
                k.wait("tensor", e, *ztk.now(i))
                for g in range(2):
                    t.matmul(pzt[:, 256:256 + D], zt[:, g, :], wo[:, g, :], start=g == 0, stop=False)
                t.matmul(pzt[:, 256:256 + D], ones[:, :], bo[:, :], start=False, stop=True).then_inc(*od.up())
            e.wait_ge(*xc.prev(0))
            project()
            e.wait_ge(*qkk.prev(0))
            scores()
            with e.Fori(0, NB - 1) as i:
                turn(i, True)
            turn(NB - 1, False)




RUNS = ((0, 1, 16), (1, 1, 8), (2, 1, 5), (3, 1, 4), (4, 1, 3), (5, 3, 2), (8, 8, 1))
NCAND = sum(n * m for _, n, m in RUNS)
RING = 8


def key_memory(k, xt):
    nc = k.nc
    DV = D + 1
    with Stage(k, "pkm") as st:
        wpk, keys = st.sb("wpk", [32, 16, D]), st.sb("keys", [32, 16, NKEY])
        wsim = st.sb("wsim", [D, 16, NKEY])
        wq, wo = st.sb("wq", [D, HEADS * D]), st.sb("wo", [128, 4, D])
        mask = st.sb("mask", [C, C])
        hoff, iot = st.sb("hoff", [C, HEADS, TOPK]), st.sb("iot", [C, NCAND])
        xb = st.sb("xb", [D, C])
        sim, rest = st.sb("sim", [C, 16, NKEY]), st.sb("rest", [C, 16, NKEY])
        val, idx = st.sb("val", [C, 16, TOPK]), st.sb("idx", [C, 16, TOPK], U32)
        idf = st.sb("idf", [C, 16, TOPK])
        cand, crest, cidx = st.sb("cand", [C, HEADS, NCAND]), st.sb("crest", [C, HEADS, NCAND]), st.sb("cidx", [C, HEADS, NCAND])
        best, pos, posf = st.sb("best", [C, HEADS, TOPK]), st.sb("pos", [C, HEADS, TOPK], U32), st.sb("posf", [C, HEADS, TOPK])
        hit = st.sb("hit", [C, 4, TOPK, NCAND])
        rowf, row = st.sb("rowf", [C, HEADS, TOPK]), st.sb("row", [C, HEADS * TOPK], U32)
        shifted, wnew, wcur = st.sb("shifted", [C, HEADS, TOPK]), st.sb("wnew", [C, HEADS, TOPK]), st.sb("wcur", [C, HEADS, TOPK])
        tot, rtot = st.sb("tot", [C, HEADS]), st.sb("rtot", [C, HEADS])
        ring = [[st.sb(f"ring{r}", [C, TOPK, 2 * D])] for r in range(RING)]
        ring = [r[0] for r in ring]
        kk, vv = st.sb("kk", [C, HEADS, D]), st.sb("vv", [C, HEADS, DV])
        qz, kt = st.sb("qz", [128, HEADS, C]), st.sb("kt", [128, 4, C])
        s, mx, p, pt_ = st.sb("s", [C, HEADS, C]), st.sb("mx", [C, HEADS]), st.sb("p", [C, HEADS, C]), st.sb("pt_", [C, HEADS, C])
        rz, zn, zt = st.sb("rz", [C, HEADS]), st.sb("zn", [C, HEADS, D]), st.sb("zt", [128, 4, C])
        pq, psim, pk = st.ps("pq", [128, 4, C]), st.ps("psim", [128, 16, NKEY]), st.ps("pk", [128, 4, C])
        pS, pT = st.ps("pS", [C, HEADS, C]), st.ps("pT", [C, HEADS, C])
        loaded, const, prep = st.sem("weights_loaded"), st.sem("constants"), st.sem("key_product")
        own = st.steps("vector_steps")
        xc, simd, simk = st.sig("x_copied", 1), st.sig("similarities_done", 1), st.sig("similarities_kept", 1)
        wsh, wex = st.sig("best_shifted", 1), st.sig("best_exps", 1)
        rows = st.sig("rows_chosen", 2)
        got = [st.sig(f"rows_gathered{r}", HEADS // RING, 256, seeded=False) for r in range(RING)]
        used = st.sig("rows_used", HEADS)
        qd, qk = st.sig("q_done", 1), st.sig("q_kept", 2)
        kd, kkept = st.sig("k_transposed", 1), st.sig("k_kept", 1)
        sc, sh, ex, tr = st.sig("scores_done", 1), st.sig("scores_shifted", 1), st.sig("exps_done", 1), st.sig("probs_transposed", 1)
        ta, tb, zd, zns = st.sig("probs_kept_low", 1), st.sig("probs_kept_high", 1), st.sig("mixed", 1), st.sig("mix_normed", 1)
        ztd, ztk, od, rd = st.sig("mix_transposed", 1), st.sig("mix_kept", 1), st.sig("out_done", 1), st.sig("resid_done", 1)
        block = st.block()

        @block.sync
        def _(e):
            for t, n in ((wpk, "k_wpk"), (keys, "k_keys"), (wq, "k_wq"), (wo, "k_wo")):
                e.dma_start(t[:], k.ins[n]).then_inc(loaded, 16)

        @block.gpsimd
        def _(e):
            e.memset(mask[:, :], 0.0).then_inc(const, 1)
            e.memset(qz[:, :, :], 0.0).then_inc(const, 1)
            e.memset(vv[:, :, :], 1.0).then_inc(const, 1)
            e.iota(hoff[:, :, :], [[NKV, HEADS], [0, TOPK]], base=0, channel_multiplier=0,
                   allow_small_or_imprecise_dtypes=True).then_inc(const, 1)
            e.iota(iot[:, :], [[1, NCAND]], base=0, channel_multiplier=0,
                   allow_small_or_imprecise_dtypes=True).then_inc(const, 1)
            e.wait_ge(const, 5)
            e.affine_select(out=mask[:, :], in_=mask[:, :], compare_op=ALU.is_ge, fill=-BIG, base=0,
                            pattern=[[-1, C]], channel_multiplier=1).then_inc(const, 1)
            with e.Fori(0, NB) as i:
                for h in range(HEADS):
                    if h % (HEADS // 2) == 0:
                        k.wait("gpsimd", e, *rows.now(i, h // (HEADS // 2)))
                    k.wait("gpsimd", e, *(used.now(i, h - RING) if h >= RING else used.prev(i, h + HEADS - RING)))
                    for j in range(TOPK):
                        e.indirect_dma_start(ring[h % RING][:, j, :], None, k.ins["k_table"],
                                             bass.IndirectOffsetOnAxis(ap=row[:, h * TOPK + j:h * TOPK + j + 1], axis=0)
                                             ).then_inc(got[h % RING].sem, 16)

        @block.vector
        def _(e):
            v = nc.vector
            for g in (xc, wsh, rows, used, kkept, sh, tb, zns, rd):
                g.seed(e)
            e.wait_ge(prep, 1)
            v.tensor_copy(wsim[:, :, :], psim[0:D, :, :]).then_inc(prep, 1)
            e.wait_ge(const, 6)

            def settle():
                k.wait("vector", e, *own.done())

            def top16(vals, spots, x, y, n, m):
                for a in range(n):
                    v.max(vals[:, a, 0:8], x[:, a, :]).then_inc(*own.up())
                settle()
                for a in range(n):
                    v.max_index(spots[:, a, 0:8], vals[:, a, 0:8], x[:, a, :]).then_inc(*own.up())
                    v.match_replace(y[:, a, :], vals[:, a, 0:8], x[:, a, :], -BIG).then_inc(*own.up())
                settle()
                for a in range(n):
                    v.max(vals[:, a, 8:16], y[:, a, :]).then_inc(*own.up())
                settle()
                for a in range(n):
                    v.max_index(spots[:, a, 8:16], vals[:, a, 8:16], y[:, a, :]).then_inc(*own.up())

            def search(i):
                k.wait("vector", e, *simd.prev(i))
                v.tensor_copy(xb[:, :], xt[0:D, bass.ds(i * C, C)]).then_inc(*xc.up())
                k.wait("vector", e, *simk.now(i))
                top16(val, idx, sim, rest, 16, NKEY)
                settle()
                v.tensor_copy(idf[:, :, :], idx[:, :, :]).then_inc(*own.up())
                settle()
                v.scalar_tensor_tensor(idf[:, HEADS:, :], idf[:, HEADS:, :], float(NKEY), hoff[:, :, :],
                                       ALU.mult, ALU.add).then_inc(*own.up())
                settle()
                o = 0
                for a, n, m in RUNS:
                    for to, at in ((cand, val), (cidx, idf)):
                        v.tensor_tensor(to[:, :, o:o + n * m].rearrange("p h (a b) -> p h a b", a=n),
                                        spread(at[:, 0:HEADS, a:a + n], 3, m),
                                        spread(at[:, HEADS:, 0:m], 2, n), ALU.add).then_inc(*own.up())
                    o += n * m
                settle()
                top16(best, pos, cand, crest, HEADS, NCAND)
                settle()
                k.wait("vector", e, *wex.prev(i))
                v.tensor_tensor(shifted[:, :, :], best[:, :, :], spread(best[:, :, 0], 2, TOPK), ALU.subtract).then_inc(*wsh.up())
                v.tensor_copy(posf[:, :, :], pos[:, :, :]).then_inc(*own.up())
                settle()
                for a in (0, 4):
                    v.tensor_tensor(hit[:, :, :, :], spread(posf[:, a:a + 4, :], 3, NCAND),
                                    spread(spread(iot[:, :], 1, TOPK), 1, 4), ALU.is_equal).then_inc(*own.up())
                    settle()
                    v.tensor_tensor(hit[:, :, :, :], hit[:, :, :, :], spread(cidx[:, a:a + 4, :], 2, TOPK), ALU.mult).then_inc(*own.up())
                    settle()
                    v.tensor_reduce(rowf[:, a:a + 4, :], hit[:, :, :, :], axis=AX.X, op=ALU.add).then_inc(*own.up())
                    settle()
                k.wait("vector", e, *wex.now(i))
                v.tensor_reduce(tot[:, :], wnew[:, :, :], axis=AX.X, op=ALU.add).then_inc(*own.up())
                settle()
                v.reciprocal(rtot[:, :], tot[:, :]).then_inc(*own.up())
                settle()
                v.tensor_tensor(wnew[:, :, :], wnew[:, :, :], spread(rtot[:, :], 2, TOPK), ALU.mult).then_inc(*own.up())
                settle()

            def choose(half):
                n = HEADS // 2
                v.tensor_copy(row[:, half * n * TOPK:(half + 1) * n * TOPK],
                              rowf[:, half * n:(half + 1) * n, :].rearrange("p h j -> p (h j)")).then_inc(*rows.up())

            def mix(i, h):
                r = ring[h % RING]
                k.wait("vector", e, *got[h % RING].now(i, h // RING))
                if h % (HEADS // 2) == HEADS // 2 - 1 and k.more:
                    choose(h // (HEADS // 2))
                v.tensor_tensor(r[:, :, :], r[:, :, :], spread(wcur[:, h, :], 2, 2 * D), ALU.mult).then_inc(*own.up())
                settle()
                if h == 0:
                    k.wait("vector", e, *kd.prev(i))
                    k.wait("vector", e, *zd.prev(i))
                v.tensor_reduce(kk[:, h, :], r[:, :, 0:D].rearrange("p j d -> p d j"), axis=AX.X, op=ALU.add).then_inc(*own.up())
                v.tensor_reduce(vv[:, h, 0:D], r[:, :, D:].rearrange("p j d -> p d j"), axis=AX.X, op=ALU.add).then_inc(*used.up())

            def attend(i):
                k.wait("vector", e, *kd.now(i))
                v.tensor_copy(kt[:, :, :], pk[:, :, :]).then_inc(*kkept.up())
                k.wait("vector", e, *sc.now(i))
                v.tensor_tensor(s[:, :, :], pS[:, :, :], spread(mask[:, :], 1, HEADS), ALU.add).then_inc(*own.up())
                settle()
                v.tensor_reduce(mx[:, :], s[:, :, :], axis=AX.X, op=ALU.max).then_inc(*own.up())
                settle()
                v.tensor_tensor(s[:, :, :], s[:, :, :], spread(mx[:, :], 2, C), ALU.subtract).then_inc(*sh.up())
                k.wait("vector", e, *tr.now(i))
                v.tensor_copy(pt_[:, 4:8, :], pT[:, 4:8, :]).then_inc(*tb.up())
                k.wait("vector", e, *zd.now(i))
                z = [pS[:, 4 * a:4 * a + 4, :].rearrange("p h c -> p (h c)")[:, 0:4 * DV].rearrange("p (h d) -> p h d", h=4)
                     for a in range(2)]
                for a in range(2):
                    v.reciprocal(rz[:, 4 * a:4 * a + 4], z[a][:, :, D]).then_inc(*own.up())
                settle()
                v.tensor_tensor(zn[:, 0:4, :], z[0][:, :, 0:D], spread(rz[:, 0:4], 2, D), ALU.mult).then_inc(*own.up())
                v.tensor_tensor(zn[:, 4:8, :], z[1][:, :, 0:D], spread(rz[:, 4:8], 2, D), ALU.mult).then_inc(*zns.up())
                k.wait("vector", e, *od.now(i))
                r = k.resid[:, bass.ds(i * D, D)]
                v.tensor_tensor(r, r, pk[:, 0, 0:D], ALU.add).then_inc(*rd.up())

            def turn(i, more):
                k.more = more
                if more:
                    search(i + 1)
                for h in range(HEADS):
                    mix(i, h)
                if more:
                    v.tensor_copy(wcur[:, :, :], wnew[:, :, :]).then_inc(*own.up())
                attend(i)

            search(0)
            choose(0)
            choose(1)
            v.tensor_copy(wcur[:, :, :], wnew[:, :, :]).then_inc(*own.up())
            own.turn(0, 0)
            first = own.n
            with e.Fori(0, NB - 1) as i:
                own.n = first
                own.turn(i, PER_PKM)
                turn(i, True)
                own.end()
            own.leave(NB - 1)
            turn(NB - 1, False)

        @block.scalar
        def _(e):
            for g in (simk, wex, qk, ex, ta, ztk):
                g.seed(e)
            e.wait_ge(const, 6)

            def search(i):
                k.wait("scalar", e, *simd.now(i))
                k.wait("scalar", e, *wsh.prev(i))
                e.activation(sim[:, :, :], psim[:, :, :], ACT.Copy).then_inc(*simk.up())
                k.wait("scalar", e, *wsh.now(i))
                e.activation(wnew[:, :, :], shifted[:, :, :], ACT.Exp).then_inc(*wex.up())

            def attend(i):
                k.wait("scalar", e, *qd.now(i))
                e.activation(qz[0:D, 0:HEADS:2, :], pq[0:D, :, :], ACT.Copy, scale=float(D) ** -0.5).then_inc(*qk.up())
                e.activation(qz[D:, 1:HEADS:2, :], pq[D:, :, :], ACT.Copy, scale=float(D) ** -0.5).then_inc(*qk.up())
                k.wait("scalar", e, *sh.now(i))
                k.wait("scalar", e, *tr.prev(i))
                e.activation(p[:, :, :], s[:, :, :], ACT.Exp).then_inc(*ex.up())
                k.wait("scalar", e, *tr.now(i))
                k.wait("scalar", e, *zd.prev(i))
                e.activation(pt_[:, 0:4, :], pT[:, 0:4, :], ACT.Copy).then_inc(*ta.up())
                k.wait("scalar", e, *ztd.now(i))
                e.activation(zt[:, :, :], pq[:, :, :], ACT.Copy).then_inc(*ztk.up())
            search(0)
            with e.Fori(0, NB - 1) as i:
                search(i + 1)
                attend(i)
            attend(NB - 1)

        @block.tensor
        def _(e):
            t = nc.tensor
            for g in (simd, qd, kd, sc, tr, zd, ztd, od):
                g.seed(e)
            e.wait_ge(loaded, 64)
            for n in range(16):
                m = t.matmul(psim[0:D, n, :], wpk[:, n, :], keys[:, n, :], start=True, stop=True)
            m.then_inc(prep, 1)
            e.wait_ge(prep, 2)
            e.wait_ge(const, 6)

            def search(i):
                k.wait("tensor", e, *xc.now(i))
                k.wait("tensor", e, *simk.prev(i))
                w = wsim[:, :, :].rearrange("p n k -> p (n k)")
                o = psim[:, :, :].rearrange("p n k -> p (n k)")
                for a in range(2):
                    m = t.matmul(o[:, a * 512:(a + 1) * 512], xb[:, :], w[:, a * 512:(a + 1) * 512], start=True, stop=True)
                m.then_inc(*simd.up())

            def attend(i):
                k.wait("tensor", e, *ztk.prev(i))
                for a in range(4):
                    m = t.matmul(pq[:, a, :], wq[:, a * 128:(a + 1) * 128], xt[0:D, bass.ds(i * C, C)], start=True, stop=True)
                m.then_inc(*qd.up())
                k.wait("tensor", e, *used.now(i))
                k.wait("tensor", e, *rd.prev(i))
                kf = kk[:, :, :].rearrange("p h d -> p (h d)")
                for a in range(4):
                    m = t.transpose(pk[:, a, :], kf[:, a * 128:(a + 1) * 128], k.ident[:, :])
                m.then_inc(*kd.up())
                k.wait("tensor", e, *kkept.now(i))
                k.wait("tensor", e, *qk.now(i))
                for h in range(HEADS):
                    m = t.matmul(pS[:, h, :], qz[:, h, :], kt[:, h // 2, :], start=True, stop=True)
                m.then_inc(*sc.up())
                k.wait("tensor", e, *ex.now(i))
                for h in range(HEADS):
                    m = t.transpose(pT[:, h, :], p[:, h, :], k.ident[:, :])
                m.then_inc(*tr.up())
                k.wait("tensor", e, *ta.now(i))
                k.wait("tensor", e, *tb.now(i))
                for h in range(HEADS):
                    o = pS[:, 4 * (h // 4):4 * (h // 4) + 4, :].rearrange("p h c -> p (h c)")
                    m = t.matmul(o[:, (h % 4) * DV:(h % 4 + 1) * DV], pt_[:, h, :], vv[:, h, :], start=True, stop=True)
                m.then_inc(*zd.up())
                k.wait("tensor", e, *zns.now(i))
                zf = zn[:, :, :].rearrange("p h d -> p (h d)")
                for a in range(4):
                    m = t.transpose(pq[:, a, :], zf[:, a * 128:(a + 1) * 128], k.ident[:, :])
                m.then_inc(*ztd.up())
                k.wait("tensor", e, *ztk.now(i))
                for a in range(4):
                    m = t.matmul(pk[:, 0, 0:D], zt[:, a, :], wo[:, a, :], start=a == 0, stop=a == 3)
                m.then_inc(*od.up())
            search(0)
            with e.Fori(0, NB - 1) as i:
                search(i + 1)
                attend(i)
            attend(NB - 1)


PER_PKM = 168


SC = 16
LR = 0.1
GATES = 3


def gated_features(k, xt, fp, gates):
    nc = k.nc
    W = 3 * D + GATES
    with Stage(k, "gated") as st:
        wf, xb = st.sb("wf", [D, W]), st.sb("xb", [D, 2 * C])
        pf = st.ps("pf", [C, 2, W])
        sq, n2 = st.sb("sq", [C, NB, D]), st.sb("n2", [C, 2, NB])
        loaded = st.sem("weights_loaded")
        own, aown = st.steps("vector_steps"), st.steps("scalar_steps")
        xc, fd, fk = st.sig("x_copied", 1), st.sig("features_done", 1), st.sig("features_kept", 1)
        block = st.block()

        @block.sync
        def _(e):
            e.dma_start(wf[:, :], k.ins["t_wf"]).then_inc(loaded, 16)

        @block.tensor
        def _(e):
            fd.seed(e)
            e.wait_ge(loaded, 16)
            with e.Fori(0, NB // 2) as i:
                k.wait("tensor", e, *xc.now(i))
                k.wait("tensor", e, *fk.prev(i))
                for g in range(2):
                    m = nc.tensor.matmul(pf[:, g, :], xb[:, g * C:(g + 1) * C], wf[:, :], start=True, stop=True)
                m.then_inc(*fd.up())

        @block.scalar
        def _(e):
            fk.seed(e)
            with e.Fori(0, NB // 2) as i:
                k.wait("scalar", e, *fd.now(i))
                e.activation(fp[:, bass.ds(2 * i, 2), :], pf[:, :, :], ACT.Copy).then_inc(*fk.up())
            e.wait_ge(*fk.now(NB // 2 - 1))
            e.activation(fp[:, :, 0:3 * D], fp[:, :, 0:3 * D], ACT.Silu).then_inc(*aown.up())
            e.activation(gates[:, :, :], fp[:, :, 3 * D:], ACT.Sigmoid).then_inc(*aown.up())
            e.wait_ge(own.sem, NORM_AT)
            e.activation(n2[:, :, :], n2[:, :, :], ACT.Sqrt).then_inc(*aown.up())

        @block.vector
        def _(e):
            v = nc.vector
            xc.seed(e)
            with e.Fori(0, NB // 2) as i:
                k.wait("vector", e, *fd.prev(i))
                v.tensor_copy(xb[:, :], xt[0:D, bass.ds(i * 2 * C, 2 * C)]).then_inc(*xc.up())
            e.wait_ge(aown.sem, 2)
            for a in range(2):
                x = fp[:, :, a * D:(a + 1) * D]
                v.tensor_tensor(sq[:, :, :], x, x, ALU.mult).then_inc(*own.up())
                e.wait_ge(*own.done())
                v.tensor_reduce(n2[:, a, :], sq[:, :, :], axis=AX.X, op=ALU.add).then_inc(*own.up())
                e.wait_ge(*own.done())
            assert own.n == NORM_AT
            v.tensor_scalar(gates[:, :, 1], gates[:, :, 1], LR, None, ALU.mult).then_inc(*own.up())
            e.wait_ge(aown.sem, 3)
            v.tensor_scalar(n2[:, :, :], n2[:, :, :], 1e-12, None, ALU.max).then_inc(*own.up())
            e.wait_ge(*own.done())
            v.reciprocal(n2[:, :, :], n2[:, :, :]).then_inc(*own.up())
            e.wait_ge(*own.done())
            for a in range(2):
                x = fp[:, :, a * D:(a + 1) * D]
                v.tensor_tensor(x, x, spread(n2[:, a, :], 2, D), ALU.mult).then_inc(*own.up())
            e.wait_ge(*own.done())


NORM_AT = 4


def load_sum(k, e, v, a, b, loaded, own):
    e.wait_ge(*loaded)
    v.tensor_tensor(a, a, b, ALU.add).then_inc(*own.up())
    e.wait_ge(*own.done())


def scan_weights(k, fp, gates, dram, ccol):
    nc = k.nc
    with Stage(k, "weights") as st:
        a0, a1 = st.sb("a0", [D, HID]), st.sb("a1", [D, HID])
        ones, zero, one = st.sb("ones", [C, C]), st.sb("zero", [C, C]), st.sb("one", [1, 1])
        qk, gt = st.sb("qk", [C, 2, D]), st.sb("gt", [C, GATES])
        qkt = st.sb("qkt", [D, 2, C])
        diag, own_g = st.sb("diag", [C, 2, C]), st.sb("own_g", [C, C])
        m2, oma, u, cr = st.sb("m2", [C, C]), st.sb("oma", [C, C]), st.sb("u", [C, C + 1]), st.sb("cr", [C, C + 1])
        cc, uq, w1, wr = st.sb("cc", [C, 2]), st.sb("uq", [C, C]), st.sb("w1", [C, C]), st.sb("wr", [C, 2, C])
        kq = st.sb("kq", [C, 2, HID])
        pt, pb, pg = st.ps("pt", [D, 2, C]), st.ps("pb", [C, 2, C]), st.ps("pg", [C, 2, C])
        pa, pc, pw = st.ps("pa", [C, 2, HID]), st.ps("pc", [C, 2]), st.ps("pw", [C, 2, C])
        loaded, const = st.sem("weights_loaded"), st.sem("constants")
        own = st.steps("vector_steps")
        xc, trd, trk, dg = st.sig("qk_copied", 1), st.sig("qk_transposed", 1), st.sig("qk_kept", 1), st.sig("diagonals", 1)
        bd, sd, gd, wd = st.sig("rows_spread", 1), st.sig("scanned", 1), st.sig("grams_done", 1), st.sig("weighted", 4)
        cd, cck, wtd, wtk = st.sig("c_turned", 1), st.sig("c_kept", 2), st.sig("weights_turned", 1), st.sig("weights_kept", 1)
        kak, stored = st.sig("first_terms_kept", 2), st.sig("stored", 7, 16)
        vdone = st.sem("v_stored")
        block = st.block()

        @block.sync
        def _(e):
            e.dma_start(a0[:, :], k.ins["t_w0"]).then_inc(loaded, 16)
            e.dma_start(a1[:, :], k.ins["t_p0"]).then_inc(loaded, 16)
            e.dma_start(dram["v"].rearrange("b t d -> t b d"), fp[:, :, 2 * D:3 * D]).then_inc(vdone, 16)
            stored.seed(e)
            with e.Fori(0, NB) as i:
                def row(t):
                    return t[bass.ds(i, 1)]
                k.wait("sync", e, *kak.now(i))
                e.dma_start(row(dram["ka"]).rearrange("o t h -> (o t) h"), kq[:, 0, :]).then_inc(*stored.up())
                e.dma_start(row(dram["qa"]).rearrange("o t h -> (o t) h"), kq[:, 1, :]).then_inc(*stored.up())
                k.wait("sync", e, *wtk.now(i))
                e.dma_start(row(dram["w"]).rearrange("o t h -> (o t) h"), wr[:, :, :].rearrange("p a s -> p (a s)")).then_inc(*stored.up())
                e.dma_start(row(dram["uq"])[:, :, 0, :].rearrange("o s t -> (o s) t"), uq[:, :]).then_inc(*stored.up())
                e.dma_start(row(dram["uq"])[:, :, 1, :].rearrange("o s t -> (o s) t"), u[:, 1:C + 1]).then_inc(*stored.up())
                e.dma_start(row(dram["c"]), cr[0:1, :]).then_inc(*stored.up())
                e.dma_start(row(dram["w1t"]).rearrange("o s t -> (o s) t"), w1[:, :]).then_inc(*stored.up())
            e.wait_ge(*stored.now(NB - 1))
            e.wait_ge(vdone, 16)

        @block.gpsimd
        def _(e):
            e.memset(ones[:, :], 1.0).then_inc(const, 1)
            e.memset(zero[:, :], 0.0).then_inc(const, 1)
            e.memset(one[:, :], 1.0).then_inc(const, 1)
            e.memset(u[:, 0:1], 0.0).then_inc(const, 1)
            e.memset(cr[:, 0:1], 1.0).then_inc(const, 1)

        @block.vector
        def _(e):
            v = nc.vector
            for s in (xc, dg, sd, wd, cck):
                s.seed(e)
            load_sum(k, e, v, a0[:, :], a1[:, :], (loaded, 32), own)
            e.sem_inc(const, 1)
            e.wait_ge(const, 6)
            first = own.n
            with e.Fori(0, NB) as i:
                own.n = first
                own.turn(i, 4)
                k.wait("vector", e, *bd.prev(i))
                v.tensor_copy(gt[:, :], gates[:, bass.ds(i, 1), :].rearrange("p o g -> p (o g)")).then_inc(*own.up())
                v.tensor_copy(qk[:, :, :], fp[:, bass.ds(i, 1), 0:2 * D].rearrange("p o (a d) -> p (o a) d", a=2)).then_inc(*xc.up())
                k.wait("vector", e, *own.done())
                v.tensor_scalar(own_g[:, :], k.ident[:, :], gt[:, 1:2], -2.0, ALU.mult, ALU.mult).then_inc(*own.up())
                v.tensor_scalar(diag[:, 0, :], k.ident[:, :], gt[:, 2:3], None, ALU.mult).then_inc(*own.up())
                v.tensor_scalar(diag[:, 1, :], k.ident[:, :], gt[:, 0:1], None, ALU.mult).then_inc(*dg.up())
                k.wait("vector", e, *own.done())
                k.wait("vector", e, *bd.now(i))
                v.tensor_scalar(oma[:, :], pb[:, 1, :], -1.0, 1.0, ALU.mult, ALU.add).then_inc(*own.up())
                v.tensor_tensor_scan(m2[:, :], pb[:, 0, :], own_g[:, :], 0.0, ALU.mult, ALU.add).then_inc(*sd.up())
                k.wait("vector", e, *own.done())
                k.wait("vector", e, *sd.now(i))
                k.wait("vector", e, *stored.prev(i))
                v.tensor_tensor_scan(u[:, 1:C + 1], oma[:, :], m2[:, :], 0.0, ALU.mult, ALU.add).then_inc(*wd.up())
                v.tensor_tensor_scan(cr[:, 1:C + 1], oma[:, :], zero[:, :], 1.0, ALU.mult, ALU.add).then_inc(*wd.up())
                k.wait("vector", e, *wd.now(i, 1))
                k.wait("vector", e, *gd.now(i))
                v.tensor_tensor(uq[:, :], pg[:, 0, :], u[:, 1:C + 1], ALU.mult).then_inc(*wd.up())
                v.tensor_tensor(w1[:, :], pg[:, 1, :], u[:, 0:C], ALU.mult).then_inc(*wd.up())
                k.wait("vector", e, *cd.now(i))
                k.wait("vector", e, *kak.prev(i))
                v.tensor_copy(cc[:, :], pc[:, :]).then_inc(*cck.up())
                v.tensor_copy(ccol[:, bass.ds(i, 1)], pc[:, 1:2]).then_inc(*cck.up())
                own.end()
            e.wait_ge(*cck.now(NB - 1))

        @block.scalar
        def _(e):
            for s in (trk, wtk, kak):
                s.seed(e)
            with e.Fori(0, NB) as i:
                k.wait("scalar", e, *trd.now(i))
                k.wait("scalar", e, *gd.prev(i))
                e.activation(qkt[:, :, :], pt[:, :, :], ACT.Copy).then_inc(*trk.up())
                k.wait("scalar", e, *cck.now(i))
                k.wait("scalar", e, *stored.prev(i))
                for a in range(2):
                    e.activation(kq[:, a, :], pa[:, a, :], ACT.Copy, scale=cc[:, a:a + 1]).then_inc(*kak.up())
                k.wait("scalar", e, *wtd.now(i))
                e.activation(wr[:, :, :], pw[:, :, :], ACT.Copy).then_inc(*wtk.up())

        @block.tensor
        def _(e):
            t = nc.tensor
            for s in (trd, bd, gd, cd, wtd):
                s.seed(e)
            e.wait_ge(const, 6)
            with e.Fori(0, NB) as i:
                k.wait("tensor", e, *xc.now(i))
                k.wait("tensor", e, *trk.prev(i))
                for a in range(2):
                    m = t.transpose(pt[:, a, :], qk[:, a, :], k.ident[:, :])
                m.then_inc(*trd.up())
                k.wait("tensor", e, *dg.now(i))
                k.wait("tensor", e, *sd.prev(i))
                t.matmul(pb[:, :, :], ones[:, :], diag[:, :, :], start=True, stop=True).then_inc(*bd.up())
                k.wait("tensor", e, *trk.now(i))
                k.wait("tensor", e, *wd.prev(i))
                k.wait("tensor", e, *kak.prev(i))
                t.matmul(pa[:, 0, :], qkt[:, 1, :], a0[:, :], start=True, stop=True)
                t.matmul(pa[:, 1, :], qkt[:, 0, :], a0[:, :], start=True, stop=True)
                t.matmul(pg[:, :, :], qkt[:, 1, :], qkt[:, :, :], start=True, stop=True).then_inc(*gd.up())
                k.wait("tensor", e, *wd.now(i, 1))
                k.wait("tensor", e, *cck.prev(i))
                t.matmul(pc[:, 0:1], cr[0:1, 0:C], one[:, :], start=True, stop=True)
                t.matmul(pc[:, 1:2], cr[0:1, 1:C + 1], one[:, :], start=True, stop=True).then_inc(*cd.up())
                k.wait("tensor", e, *wd.now(i))
                k.wait("tensor", e, *wtk.prev(i))
                t.transpose(pw[:, 0, :], w1[:, :], k.ident[:, :])
                t.transpose(pw[:, 1, :], u[:, 0:C], k.ident[:, :]).then_inc(*wtd.up())


COST = {"v": 2.2, "g": 4.4, "s": 4.2, "sum_v": 2.2, "sum_t": 3.5, "sum_s": 5.5}


def share_dots(blocks):
    best = None
    for made in range(1, blocks + 1):
        for sums in range(0, made):
            t = max(COST["v"] * made + COST["sum_v"] * (blocks - sums), COST["g"] * (blocks - made) + COST["sum_v"],
                    COST["v"] + COST["sum_s"] * sums)
            if best is None or t < best[0]:
                best = t, made, sums
    return best[1:]


def share_mix(blocks):
    best = None
    for s in range(0, blocks):
        for g in range(0, blocks - s):
            v = blocks - s - g
            if v < 1:
                continue
            made = sorted([(COST["v"] * (n + 1), "v") for n in range(v)] + [(COST["s"] * (n + 1), "s") for n in range(s)]
                          + [(COST["g"] * (n + 1), "g") for n in range(g)])
            tv, tt, plan = COST["v"] * v, 0.0, []
            for ready, who in made:
                a, b = max(tv, ready) + COST["sum_v"], max(tt, ready) + COST["sum_t"]
                if b <= a:
                    tt = b
                    plan.append((who, "t"))
                else:
                    tv = a
                    plan.append((who, "v"))
            if best is None or max(tv, tt) < best[0]:
                best = max(tv, tt), plan
    return best[1]


class ChunkSignal:

    def __init__(self, st, name, per):
        self.sem = st.sem(name)
        self.base, total = [], 0
        for c in range(C // SC):
            self.base.append(total)
            total += SC * per(c)
        self.per = per

    def up(self):
        return self.sem, 1

    def now(self, c, it, j):
        assert 0 <= j < self.per(c), (c, j)
        return self.sem, it * self.per(c) + (self.base[c] + j + 1)


def scan(k, dram):
    nc = k.nc
    HH, DD, NC = HID // 2, D // 2, C // SC
    BG = 16
    DOTS = [share_dots(c + 1) for c in range(NC)]
    MIX = [share_mix(c + 1) for c in range(NC)]
    THIN = [SC * (c + 1) - SC * ((c + 1) // 3) for c in range(NC)]
    made_by = lambda c, who: [b for b, (w, _) in enumerate(MIX[c]) if w == who]
    summed_by = lambda c, who: [b for b, (_, w) in enumerate(MIX[c]) if w == who]
    with Stage(k, "scan") as st:
        hh, ee = st.sb("hh", [128, C, HH]), st.sb("ee", [128, C, DD])
        gc = st.sb("gc", [128, SC, HH])
        wc, ka, vc = st.sb("wc", [128, SC, 2, C]), st.sb("ka", [128, SC, HH]), st.sb("vc", [128, SC, DD])
        cp = st.sb("cp", [128, C + 1])
        prod = st.sb("prod", [128, NC, SC * HH])
        part = st.sb("part", [128, NC, HH])
        acc, pre, sg, h, ds = [st.sb(n, [128, HH]) for n in ("acc", "pre", "sg", "h", "ds")]
        gr, w = st.sb("gr", [128, C]), st.sb("w", [128, C])
        er, eacc = st.sb("er", [128, DD]), st.sb("eacc", [128, DD])
        ht, et = st.sb("ht", [128, 128]), st.sb("et", [DD, 128])
        b0, c0 = st.sb("b0", [128, 2, D]), st.sb("c0", [DD, 2, HID])
        flat = prod[:, :, :].rearrange("p b n -> p (b n)")
        b1 = flat[:, 0:2 * D].rearrange("p (a d) -> p a d", a=2)
        c1 = flat[0:DD, 2 * D:2 * D + 2 * HID].rearrange("p (a h) -> p a h", a=2)
        old = [flat[:, a * 4096:(a + 1) * 4096].rearrange("p (b h) -> p b h", b=BG) for a in range(2)]
        oldw = [flat[:, 8192 + a * 256:8192 + (a + 1) * 256].rearrange("p (b t) -> p b t", b=BG) for a in range(2)]
        said = [flat[0:SC, 10240 + 2048 * a:10240 + 2048 * (a + 1)].rearrange("p (b h) -> p b h", b=8) for a in range(2)]
        olds = flat[:, 14336:14336 + SC * HH].rearrange("p (t h) -> p t h", t=SC)
        pair = st.sb("pair", [128, 128])
        pht, ppb = st.ps("pht", [128, 128]), st.ps("ppb", [128, DD])
        pgr, pmx = st.ps("pgr", [128, 2, C]), st.ps("pmx", [128, 512])
        pet, pdb = st.ps("pet", [DD, 128]), st.ps("pdb", [128, HH])
        pold = st.ps("pold", [SC, 2, 2, HID])
        loaded, cleared, const = st.sem("weights_loaded"), st.sem("cleared"), st.sem("constants")
        chunk, over, kept = st.sem("chunk_loaded"), st.sem("chunk_over"), st.sem("histories_stored")
        gstored = st.sem("gradients_stored")
        oldl, oldd = [st.sem(f"older_loaded{a}") for a in range(2)], st.sem("older_products")
        olde, olds_ld = st.sem("older_kept"), st.sem("older_reloaded")
        olds_st = [st.sem(f"older_stored{a}") for a in range(2)]
        own = st.steps("vector_steps")
        pr, sgd, hd = st.sig("pre_done", 1), st.sig("sigmoid_done", 1), st.sig("hidden_done", 1)
        htd, htk, pbd = st.sig("hidden_turned", 1), st.sig("hidden_kept", 1), st.sig("first_prediction_done", 1)
        grd, prd = st.sig("gram_halves", 2), st.sig("gram_sums", 2)
        wd = st.sig("coefficients_done", 2)
        ed, etd, etk, dbd = st.sig("error_done", 1), st.sig("error_turned", 1), st.sig("error_kept", 1), st.sig("first_backward_done", 1)
        gdone = st.sig("gradient_done", 1)
        mxd = st.sig("rows_summed", 1)
        adots = st.sig("scalar_dots_done", 1)
        vdot = ChunkSignal(st, "vector_dot_products", lambda c: max(DOTS[c][1], 1))
        vmix = ChunkSignal(st, "vector_mix_products", lambda c: len(made_by(c, "v")))
        smix = ChunkSignal(st, "scalar_mix_products", lambda c: max(len(made_by(c, "s")), 1))
        gdot = ChunkSignal(st, "gpsimd_dot_products", lambda c: max(c + 1 - DOTS[c][0], 1))
        gmix = ChunkSignal(st, "gpsimd_mix_products", lambda c: max(len(made_by(c, "g")), 1))
        gthin = ChunkSignal(st, "gpsimd_thin_products", lambda c: 2)
        block = st.block()
        blk = lambda b: prod[:, b, :].rearrange("p (s w) -> p s w", s=SC)
        hist = lambda b: hh[:, b * SC:(b + 1) * SC, :]
        coef = lambda b: spread(w[:, b * SC:(b + 1) * SC], 2, HH)
        thin = lambda a, b: flat[:, a * DD:b * DD].rearrange("p (s w) -> p s w", s=b - a)
        one = lambda t, j: t[:, bass.ds(j, 1), :].rearrange("p o w -> p (o w)")

        def own_steps(c):
            made, sums = DOTS[c]
            mine, rest = len(summed_by(c, "v")), bool(summed_by(c, "t"))
            return 13 + made - sums + c - sums + mine + rest + (mine + rest > 1)

        def store_old(e, c, q):
            for a in range(2):
                g = ((c - 1) * (NB // BG) + q) * 2 + a
                e.wait_ge(olde, 4 * (g + 1))
                b = q * BG + 8 * a
                e.dma_start(dram["po"][b:b + 8, :, :].rearrange("b t h -> t b h"), said[a][:, :, :]).then_inc(olds_st[a], 16)

        def gap(e, c, *missing):
            for s, n in missing:
                if n:
                    e.sem_inc(s.sem, n * SC)

        def older(e, c):
            for q in range(NB // BG):
                for j in range(8):
                    g = ((c - 1) * (NB // BG) + q) * 8 + j
                    e.wait_ge(oldd, g + 1)
                    if g >= 8 and j % 4 == 0:
                        e.wait_ge(olds_st[j // 4], 16 * (g // 8))
                    e.activation(said[j // 4][:, 2 * (j % 4):2 * (j % 4) + 2, :], pold[:, g % 2, :, :], ACT.Copy).then_inc(olde, 1)

        @block.sync
        def _(e):
            for t, n in ((b0, "t_w1"), (b1, "t_p1"), (c0, "t_w1t"), (c1, "t_p1t")):
                e.dma_start(t[:, :, :], k.ins[n]).then_inc(loaded, 16)
            for a in range(2):
                e.dma_start(cp[64 * a:64 * a + 64, :], dram["c"]).then_inc(loaded, 16)
            for c in range(NC + 1):
                s = slice(c * SC, (c + 1) * SC)
                if c:
                    e.wait_ge(over, c)
                    for a in range(2):
                        e.dma_start(dram["g"][:, (c - 1) * SC:c * SC, a * HH:(a + 1) * HH],
                                    gc[64 * a:64 * a + 64, :, :]).then_inc(gstored, 16)
                if c < NC:
                    for a in range(2):
                        r = slice(64 * a, 64 * a + 64)
                        e.dma_start(wc[r, :, :, :].rearrange("p t a s -> p t (a s)"), dram["w"][:, s, :]).then_inc(chunk, 16)
                        e.dma_start(ka[r, :, :], dram["ka"][:, s, a * HH:(a + 1) * HH]).then_inc(chunk, 16)
                        e.dma_start(vc[r, :, :], dram["v"][:, s, a * DD:(a + 1) * DD]).then_inc(chunk, 16)
                if 0 < c < NC:
                    n = c * SC
                    e.wait_ge(gstored, 32 * c)
                    for q in range(NB // BG):
                        g = (c - 1) * (NB // BG) + q
                        if q >= 2:
                            e.wait_ge(oldd, 8 * (g - 1))
                        b = slice(q * BG, (q + 1) * BG)
                        e.dma_start(old[q % 2][0:n, :, :], dram["g"][b, 0:n, :].rearrange("b s h -> s b h")).then_inc(oldl[q % 2], 16)
                        e.dma_start(oldw[q % 2][0:n, :, :], dram["w1t"][b, 0:n, s].rearrange("b s t -> s b t")).then_inc(oldl[q % 2], 16)
                        if q:
                            store_old(e, c, q - 1)
                    store_old(e, c, NB // BG - 1)
                    for a in range(2):
                        e.wait_ge(olds_st[a], 16 * (NB // BG) * c)
                    for a in range(2):
                        e.dma_start(olds[64 * a:64 * a + 64, :, :], dram["po"][:, :, a * HH:(a + 1) * HH]).then_inc(olds_ld, 16)
            for a in range(2):
                r = slice(64 * a, 64 * a + 64)
                e.dma_start(dram["h"][:, :, a * HH:(a + 1) * HH], hh[r, :, :]).then_inc(kept, 16)
                e.dma_start(dram["e"][:, :, a * DD:(a + 1) * DD], ee[r, :, :]).then_inc(kept, 16)
            e.wait_ge(kept, 64)
            e.wait_ge(gstored, 32 * NC)

        @block.gpsimd
        def _(e):
            e.memset(gc[:, :, :], 0.0).then_inc(cleared, 1)
            e.memset(ee[:, :, :], 0.0).then_inc(cleared, 1)
            e.memset(hh[:, :, :], 0.0).then_inc(cleared, 1)
            e.memset(gr[:, :], 0.0).then_inc(cleared, 1)
            e.wait_ge(cleared, 4)
            for c in range(NC):
                n, x = SC * (c + 1), THIN[c]
                busy = c + 1 > DOTS[c][0] or made_by(c, "g") or x < n
                if not busy:
                    gap(e, c, (gdot, 1), (gmix, 1), (gthin, 2))
                    continue
                with e.Fori(0, SC) as it:
                    i = it + c * SC
                    k.wait("gpsimd", e, *hd.now(i))
                    for j, b in enumerate(range(DOTS[c][0], c + 1)):
                        e.tensor_tensor(blk(b), hist(b), spread(h[:, :], 1, SC), ALU.mult).then_inc(*gdot.up())
                    if x < n:
                        k.wait("gpsimd", e, *wd.now(i, 0))
                        e.tensor_tensor(thin(x, n), ee[:, x:n, :], spread(w[:, x:n], 2, DD), ALU.mult).then_inc(*gthin.up())
                        k.wait("gpsimd", e, *ed.now(i))
                        e.tensor_tensor(thin(x, n), ee[:, x:n, :], spread(er[:, :], 1, n - x), ALU.mult).then_inc(*gthin.up())
                    k.wait("gpsimd", e, *wd.now(i, 1))
                    for b in made_by(c, "g"):
                        e.tensor_tensor(blk(b), hist(b), coef(b), ALU.mult).then_inc(*gmix.up())
                gap(e, c, (gdot, max(c + 1 - DOTS[c][0], 1) - (c + 1 - DOTS[c][0])),
                    (gmix, max(len(made_by(c, "g")), 1) - len(made_by(c, "g"))), (gthin, 0 if x < n else 2))

        @block.vector
        def _(e):
            v = nc.vector
            for s in (pr, hd, grd, wd, ed, gdone):
                s.seed(e)

            def settle():
                k.wait("vector", e, *own.done())
            for a in range(2):
                for b in range(2):
                    v.tensor_copy(pair[64 * a:64 * a + 64, 64 * b:64 * b + 64],
                                  k.ident[64 * a:64 * a + 64, 64 * a:64 * a + 64]).then_inc(const, 1)
            e.wait_ge(loaded, 96)
            v.tensor_tensor(b0[:, :, :], b0[:, :, :], b1, ALU.add).then_inc(const, 1)
            v.tensor_tensor(c0[:, :, :], c0[:, :, :], c1, ALU.add).then_inc(const, 1)
            e.wait_ge(const, 6)
            e.wait_ge(cleared, 4)

            def dots(c, it, i):
                made, sums = DOTS[c]
                for b in range(made):
                    v.tensor_tensor(blk(b), hist(b), spread(h[:, :], 1, SC), ALU.mult).then_inc(
                        *(vdot.up() if b < sums else own.up()))
                settle()
                for b in range(sums, c + 1):
                    if b >= made:
                        k.wait("vector", e, *gdot.now(c, it, b - made))
                    v.tensor_reduce(gr[:, b * SC:(b + 1) * SC], blk(b), axis=AX.X, op=ALU.add).then_inc(
                        *(grd.up() if b == c else own.up()))

            def mix(c, it, i):
                for b in made_by(c, "v"):
                    v.tensor_tensor(blk(b), hist(b), coef(b), ALU.mult).then_inc(*vmix.up())
                sums, first = summed_by(c, "v"), True
                rest = summed_by(c, "t")
                for j, b in enumerate(sums):
                    who = MIX[c][b][0]
                    s = {"v": vmix, "s": smix, "g": gmix}[who]
                    k.wait("vector", e, *s.now(c, it, made_by(c, who).index(b)))
                    out = acc[:, :] if len(sums) == 1 and not rest else part[:, j, :]
                    v.tensor_reduce(out, blk(b).rearrange("p s w -> p w s"), axis=AX.X, op=ALU.add).then_inc(*own.up())
                if rest:
                    k.wait("vector", e, *mxd.now(i))
                    out = part[:, len(sums), :] if sums else acc[:, :]
                    v.tensor_reduce(out, pmx[:, :].rearrange("p (j w) -> p w j", j=4), axis=AX.X, op=ALU.add).then_inc(*own.up())
                pieces = len(sums) + bool(rest)
                settle()
                if pieces > 1:
                    v.tensor_reduce(acc[:, :], part[:, 0:pieces, :].rearrange("p b w -> p w b"), axis=AX.X, op=ALU.add).then_inc(*own.up())
                    settle()

            for c in range(NC):
                n, x = SC * (c + 1), THIN[c]
                e.wait_ge(chunk, 96 * (c + 1))
                if c:
                    own.leave(SC)
                    e.wait_ge(olds_ld, 32 * c)
                    v.tensor_tensor(ka[:, :, :], ka[:, :, :], olds, ALU.add).then_inc(*own.up())
                    settle()
                    e.wait_ge(gstored, 32 * c)
                    v.memset(gc[:, :, :], 0.0).then_inc(*own.up())
                    settle()
                first = own.n
                with e.Fori(0, SC) as it:
                    i = it + c * SC
                    own.n = first
                    own.turn(it, own_steps(c))
                    row = lambda a, m0, m1: wc[:, bass.ds(it, 1), a, m0:m1].rearrange("p o s -> p (o s)")
                    v.tensor_tensor(blk(0), gc[:, :, :], spread(row(0, n - SC, n), 2, HH), ALU.mult).then_inc(*own.up())
                    settle()
                    v.tensor_reduce(acc[:, :], blk(0).rearrange("p s w -> p w s"), axis=AX.X, op=ALU.add).then_inc(*own.up())
                    settle()
                    v.tensor_tensor(pre[:, :], acc[:, :], one(ka, it), ALU.add).then_inc(*pr.up())
                    k.wait("vector", e, *sgd.now(i))
                    k.wait("vector", e, *pr.now(i))
                    v.tensor_tensor(h[:, :], pre[:, :], sg[:, :], ALU.mult).then_inc(*hd.up())
                    k.wait("vector", e, *hd.now(i))
                    dots(c, it, i)
                    v.tensor_tensor(ds[:, :], h[:, :], sg[:, :], ALU.mult).then_inc(*own.up())
                    settle()
                    v.tensor_tensor(ds[:, :], h[:, :], ds[:, :], ALU.subtract).then_inc(*own.up())
                    settle()
                    v.tensor_tensor(ds[:, :], ds[:, :], sg[:, :], ALU.add).then_inc(*own.up())
                    k.wait("vector", e, *prd.now(i, 0))
                    v.tensor_tensor(w[:, 0:n], pgr[:, 0, 0:n], row(1, 0, n), ALU.mult).then_inc(*wd.up())
                    k.wait("vector", e, *wd.now(i, 0))
                    v.tensor_tensor(thin(0, x), ee[:, 0:x, :], spread(w[:, 0:x], 2, DD), ALU.mult).then_inc(*own.up())
                    settle()
                    if x < n:
                        k.wait("vector", e, *gthin.now(c, it, 0))
                    v.tensor_reduce(eacc[:, :], thin(0, n).rearrange("p s w -> p w s"), axis=AX.X, op=ALU.add).then_inc(*own.up())
                    settle()
                    k.wait("vector", e, *pbd.now(i))
                    v.scalar_tensor_tensor(eacc[:, :], ppb[:, :], cp[:, bass.ds(i, 1)], eacc[:, :], ALU.mult, ALU.add).then_inc(*own.up())
                    settle()
                    v.tensor_tensor(eacc[:, :], eacc[:, :], one(vc, it), ALU.subtract).then_inc(*own.up())
                    settle()
                    v.tensor_scalar(er[:, :], eacc[:, :], 2.0 / D, None, ALU.mult).then_inc(*ed.up())
                    k.wait("vector", e, *ed.now(i))
                    v.tensor_tensor(thin(0, x), ee[:, 0:x, :], spread(er[:, :], 1, x), ALU.mult).then_inc(*own.up())
                    settle()
                    if x < n:
                        k.wait("vector", e, *gthin.now(c, it, 1))
                    v.tensor_reduce(gr[:, 0:n], thin(0, n), axis=AX.X, op=ALU.add).then_inc(*grd.up())
                    k.wait("vector", e, *prd.now(i, 1))
                    v.tensor_tensor(w[:, 0:n], pgr[:, 1, 0:n], row(1, 0, n), ALU.mult).then_inc(*wd.up())
                    k.wait("vector", e, *wd.now(i, 1))
                    mix(c, it, i)
                    k.wait("vector", e, *dbd.now(i))
                    v.scalar_tensor_tensor(acc[:, :], pdb[:, :], cp[:, bass.ds(i, 1)], acc[:, :], ALU.mult, ALU.add).then_inc(*own.up())
                    settle()
                    v.tensor_copy(one(hh, i), h[:, :]).then_inc(*own.up())
                    v.tensor_copy(one(ee, i), er[:, :]).then_inc(*own.up())
                    v.tensor_tensor(one(gc, it), acc[:, :], ds[:, :], ALU.mult).then_inc(*gdone.up())
                    k.wait("vector", e, *gdone.now(i))
                    own.end()
                gap(e, c, (vdot, max(DOTS[c][1], 1) - DOTS[c][1]))
                e.sem_inc(over, 1)

        @block.scalar
        def _(e):
            for s in (sgd, htk, etk, adots):
                s.seed(e)
            for c in range(NC):
                if c:
                    older(e, c)
                made, sums = DOTS[c]
                with e.Fori(0, SC) as it:
                    i = it + c * SC
                    k.wait("scalar", e, *pr.now(i))
                    e.activation(sg[:, :], pre[:, :], ACT.Sigmoid).then_inc(*sgd.up())
                    k.wait("scalar", e, *htd.now(i))
                    e.activation(ht[:, :], pht[:, :], ACT.Copy).then_inc(*htk.up())
                    for b in range(sums):
                        k.wait("scalar", e, *vdot.now(c, it, b))
                        for s in range(SC):
                            m = e.activation(blk(b)[:, s, :], blk(b)[:, s, :], ACT.Copy,
                                             accum_out=gr[:, b * SC + s:b * SC + s + 1])
                            if s == SC - 1 and b == sums - 1:
                                m.then_inc(*adots.up())
                    if not sums:
                        e.sem_inc(adots.sem, 1)
                    k.wait("scalar", e, *etd.now(i))
                    e.activation(et[:, :], pet[:, :], ACT.Copy).then_inc(*etk.up())
                    if made_by(c, "s"):
                        k.wait("scalar", e, *wd.now(i, 1))
                    for b in made_by(c, "s"):
                        for s in range(SC):
                            m = e.activation(blk(b)[:, s, :], hist(b)[:, s, :], ACT.Copy, scale=w[:, b * SC + s:b * SC + s + 1])
                        m.then_inc(*smix.up())
                gap(e, c, (smix, max(len(made_by(c, "s")), 1) - len(made_by(c, "s"))))

        @block.tensor
        def _(e):
            t = nc.tensor
            for s in (htd, pbd, prd, etd, dbd, mxd):
                s.seed(e)
            e.wait_ge(const, 6)
            for c in range(NC):
                for q in range(NB // BG if c else 0):
                    g = (c - 1) * (NB // BG) + q
                    e.wait_ge(oldl[q % 2], 32 * (g // 2 + 1))
                    for j in range(8):
                        if g * 8 + j >= 2:
                            e.wait_ge(olde, g * 8 + j - 1)
                        for b in range(2):
                            m = t.matmul(pold[:, (g * 8 + j) % 2, b, :], oldw[q % 2][0:c * SC, 2 * j + b, :],
                                         old[q % 2][0:c * SC, 2 * j + b, :], start=True, stop=True)
                        m.then_inc(oldd, 1)
                made, sums = DOTS[c]
                with e.Fori(0, SC) as it:
                    i = it + c * SC
                    k.wait("tensor", e, *hd.now(i))
                    t.transpose(pht[:, :], h[:, :], k.ident[:, :]).then_inc(*htd.up())
                    k.wait("tensor", e, *htk.now(i))
                    for to in range(2):
                        for a in range(2):
                            m = t.matmul(ppb[64 * to:64 * to + 64, :], ht[:, 64 * a:64 * a + 64],
                                         b0[:, a, DD * to:DD * to + DD], start=a == 0, stop=a == 1)
                    m.then_inc(*pbd.up())
                    k.wait("tensor", e, *grd.now(i, 0))
                    k.wait("tensor", e, *adots.now(i))
                    t.matmul(pgr[:, 0, :], pair[:, :], gr[:, :], start=True, stop=True).then_inc(*prd.up())
                    k.wait("tensor", e, *ed.now(i))
                    t.transpose(pet[:, :], er[:, :], k.ident[:, :]).then_inc(*etd.up())
                    k.wait("tensor", e, *etk.now(i))
                    for to in range(2):
                        for a in range(2):
                            m = t.matmul(pdb[64 * to:64 * to + 64, :], et[:, 64 * a:64 * a + 64],
                                         c0[:, a, HH * to:HH * to + HH], start=a == 0, stop=a == 1)
                    m.then_inc(*dbd.up())
                    k.wait("tensor", e, *grd.now(i, 1))
                    t.matmul(pgr[:, 1, :], pair[:, :], gr[:, :], start=True, stop=True).then_inc(*prd.up())
                    rest = summed_by(c, "t")
                    for b in rest:
                        who = MIX[c][b][0]
                        s = {"v": vmix, "s": smix, "g": gmix}[who]
                        k.wait("tensor", e, *s.now(c, it, made_by(c, who).index(b)))
                        for j in range(4):
                            m = t.matmul(pmx[:, :], k.ident[:, :], prod[:, b, j * 512:(j + 1) * 512],
                                         start=b == rest[0] and j == 0, stop=b == rest[-1] and j == 3)
                    if rest:
                        m.then_inc(*mxd.up())
                    else:
                        e.sem_inc(mxd.sem, 1)


def scan_outputs(k, dram, ccol):
    nc = k.nc
    with Stage(k, "answers") as st:
        gb, hb, eb = st.sb("gb", [C, HID]), st.sb("hb", [C, HID]), st.sb("eb", [C, D])
        uq, qa = st.sb("uq", [C, 2, C]), st.sb("qa", [C, HID])
        pre, hq, tt, w = st.sb("pre", [C, HID]), st.sb("hq", [C, HID]), st.sb("tt", [128, 4, C]), st.sb("w", [C, C])
        y = st.sb("y", [C, D])
        b0, b1 = st.sb("b0", [128, 2, D]), st.sb("b1", [128, 2, D])
        pp, ptt, pg, po = st.ps("pp", [C, HID]), st.ps("ptt", [128, 4, C]), st.ps("pg", [C, C]), st.ps("po", [C, 2, D])
        pb = st.ps("pb", [C, D])
        loaded = st.sem("weights_loaded")
        own = st.steps("vector_steps")
        ld = st.sig("batch_loaded", 5, 16)
        ppd, prd, hqd = st.sig("history_term", 1), st.sig("pre_done", 1), st.sig("hidden_done", 1)
        trd, trk, gd, wd = st.sig("turned", 1), st.sig("turned_kept", 1), st.sig("gram_done", 1), st.sig("weighted", 1)
        od, rd = st.sig("out_done", 1), st.sig("resid_done", 1)
        block = st.block()

        @block.sync
        def _(e):
            for t, n in ((b0, "t_w1"), (b1, "t_p1")):
                e.dma_start(t[:], k.ins[n]).then_inc(loaded, 16)
            ld.seed(e)
            with e.Fori(0, NB) as i:
                k.wait("sync", e, *rd.prev(i))
                for t, n in ((gb, "g"), (hb, "h"), (eb, "e"), (qa, "qa")):
                    e.dma_start(t[:, :], dram[n][bass.ds(i, 1), :, :].rearrange("o s w -> (o s) w")).then_inc(*ld.up())
                e.dma_start(uq[:, :, :], dram["uq"][bass.ds(i, 1), :, :, :].rearrange("o s a t -> (o s) a t")).then_inc(*ld.up())

        @block.tensor
        def _(e):
            t = nc.tensor
            for s in (ppd, trd, gd, od):
                s.seed(e)
            e.wait_ge(own.sem, 1)
            with e.Fori(0, NB) as i:
                k.wait("tensor", e, *ld.now(i))
                t.matmul(pp[:, :], uq[:, 0, :], gb[:, :], start=True, stop=True).then_inc(*ppd.up())
                k.wait("tensor", e, *hqd.now(i))
                for a, x in enumerate((hb, hb, hq, hq)):
                    m = t.transpose(ptt[:, a, :], x[:, (a % 2) * 128:(a % 2 + 1) * 128], k.ident[:, :])
                m.then_inc(*trd.up())
                k.wait("tensor", e, *trk.now(i))
                for a in range(2):
                    m = t.matmul(pg[:, :], tt[:, a, :], tt[:, 2 + a, :], start=a == 0, stop=a == 1)
                m.then_inc(*gd.up())
                for a in range(2):
                    t.matmul(pb[:, :], tt[:, 2 + a, :], b0[:, a, :], start=a == 0, stop=a == 1)
                k.wait("tensor", e, *wd.now(i))
                t.matmul(po[:, 0, :], w[:, :], eb[:, :], start=True, stop=True).then_inc(*od.up())

        @block.scalar
        def _(e):
            for s in (hqd, trk):
                s.seed(e)
            with e.Fori(0, NB) as i:
                k.wait("scalar", e, *prd.now(i))
                e.activation(hq[:, :], pre[:, :], ACT.Silu).then_inc(*hqd.up())
                k.wait("scalar", e, *trd.now(i))
                e.activation(tt[:, :, :], ptt[:, :, :], ACT.Copy).then_inc(*trk.up())

        @block.vector
        def _(e):
            v = nc.vector
            for s in (prd, wd, rd):
                s.seed(e)
            load_sum(k, e, v, b0[:, :, :], b1[:, :, :], (loaded, 32), own)
            first = own.n
            with e.Fori(0, NB) as i:
                own.n = first
                own.turn(i, 1)
                k.wait("vector", e, *ppd.now(i))
                v.tensor_tensor(pre[:, :], pp[:, :], qa[:, :], ALU.add).then_inc(*prd.up())
                k.wait("vector", e, *gd.now(i))
                v.tensor_tensor(w[:, :], pg[:, :], uq[:, 1, :], ALU.mult).then_inc(*wd.up())
                k.wait("vector", e, *od.now(i))
                r = k.resid[:, bass.ds(i * D, D)]
                v.scalar_tensor_tensor(y[:, :], pb[:, :], ccol[:, bass.ds(i, 1)], r, ALU.mult, ALU.add).then_inc(*own.up())
                k.wait("vector", e, *own.done())
                v.tensor_tensor(r, y[:, :], po[:, 0, :], ALU.add).then_inc(*rd.up())
                own.end()


def experts(k, xt):
    nc = k.nc
    G, NG = 4, NB // 4
    with Stage(k, "experts") as st:
        wr, w1, w2 = st.sb("wr", [D + 1, EXPERTS]), st.sb("w1", [D + 1, EXPERTS, DFF]), st.sb("w2", [DFF, EXPERTS, D])
        b2 = st.sb("b2", [C, EXPERTS, D])
        iot = st.sb("iot", [C, EXPERTS])
        xs = st.sb("xs", [D + 1, G * C])
        lg, top, place, pf = st.sb("lg", [C, G, 8]), st.sb("top", [C, G, 8]), st.sb("place", [C, G, 8], U32), st.sb("pf", [C, G, 8])
        gap, e2, share = st.sb("gap", [C, G]), st.sb("e2", [C, G]), st.sb("share", [C, G, 2])
        one_hot, wf = st.sb("one_hot", [C, G, 2, 8]), st.sb("wf", [C, G, 8])
        hb = st.sb("hb", [DFF, 2, G * C])
        prod, y = st.sb("prod", [C, 2, EXPERTS, D]), st.sb("y", [C, G, D])
        py, ph, pl = st.ps("py", [C, G, EXPERTS * D]), st.ps("ph", [DFF, 2, G * C]), st.ps("pl", [C, G, 8])
        loaded, const = st.sem("weights_loaded"), st.sem("constants")
        own = st.steps("vector_steps")
        xc, ld, gp, ex2 = st.sig("x_copied", 1), st.sig("logits_done", 1), st.sig("gap_done", 1), st.sig("gap_exp", 1)
        lk = st.sig("logits_kept", 1)
        hd, gl, rd = st.sig("hidden_done", EXPERTS), st.sig("gelu_done", EXPERTS), st.sig("resid_done", 1)
        yu = st.sig("answers_used", G)
        used = st.sig("hidden_used", EXPERTS)
        block = st.block()

        @block.sync
        def _(e):
            for t, n in ((wr, "m_wr"), (w1, "m_w1"), (w2, "m_w2")):
                e.dma_start(t[:], k.ins[n]).then_inc(loaded, 16)
            e.dma_start(b2[:, :, :].rearrange("p x d -> p (x d)"), k.ins["m_b2"].to_broadcast([C, EXPERTS * D])).then_inc(loaded, 16)

        @block.gpsimd
        def _(e):
            e.iota(iot[:, :], [[1, EXPERTS]], base=0, channel_multiplier=0,
                   allow_small_or_imprecise_dtypes=True).then_inc(const, 1)

        @block.tensor
        def _(e):
            t = nc.tensor
            for s in (ld, hd, used):
                s.seed(e)
            e.wait_ge(loaded, 64)
            e.wait_ge(const, 1)
            with e.Fori(0, NG) as i:
                k.wait("tensor", e, *xc.now(i))
                k.wait("tensor", e, *lk.prev(i))
                for g in range(G):
                    m = t.matmul(pl[:, g, :], xs[:, g * C:(g + 1) * C], wr[:, :], start=True, stop=True)
                m.then_inc(*ld.up())

                def hidden(x):
                    k.wait("tensor", e, *(gl.now(i, x - 2) if x >= 2 else gl.prev(i, x + EXPERTS - 2)))
                    t.matmul(ph[:, x % 2, :], w1[:, x, :], xs[:, :], start=True, stop=True).then_inc(*hd.up())
                hidden(0)
                for g in range(G):
                    k.wait("tensor", e, *yu.prev(i, g))
                for x in range(EXPERTS):
                    if x + 1 < EXPERTS:
                        hidden(x + 1)
                    k.wait("tensor", e, *gl.now(i, x))
                    for g in range(G):
                        m = t.matmul(py[:, g, x * D:(x + 1) * D], hb[:, x % 2, g * C:(g + 1) * C], w2[:, x, :],
                                     start=True, stop=True)
                    m.then_inc(*used.up())

        @block.scalar
        def _(e):
            for s in (ex2, gl):
                s.seed(e)
            with e.Fori(0, NG) as i:
                for x in range(EXPERTS):
                    k.wait("scalar", e, *hd.now(i, x))
                    k.wait("scalar", e, *(used.now(i, x - 2) if x >= 2 else used.prev(i, x + EXPERTS - 2)))
                    e.activation(hb[:, x % 2, :], ph[:, x % 2, :], ACT.Gelu).then_inc(*gl.up())
                k.wait("scalar", e, *gp.now(i))
                e.activation(e2[:, :], gap[:, :], ACT.Exp).then_inc(*ex2.up())

        @block.vector
        def _(e):
            v = nc.vector
            for s in (xc, lk, gp, yu, rd):
                s.seed(e)
            e.wait_ge(const, 1)
            e.wait_ge(loaded, 64)

            def settle():
                k.wait("vector", e, *own.done())
            with e.Fori(0, NG) as i:
                own.n = 0
                own.turn(i, PER_EXPERTS)
                k.wait("vector", e, *used.prev(i))
                v.tensor_copy(xs[:, :], xt[:, bass.ds(i * G * C, G * C)]).then_inc(*xc.up())
                k.wait("vector", e, *ld.now(i))
                v.tensor_copy(lg[:, :, :], pl[:, :, :]).then_inc(*lk.up())
                k.wait("vector", e, *lk.now(i))
                for g in range(G):
                    v.max(top[:, g, :], lg[:, g, :]).then_inc(*own.up())
                settle()
                for g in range(G):
                    v.max_index(place[:, g, :], top[:, g, :], lg[:, g, :]).then_inc(*own.up())
                v.tensor_tensor(gap[:, :], top[:, :, 1], top[:, :, 0], ALU.subtract).then_inc(*gp.up())
                settle()
                v.tensor_copy(pf[:, :, :], place[:, :, :]).then_inc(*own.up())
                settle()
                v.tensor_tensor(one_hot[:, :, :, :], spread(pf[:, :, 0:2], 3, 8),
                                spread(spread(iot[:, :], 1, 2), 1, G), ALU.is_equal).then_inc(*own.up())
                k.wait("vector", e, *ex2.now(i))
                v.tensor_scalar(share[:, :, 0], e2[:, :], 1.0, None, ALU.add).then_inc(*own.up())
                settle()
                v.reciprocal(share[:, :, 0], share[:, :, 0]).then_inc(*own.up())
                settle()
                v.tensor_tensor(share[:, :, 1], share[:, :, 0], e2[:, :], ALU.mult).then_inc(*own.up())
                settle()
                v.tensor_tensor(one_hot[:, :, :, :], one_hot[:, :, :, :], spread(share[:, :, :], 3, 8), ALU.mult).then_inc(*own.up())
                settle()
                v.tensor_tensor(wf[:, :, :], one_hot[:, :, 0, :], one_hot[:, :, 1, :], ALU.add).then_inc(*own.up())
                settle()
                k.wait("vector", e, *used.now(i))
                for g in range(G):
                    v.tensor_tensor(prod[:, g % 2, :, :], py[:, g, :].rearrange("p (x d) -> p x d", x=EXPERTS),
                                    b2[:, :, :], ALU.add).then_inc(*yu.up())
                    k.wait("vector", e, *yu.now(i, g))
                    v.tensor_tensor(prod[:, g % 2, :, :], prod[:, g % 2, :, :], spread(wf[:, g, :], 2, D), ALU.mult).then_inc(*own.up())
                    settle()
                    v.tensor_reduce(y[:, g, :], prod[:, g % 2, :, :].rearrange("p x d -> p d x"), axis=AX.X, op=ALU.add).then_inc(*own.up())
                settle()
                r = k.resid[:, bass.ds(i * G * D, G * D)]
                v.tensor_tensor(r, r, y[:, :, :].rearrange("p g d -> p (g d)"), ALU.add).then_inc(*rd.up())
                own.end()


PER_EXPERTS = 23


def store(k):
    nc = k.nc
    with Stage(k, "store") as st:
        stored = st.sem("out_stored")
        block = st.block()

        @block.sync
        def _(e):
            e.dma_start(k.out.rearrange("b s d -> s b d"), k.resid[:, :].rearrange("s (b d) -> s b d", b=NB)).then_inc(stored, 16)
            e.wait_ge(stored, 16)


def build(nc, ins, out):
    with ExitStack() as ctx:
        k = Core(nc, ctx, ins, out)
        make_constants(k)
        with ExitStack() as t:
            feats = t.enter_context(nc.sbuf_tensor("feats", [C, NB * LEN3], F32))
            lrow = t.enter_context(nc.sbuf_tensor("lrow", [1, NB * LEN3], F32))
            conv_stack(k, feats)
            importance(k, feats, lrow)
            pool_frames(k, feats, lrow)
        with ExitStack() as t:
            xt = t.enter_context(nc.sbuf_tensor("xt", [D + 1, NB * C], F32))
            norm_transpose(k, "norm1", xt)
            odd_attention(k, xt)
        with ExitStack() as t:
            xt = t.enter_context(nc.sbuf_tensor("xt2", [D + 1, NB * C], F32))
            norm_transpose(k, "norm2", xt)
            key_memory(k, xt)
        ccol = ctx.enter_context(nc.sbuf_tensor("ccol", [C, NB], F32))
        shapes = {"v": (NB, C, D), "ka": (NB, C, HID), "qa": (NB, C, HID), "w": (NB, C, 2 * C), "uq": (NB, C, 2, C),
                  "c": (NB, C + 1), "w1t": (NB, C, C), "po": (NB, SC, HID), "g": (NB, C, HID), "h": (NB, C, HID), "e": (NB, C, D)}
        dram = {n: nc.dram_tensor(f"history_{n}", s, F32, kind="Internal").ap() for n, s in shapes.items()}
        with ExitStack() as t:
            fp = t.enter_context(nc.sbuf_tensor("fp", [C, NB, 3 * D + GATES], F32))
            gates = t.enter_context(nc.sbuf_tensor("gates", [C, NB, GATES], F32))
            with ExitStack() as u:
                xt = u.enter_context(nc.sbuf_tensor("xt3", [D + 1, NB * C], F32))
                norm_transpose(k, "norm3", xt)
                gated_features(k, xt, fp, gates)
            scan_weights(k, fp, gates, dram, ccol)
        scan(k, dram)
        scan_outputs(k, dram, ccol)
        with ExitStack() as t:
            xt = t.enter_context(nc.sbuf_tensor("xt4", [D + 1, NB * C], F32))
            norm_transpose(k, "norm4", xt, "m_affine")
            experts(k, xt)
        store(k)


def laid_out(a):
    import numpy as np
    t = lambda n: np.asarray(a["L0_tok_" + n])
    x = np.pad(np.asarray(a["x"])[:, 0, :], ((0, 0), (3, 4)), mode="reflect")
    o = {"x": x[:, :5 * (LEN0 + 1)].reshape(NB, LEN0 + 1, 5).transpose(0, 2, 1)}
    o["conv0"] = t("conv0_w")[:, 0, :].T
    for n in (1, 2, 3):
        o[f"conv{n}"] = t(f"conv{n}_w").transpose(1, 2, 0)
    o["conv_b"] = np.stack([t(f"conv{n}_b") for n in range(4)], 1)
    o["norm_g"] = np.stack([t(f"n{n}_w") for n in range(5)], 1)
    o["norm_b"] = np.stack([t(f"n{n}_b") for n in range(5)], 1)
    o["mlp_w1"] = t("mlp_w1")
    o["mlp_w2"] = t("mlp_w2").reshape(4, C, DMLP).transpose(1, 0, 2)
    o["mlp_w3"] = t("mlp_w3").reshape(4, C).T
    o["mlp_b1"] = t("mlp_b1").reshape(4, C).T
    o["mlp_b2"] = t("mlp_b2").reshape(4, C).T
    o["mlp_b3"] = t("mlp_b3").reshape(1, 1)
    b = lambda n: np.asarray(a["L0_attn_" + n])
    for n in "QKV":
        w = b("W_" + n).transpose(1, 0, 2).reshape(D, HEADS * DH)
        o["a_w" + n.lower()] = np.concatenate([w, b("b_" + n).reshape(1, -1)], 0)
    o["a_wo"] = b("W_O").reshape(2, 128, D).transpose(1, 0, 2)
    o["a_bo"] = b("b_O").reshape(1, D)
    f = lambda n: np.asarray(a["L0_ffn_" + n])
    o["k_wpk"] = f("Wq_pk").T.reshape(16, 32, D).transpose(1, 0, 2)
    o["k_keys"] = f("pk_keys").transpose(3, 0, 2, 1).reshape(32, 16, NKEY)
    o["k_wq"] = f("Wq")
    o["k_wo"] = f("Wo").reshape(4, 128, D).transpose(1, 0, 2)
    o["k_table"] = np.concatenate([f("keys_table"), f("values_table")], 1)
    g = lambda n: np.asarray(a["L1_attn_" + n])
    o["t_wf"] = g("W_fused").T
    o["t_w0"], o["t_p0"] = g("W0"), g("P0")
    for n, w in (("w1", g("W1")), ("p1", g("P1"))):
        o["t_" + n] = w.reshape(2, 128, D).transpose(1, 0, 2)
        o["t_" + n + "t"] = w.T.reshape(2, D // 2, HID).transpose(1, 0, 2)
    h = lambda n: np.asarray(a["L1_ffn_" + n])
    o["m_affine"] = np.stack([h("gamma"), h("beta")], 1)
    o["m_wr"] = np.concatenate([h("Wr"), h("br").reshape(1, EXPERTS)], 0)
    o["m_w1"] = np.concatenate([h("W1").transpose(1, 0, 2), h("b1").reshape(1, EXPERTS, DFF)], 0)
    o["m_w2"] = h("W2").transpose(1, 0, 2)
    o["m_b2"] = h("b2").reshape(1, EXPERTS * D)
    return {n: np.ascontiguousarray(v) for n, v in o.items()}


def kernel(**inputs):
    import concourse.bacc as _bacc
    from concourse import mybir as _mybir
    from concourse.bass_utils import run_bass_kernel_spmd as _run

    nc = _bacc.Bacc("TRN2", target_bir_lowering=False, num_devices=1)
    arrays = laid_out(inputs)
    ins = {n: nc.dram_tensor(n, v.shape, _mybir.dt.from_np(v.dtype), kind="ExternalInput").ap()
           for n, v in arrays.items()}
    out = nc.dram_tensor("out", (NB, C, D), _mybir.dt.float32, kind="ExternalOutput").ap()
    build(nc, ins, out)
    r = _run(nc, [arrays], core_ids=[0])
    return r.results[0]["out"]
```

```python
import concourse.bass as bass
from concourse import mybir
from contextlib import ExitStack

F32 = mybir.dt.float32
U32 = mybir.dt.uint32
ALU = mybir.AluOpType
ACT = mybir.ActivationFunctionType
AX = mybir.AxisListType
EPS = 1e-5

NB = 64
C = 128
D = 64
LEN0, LEN1, LEN2, LEN3 = 2048, 512, 256, 128
DMLP = 512
HEADS, DH = 8, 32
NKEY, NKV, TOPK = 64, 4096, 16
HID = 256
EXPERTS, DFF = 8, 128
BIG = 1.0e30


class Signal:

    def __init__(self, nc, ctx, name, per, by=1, seeded=True):
        self.sem, self.per, self.by = ctx.enter_context(nc.semaphore(name)), per, by
        self.lead = per if seeded else 0

    def seed(self, e):
        e.sem_inc(self.sem, self.lead * self.by)

    def up(self):
        return self.sem, self.by

    def now(self, i, j=None):
        j = self.per - 1 if j is None else j
        return self.sem, (i * self.per + (self.lead + j + 1)) * self.by

    def prev(self, i, j=None):
        j = self.per - 1 if j is None else j
        assert self.lead
        return self.sem, (i * self.per + (j + 1)) * self.by


class Steps:

    def __init__(self, nc, ctx, name):
        self.sem, self.base, self.n = ctx.enter_context(nc.semaphore(name)), 0, 0

    def turn(self, i, per):
        self.base, self.per, self.n0 = i * per, per, self.n

    def end(self):
        assert self.n - self.n0 == self.per, (self.n - self.n0, self.per)

    def up(self):
        self.n += 1
        return self.sem, 1

    def done(self):
        return self.sem, self.base + self.n

    def leave(self, turns):
        self.base = 0
        self.n = self.n0 + turns * self.per


class Core:

    def __init__(self, nc, ctx, ins, out):
        self.nc, self.ctx, self.ins, self.out = nc, ctx, ins, out
        self.gates = {n: ctx.enter_context(nc.semaphore(f"{n}_passed_wait")) for n in
                      ("tensor", "vector", "scalar", "gpsimd", "sync")}
        self.resid = ctx.enter_context(nc.sbuf_tensor("resid", [C, NB * D], F32))
        self.ident = ctx.enter_context(nc.sbuf_tensor("ident", [128, 128], F32))

    def wait(self, name, e, sem, value):
        e.wait_ge(sem, value)
        e.sem_inc(self.gates[name], 1)


def spread(ap, axis, n):
    a = ap.unsqueeze(axis)
    shape = list(a.shape)
    shape[axis] = n
    return a.to_broadcast(shape)


class Stage:

    def __init__(self, k, name):
        self.k, self.nc, self.ctx, self.sems, self.name = k, k.nc, ExitStack(), [], name

    def __enter__(self):
        return self

    def sb(self, name, shape, dt=F32):
        return self.ctx.enter_context(self.nc.sbuf_tensor(f"{self.name}_{name}", shape, dt))

    def ps(self, name, shape):
        return self.ctx.enter_context(self.nc.psum_tensor(f"{self.name}_{name}", shape, F32))

    def sem(self, name):
        s = self.ctx.enter_context(self.nc.semaphore(f"{self.name}_{name}"))
        self.sems.append(s)
        return s

    def sig(self, name, per, by=1, seeded=True):
        s = Signal(self.nc, self.ctx, f"{self.name}_{name}", per, by, seeded)
        self.sems.append(s.sem)
        return s

    def steps(self, name):
        s = Steps(self.nc, self.ctx, f"{self.name}_{name}")
        self.sems.append(s.sem)
        return s

    def block(self):
        self.blk = ExitStack()
        return self.blk.enter_context(self.nc.Block())

    def __exit__(self, *a):
        if a[0] is None:
            self.blk.close()
            for s in self.sems:
                self.nc.sync.sem_clear(s)
            self.nc.all_engine_barrier()
            self.ctx.close()


def make_constants(k):
    nc = k.nc
    with Stage(k, "const") as st:
        made = st.sem("ident_made")
        block = st.block()

        @block.gpsimd
        def _(e):
            e.memset(k.ident[:, :], 0.0).then_inc(made, 1)
            e.wait_ge(made, 1)
            e.affine_select(out=k.ident[:, :], in_=k.ident[:, :], compare_op=ALU.not_equal, fill=1.0,
                            base=0, pattern=[[-1, 128]], channel_multiplier=1).then_inc(made, 1)
            e.wait_ge(made, 2)


def conv_stack(k, feats):
    nc, ins = k.nc, k.ins
    with Stage(k, "conv") as st:
        sb = st.sb
        ps = st.ps
        sig = st.sig
        w0 = sb("w0", [10, C])
        w1, w2, w3 = sb("w1", [C, 8, C]), sb("w2", [C, 4, C]), sb("w3", [C, 4, C])
        s0, ssum = sb("s0", [10, 1]), sb("ssum", [C, 16])
        bias, biasc, gamma, beta = sb("bias", [C, 4]), sb("biasc", [C, 4]), sb("gamma", [C, 5]), sb("beta", [C, 5])
        cent, avg = sb("cent", [C, C]), sb("avg", [C, C])
        xcol = sb("xcol", [10, LEN0])
        h0, h1, h2 = sb("h0", [C, LEN0 + 4]), sb("h1", [C, LEN1 + 2]), sb("h2", [C, LEN2 + 2])
        sq, normal, inv = sb("sq", [C, 7, 512]), sb("normal", [C, 7, 512]), sb("inv", [C, 7, 512])
        root, epsc = sb("root", [C, 7, 512]), sb("epsc", [C, 1])
        py, pv = ps("py", [C, 4, 512]), ps("pv", [C, 4, 512])
        loaded = st.sem("weights_loaded")
        ready = st.sem("weights_centred")
        bias_mm = st.sem("bias_product")
        setup = st.steps("vector_setup_steps")
        xin = sig("x_loaded", 1, 32, seeded=False)
        conv, var = sig("conv_done", 7), sig("variance_done", 7)
        squared, rooted, inverted = sig("squared", 7), sig("roots_done", 7), sig("inverted", 7)
        normed, relued, padded = sig("normed", 7), sig("relu_done", 7), sig("padded", 8)
        width = [512, 512, LEN1, LEN3, 512, 512, LEN2]
        layer = [0, 0, 1, 3, 0, 0, 2]
        chunks = {0: 0, 1: 1, 4: 2, 5: 3}
        bank = [0, 1, 2, 3, 0, 1, 3]
        yb = [py[:, bank[s], 0:width[s]] for s in range(7)]
        vb = [pv[:, bank[s], 0:width[s]] for s in range(7)]

        def filled(i, slot):
            if not isinstance(i, int):
                return True
            batch = i + 1 if slot in chunks else i - 1 if slot == 3 else i
            return 0 <= batch < NB

        def wait(name, e, sem, value):
            if not isinstance(value, int) or value > 0:
                k.wait(name, e, sem, value)

        def bank_free(s, i, slot):
            return s.prev(i, {0: 4, 1: 5, 2: 2, 3: 6}[slot]) if slot < 4 else s.now(i, {4: 0, 5: 1, 6: 3}[slot])

        def empty(name, e, s, i, slot):
            if i < NB or slot < 3:
                wait(name, e, *(s.now(i, slot - 1) if slot else s.prev(i, 6)))
                e.sem_inc(s.sem, 1)

        def turns(e, turn):
            turn(-1)
            turn(0)
            with e.Fori(0, NB - 3) as i:
                turn(i + 1)
            turn(NB - 2)
            turn(NB - 1)
            turn(NB)
        block = st.block()

        @block.sync
        def _(e):
            for t, n in ((w0, "conv0"), (w1, "conv1"), (w2, "conv2"), (w3, "conv3"), (bias, "conv_b"),
                         (gamma, "norm_g"), (beta, "norm_b")):
                e.dma_start(t[:], ins[n]).then_inc(loaded, 16)
            x = ins["x"]

            def load(xi):
                e.dma_start(xcol[0:5, :], xi[:, 0:LEN0]).then_inc(xin.sem, 16)
                e.dma_start(xcol[5:10, :], xi[:, 1:LEN0 + 1]).then_inc(xin.sem, 16)
            load(x[0, :, :])
            with e.Fori(0, NB - 1) as i:
                e.wait_ge(*conv.prev(i, 5))
                load(x[bass.ds(i + 1, 1), :, :].rearrange("o r t -> (o r) t"))

        @block.tensor
        def _(e):
            t = nc.tensor

            def chunk(slot):
                q = chunks[slot]
                t.matmul(yb[slot], w0[:, :], xcol[:, q * 512:(q + 1) * 512], start=True, stop=True).then_inc(*conv.up())

            def sum_squares(slot):
                t.matmul(vb[slot], avg[:, :], sq[:, slot, 0:width[slot]], start=True, stop=True).then_inc(*var.up())
            e.wait_ge(ready, 1)
            t.matmul(py[:, 0, 0:4], cent[:, :], bias[:, :], start=True, stop=True).then_inc(bias_mm, 1)
            e.wait_ge(ready, 2)

            def product(i, slot):
                if not filled(i, slot):
                    return empty("tensor", e, conv, i, slot)
                wait("tensor", e, *bank_free(normed, i, slot))
                if slot in chunks:
                    if slot == 0:
                        k.wait("tensor", e, *xin.now(i + 1))
                    return chunk(slot)
                h, w, taps, stride, ends = {2: (h0, w1, 8, 4, padded.prev(i, 5)), 3: (h2, w3, 4, 2, padded.prev(i, 7)),
                                            6: (h1, w2, 4, 2, padded.now(i, 3))}[slot]
                k.wait("tensor", e, *ends)
                for tap in range(taps):
                    src = h[:, tap:tap + stride * (width[slot] - 1) + 1:stride]
                    m = t.matmul(yb[slot], w[:, tap, :], src, start=tap == 0, stop=tap == taps - 1)
                m.then_inc(*conv.up())

            def variance(i, slot):
                if not filled(i, slot):
                    return empty("tensor", e, var, i, slot)
                k.wait("tensor", e, *squared.now(i, slot))
                wait("tensor", e, *bank_free(rooted, i, slot))
                sum_squares(slot)

            def turn(i):
                variance(i, 0)
                variance(i, 1)
                product(i, 2)
                product(i, 3)
                variance(i, 2)
                variance(i, 3)
                product(i, 4)
                product(i, 5)
                variance(i, 4)
                variance(i, 5)
                product(i, 6)
                if not isinstance(i, int) or i < NB:
                    product(i + 1, 0)
                    product(i + 1, 1)
                variance(i, 6)
            product(-1, 0)
            product(-1, 1)
            turns(e, turn)

        @block.scalar
        def _(e):
            def square(slot):
                e.activation(sq[:, slot, 0:width[slot]], yb[slot], ACT.Square,
                             bias=biasc[:, layer[slot]:layer[slot] + 1]).then_inc(*squared.up())

            def square_root(slot):
                e.activation(root[:, slot, 0:width[slot]], vb[slot], ACT.Sqrt, bias=epsc[:, 0:1]).then_inc(*rooted.up())

            def relu_to(slot, dst):
                n = layer[slot]
                e.activation(dst, normal[:, slot, 0:width[slot]], ACT.Relu,
                             bias=beta[:, n:n + 1], scale=gamma[:, n:n + 1]).then_inc(*relued.up())
            e.wait_ge(ready, 3)

            def squares(i, slot):
                if not filled(i, slot):
                    return empty("scalar", e, squared, i, slot)
                k.wait("scalar", e, *conv.now(i, slot))
                wait("scalar", e, *var.prev(i, slot))
                square(slot)

            def roots(i, slot):
                if not filled(i, slot):
                    return empty("scalar", e, rooted, i, slot)
                k.wait("scalar", e, *var.now(i, slot))
                wait("scalar", e, *inverted.prev(i, slot))
                square_root(slot)

            def relu(i, slot):
                if not filled(i, slot):
                    return empty("scalar", e, relued, i, slot)
                k.wait("scalar", e, *normed.now(i, slot))
                if slot in chunks:
                    wait("scalar", e, *conv.now(i, 2))
                    dst = h0[:, 2 + chunks[slot] * 512:2 + (chunks[slot] + 1) * 512]
                elif slot == 2:
                    wait("scalar", e, *conv.prev(i, 6))
                    dst = h1[:, 1:1 + LEN1]
                elif slot == 6:
                    wait("scalar", e, *conv.now(i, 3))
                    dst = h2[:, 1:1 + LEN2]
                else:
                    dst = feats[:, bass.ds((i - 1) * LEN3, LEN3)]
                relu_to(slot, dst)

            def turn(i):
                roots(i, 1)
                squares(i, 2)
                relu(i, 0)
                squares(i, 3)
                roots(i, 2)
                relu(i, 1)
                roots(i, 3)
                squares(i, 4)
                squares(i, 5)
                roots(i, 4)
                relu(i, 2)
                relu(i, 3)
                roots(i, 5)
                relu(i, 4)
                squares(i, 6)
                more = not isinstance(i, int) or i < NB
                if more:
                    squares(i + 1, 0)
                    squares(i + 1, 1)
                roots(i, 6)
                if more:
                    roots(i + 1, 0)
                relu(i, 5)
                relu(i, 6)
            squares(-1, 0)
            squares(-1, 1)
            roots(-1, 0)
            turns(e, turn)

        @block.gpsimd
        def _(e):
            def turn(i):
                for slot, n, h, ends in ((0, 0, h0, ((0, 4), (1, 3))),
                                         (2, 2, h1, ((0, 2), (LEN1 + 1, LEN1 - 1))),
                                         (5, 4, h0, ((LEN0 + 2, LEN0), (LEN0 + 3, LEN0 - 1))),
                                         (6, 6, h2, ((0, 2), (LEN2 + 1, LEN2 - 1)))):
                    if filled(i, slot):
                        k.wait("gpsimd", e, *relued.now(i, slot))
                        for to, at in ends:
                            e.tensor_copy(h[:, to:to + 1], h[:, at:at + 1]).then_inc(*padded.up())
                    elif i < NB:
                        wait("gpsimd", e, *(padded.now(i, n - 1) if n else padded.prev(i, 7)))
                        e.sem_inc(padded.sem, 2)
            turns(e, turn)

        @block.vector
        def _(e):
            v = nc.vector
            v.memset(avg[:, :], 1.0 / (C - 1)).then_inc(*setup.up())
            v.memset(epsc[:, :], EPS).then_inc(*setup.up())
            v.tensor_scalar(cent[:, :], k.ident[:, :], -1.0 / C, None, ALU.add).then_inc(*setup.up())
            e.wait_ge(*setup.done())
            e.wait_ge(loaded, 16 * 7)
            v.tensor_reduce(s0[:, :], w0[:, :], axis=AX.X, op=ALU.add).then_inc(ready, 1)
            for t, n, o in ((w1, 8, 0), (w2, 4, 8), (w3, 4, 12)):
                v.tensor_reduce(ssum[:, o:o + n], t[:, :, :], axis=AX.X, op=ALU.add).then_inc(*setup.up())
            e.wait_ge(*setup.done())
            e.wait_ge(ready, 1)
            v.tensor_scalar(s0[:, :], s0[:, :], -1.0 / C, None, ALU.mult).then_inc(*setup.up())
            v.tensor_scalar(ssum[:, :], ssum[:, :], -1.0 / C, None, ALU.mult).then_inc(*setup.up())
            e.wait_ge(*setup.done())
            v.tensor_scalar(w0[:, :], w0[:, :], s0[:, 0:1], None, ALU.add).then_inc(*setup.up())
            for t, n, o in ((w1, 8, 0), (w2, 4, 8), (w3, 4, 12)):
                v.tensor_tensor(t[:, :, :], t[:, :, :], spread(ssum[:, o:o + n], 2, C), ALU.add).then_inc(*setup.up())
            e.wait_ge(*setup.done())
            e.wait_ge(bias_mm, 1)
            v.tensor_copy(biasc[:, :], py[:, 0, 0:4]).then_inc(ready, 1)
            e.wait_ge(ready, 2)
            e.sem_inc(ready, 1)

            def invert(slot):
                v.reciprocal(inv[:, slot, 0:width[slot]], root[:, slot, 0:width[slot]]).then_inc(*inverted.up())

            def normalise(slot):
                v.scalar_tensor_tensor(normal[:, slot, 0:width[slot]], yb[slot], biasc[:, layer[slot]:layer[slot] + 1],
                                       inv[:, slot, 0:width[slot]], ALU.add, ALU.mult).then_inc(*normed.up())

            def turn(i):
                for slot in range(7):
                    if not filled(i, slot):
                        empty("vector", e, inverted, i, slot)
                        empty("vector", e, normed, i, slot)
                        continue
                    k.wait("vector", e, *rooted.now(i, slot))
                    invert(slot)
                    k.wait("vector", e, *inverted.now(i, slot))
                    wait("vector", e, *relued.prev(i, slot))
                    normalise(slot)
            turns(e, turn)


def importance(k, feats, lrow):
    nc, ins = k.nc, k.ins
    with Stage(k, "imp") as st:
        sb = st.sb
        sig = st.sig
        w1, w2, w3 = sb("mw1", [C, DMLP]), sb("mw2", [C, 4, DMLP]), sb("mw3", [C, 4])
        b1, b2, b3 = sb("mb1", [C, 4]), sb("mb2", [C, 4]), sb("mb3", [1, 1])
        z1, z2 = sb("z1", [C, 4, 512]), sb("z2", [C, 4, 512])
        p1 = st.ps("p1", [C, 4, 512])
        p2 = st.ps("p2", [C, 4, 512])
        loaded = st.sem("mlp_weights_loaded")
        mm1, mm2, mm3 = sig("layer1_done", 4), sig("layer2_done", 4), sig("layer3_done", 1)
        g1, g2, row = sig("gelu1_done", 4), sig("gelu2_done", 4), sig("logits_kept", 1)
        block = st.block()

        @block.sync
        def _(e):
            for t, n in ((w1, "mlp_w1"), (w2, "mlp_w2"), (w3, "mlp_w3"), (b1, "mlp_b1"), (b2, "mlp_b2"), (b3, "mlp_b3")):
                e.dma_start(t[:], ins[n]).then_inc(loaded, 16)

        @block.tensor
        def _(e):
            for s in (mm1, mm2, mm3):
                s.seed(e)
            e.wait_ge(loaded, 96)
            with e.Fori(0, NB // 4) as i:
                for m in range(4):
                    if m == 0:
                        k.wait("tensor", e, *row.prev(i))
                    k.wait("tensor", e, *g1.prev(i, m))
                    nc.tensor.matmul(p1[:, m, :], w1[:, m * C:(m + 1) * C], feats[:, bass.ds(i * 512, 512)],
                                     start=True, stop=True).then_inc(*mm1.up())
                for m in range(4):
                    k.wait("tensor", e, *g2.prev(i, m))
                    for c in range(4):
                        if m == 0:
                            k.wait("tensor", e, *g1.now(i, c))
                        x = nc.tensor.matmul(p2[:, m, :], w2[:, c, m * C:(m + 1) * C], z1[:, c, :],
                                             start=c == 0, stop=c == 3)
                    x.then_inc(*mm2.up())
                for c in range(4):
                    k.wait("tensor", e, *g2.now(i, c))
                    x = nc.tensor.matmul(p1[0:1, 0, :], w3[:, c:c + 1], z2[:, c, :], start=c == 0, stop=c == 3)
                x.then_inc(*mm3.up())

        @block.scalar
        def _(e):
            for s in (g1, g2, row):
                s.seed(e)
            e.wait_ge(loaded, 96)
            with e.Fori(0, NB // 4) as i:
                for m in range(4):
                    k.wait("scalar", e, *mm1.now(i, m))
                    k.wait("scalar", e, *mm2.prev(i))
                    e.activation(z1[:, m, :], p1[:, m, :], ACT.Gelu, bias=b1[:, m:m + 1]).then_inc(*g1.up())
                for m in range(4):
                    k.wait("scalar", e, *mm2.now(i, m))
                    k.wait("scalar", e, *mm3.prev(i))
                    e.activation(z2[:, m, :], p2[:, m, :], ACT.Gelu, bias=b2[:, m:m + 1]).then_inc(*g2.up())
                k.wait("scalar", e, *mm3.now(i))
                e.activation(lrow[:, bass.ds(i * 512, 512)], p1[0:1, 0, :], ACT.Identity,
                             bias=b3[:, 0:1]).then_inc(*row.up())


def pool_frames(k, feats, lrow):
    nc, ins = k.nc, k.ins
    G, NG = 8, NB // 8
    with Stage(k, "pool") as st:
        sb = st.sb
        ps = st.ps
        sig = st.sig
        imp, cs = sb("imp", [NB, C]), sb("cs", [NB, C + 1])
        zero, tot = sb("zero", [NB, C]), sb("tot", [NB, 1])
        cst, csp = sb("cst", [C, NB]), sb("csp", [C, NB])
        step = sb("step", [C, D + 1])
        pa, pb = sb("pa", [C, G, D + 1]), sb("pb", [C, G, D + 1])
        da, db, wm = sb("da", [C, G, D]), sb("db", [C, G, D]), sb("wm", [C, G, D])
        avg = sb("avgp", [C, C])
        gamma, beta = sb("gammap", [C, 5]), sb("betap", [C, 5])
        fg, fm, ft = sb("fg", [C, G * C]), sb("fm", [C, G]), sb("ft", [C, G, C])
        sq, root, inv, normal = sb("sqp", [C, 512]), sb("rootp", [C, 512]), sb("invp", [C, 512]), sb("normp", [C, 512])
        epsc = sb("epscp", [C, 1])
        pt = ps("pt", [C, G, C])
        po, pv, pc = ps("po", [C, 512]), ps("pvp", [C, 512]), ps("pc", [C, 2, NB])
        scratch = nc.dram_tensor("logit_rows", (NB, C), F32, kind="Internal").ap()
        moved = st.sem("logits_moved")
        act0 = st.sem("sigmoid_done")
        tr0 = st.sem("sums_transposed")
        vec0 = st.sem("sums_done")
        iot = st.sem("steps_made")
        own = st.steps("vector_pool_steps")
        grp, ftd, mm, var = sig("group_copied", 1), sig("frames_transposed", 1), sig("pooled", 1), sig("pool_variance", 1)
        sqd, rtd, rel = sig("pool_squared", 1), sig("pool_rooted", 1), sig("pool_relu", 1)
        cen, wts, nrm = sig("frames_centred", 1), sig("weights_made", 1), sig("pool_normed", 1)
        block = st.block()

        @block.sync
        def _(e):
            e.dma_start(scratch.rearrange("b t -> (b t)").rearrange("(o n) -> o n", o=1), lrow[:, :]).then_inc(moved, 16)
            e.wait_ge(moved, 16)
            e.dma_start(imp[:, :], scratch).then_inc(moved, 16)
            e.dma_start(gamma[:, :], ins["norm_g"]).then_inc(moved, 16)
            e.dma_start(beta[:, :], ins["norm_b"]).then_inc(moved, 16)

        @block.gpsimd
        def _(e):
            e.iota(step[:, :], [[-1, D + 1]], base=0, channel_multiplier=0,
                   allow_small_or_imprecise_dtypes=True).then_inc(iot, 1)
            e.wait_ge(iot, 1)
            e.memset(step[:, D:D + 1], -BIG).then_inc(iot, 1)
            e.memset(avg[:, :], 1.0 / (C - 1)).then_inc(iot, 1)
            e.memset(epsc[:, :], EPS).then_inc(iot, 1)
            e.memset(zero[:, :], 0.0).then_inc(iot, 1)
            e.memset(cs[:, 0:1], 0.0).then_inc(iot, 1)

        @block.scalar
        def _(e):
            for s in (grp, sqd, rtd, rel):
                s.seed(e)
            e.wait_ge(moved, 64)
            e.wait_ge(iot, 6)
            e.activation(imp[:, :], imp[:, :], ACT.Sigmoid).then_inc(act0, 1)
            with e.Fori(0, NG) as i:
                k.wait("scalar", e, *ftd.prev(i))
                e.activation(fg[:, :], feats[:, bass.ds(i * G * C, G * C)], ACT.Copy).then_inc(*grp.up())
                k.wait("scalar", e, *mm.now(i))
                k.wait("scalar", e, *var.prev(i))
                e.activation(sq[:, :], po[:, :], ACT.Square).then_inc(*sqd.up())
                k.wait("scalar", e, *var.now(i))
                k.wait("scalar", e, *nrm.prev(i))
                e.activation(root[:, :], pv[:, :], ACT.Sqrt, bias=epsc[:, 0:1]).then_inc(*rtd.up())
                k.wait("scalar", e, *nrm.now(i))
                e.activation(k.resid[:, bass.ds(i * G * D, G * D)], normal[:, :], ACT.Relu,
                             bias=beta[:, 4:5], scale=gamma[:, 4:5]).then_inc(*rel.up())

        @block.tensor
        def _(e):
            for s in (ftd, mm, var):
                s.seed(e)
            e.wait_ge(vec0, 1)
            nc.tensor.transpose(pc[:, 0, :], cs[:, 1:C + 1], k.ident[0:NB, 0:NB]).then_inc(tr0, 1)
            nc.tensor.transpose(pc[:, 1, :], cs[:, 0:C], k.ident[0:NB, 0:NB]).then_inc(tr0, 1)
            with e.Fori(0, NG) as i:
                k.wait("tensor", e, *grp.now(i))
                k.wait("tensor", e, *cen.prev(i))
                for g in range(G):
                    m = nc.tensor.transpose(pt[:, g, :], fg[:, g * C:(g + 1) * C], k.ident[:, :])
                m.then_inc(*ftd.up())
                k.wait("tensor", e, *cen.now(i))
                k.wait("tensor", e, *wts.now(i))
                k.wait("tensor", e, *nrm.prev(i))
                for g in range(G):
                    m = nc.tensor.matmul(po[:, g * D:(g + 1) * D], ft[:, g, :], wm[:, g, :], start=True, stop=True)
                m.then_inc(*mm.up())
                k.wait("tensor", e, *sqd.now(i))
                k.wait("tensor", e, *rtd.prev(i))
                nc.tensor.matmul(pv[:, :], avg[:, :], sq[:, :], start=True, stop=True).then_inc(*var.up())

        @block.vector
        def _(e):
            v = nc.vector
            for s in (cen, wts, nrm):
                s.seed(e)
            e.wait_ge(act0, 1)
            v.tensor_scalar(imp[:, :], imp[:, :], 1e-5, None, ALU.add).then_inc(*own.up())
            e.wait_ge(*own.done())
            v.tensor_reduce(tot[:, :], imp[:, :], axis=AX.X, op=ALU.add).then_inc(*own.up())
            e.wait_ge(*own.done())
            v.reciprocal(tot[:, :], tot[:, :]).then_inc(*own.up())
            e.wait_ge(*own.done())
            v.tensor_scalar(imp[:, :], imp[:, :], tot[:, 0:1], float(D), ALU.mult, ALU.mult).then_inc(*own.up())
            e.wait_ge(*own.done())
            v.tensor_tensor_scan(cs[:, 1:C + 1], imp[:, :], zero[:, :], 0.0, ALU.add, ALU.add).then_inc(vec0, 1)
            e.wait_ge(tr0, 2)
            v.tensor_copy(cst[:, :], pc[:, 0, :]).then_inc(*own.up())
            v.tensor_copy(csp[:, :], pc[:, 1, :]).then_inc(*own.up())
            e.wait_ge(*own.done())
            base = own.n
            with e.Fori(0, NG) as i:
                own.n = base
                own.turn(i, PER_POOL)
                for p, s in ((pa, cst), (pb, csp)):
                    v.tensor_tensor(p[:, :, :], spread(step[:, :], 1, G),
                                    spread(s[:, bass.ds(i * G, G)], 2, D + 1), ALU.add).then_inc(*own.up())
                k.wait("vector", e, *own.done())
                for p in (pa, pb):
                    v.tensor_scalar(p[:, :, :], p[:, :, :], 0.0, None, ALU.max).then_inc(*own.up())
                k.wait("vector", e, *own.done())
                for p, d in ((pa, da), (pb, db)):
                    v.tensor_tensor(d[:, :, :], p[:, :, 0:D], p[:, :, 1:D + 1], ALU.subtract).then_inc(*own.up())
                k.wait("vector", e, *own.done())
                k.wait("vector", e, *mm.prev(i))
                v.tensor_tensor(wm[:, :, :], da[:, :, :], db[:, :, :], ALU.subtract).then_inc(*wts.up())
                k.wait("vector", e, *ftd.now(i))
                for g2 in range(2):
                    v.tensor_reduce(fm[:, 4 * g2:4 * g2 + 4], pt[:, 4 * g2:4 * g2 + 4, :], axis=AX.X, op=ALU.add).then_inc(*own.up())
                k.wait("vector", e, *own.done())
                v.tensor_scalar(fm[:, :], fm[:, :], 1.0 / C, None, ALU.mult).then_inc(*own.up())
                k.wait("vector", e, *own.done())
                v.tensor_tensor(ft[:, 0:4, :], pt[:, 0:4, :], spread(fm[:, 0:4], 2, C), ALU.subtract).then_inc(*own.up())
                v.tensor_tensor(ft[:, 4:8, :], pt[:, 4:8, :], spread(fm[:, 4:8], 2, C), ALU.subtract).then_inc(*cen.up())
                k.wait("vector", e, *rtd.now(i))
                v.reciprocal(inv[:, :], root[:, :]).then_inc(*own.up())
                k.wait("vector", e, *own.done())
                k.wait("vector", e, *rel.prev(i))
                v.tensor_tensor(normal[:, :], po[:, :], inv[:, :], ALU.mult).then_inc(*nrm.up())
                own.end()


PER_POOL = 11


def norm_transpose(k, name, xt, affine=None):
    G, NT, PAIR = 8, NB // 16, range(2)
    nc = k.nc
    with Stage(k, name) as st:
        two = lambda n, shape: [st.sb(f"{n}{a}", shape) for a in PAIR]
        mean, dev, sq = two("mean", [C, G]), two("dev", [C, G, D]), two("sq", [C, G, D])
        ss, root, inv, xn = two("ss", [C, G]), two("root", [C, G]), two("inv", [C, G]), two("xn", [C, G, D])
        epsc = st.sb("epsc", [C, 1])
        gb = st.sb("gb", [D, 2])
        pt = [st.ps(f"pt{a}", [D, G, C]) for a in PAIR]
        loaded = st.sem("affine_loaded")
        const = st.sem("norm_constants")
        own = st.steps("vector_norm_steps")
        devd, sqd, var = st.sig("deviations", 2), st.sig("squares", 2), st.sig("variances", 2)
        rtd, nrm, trd, kept = st.sig("roots", 2), st.sig("normed", 2), st.sig("transposed", 2), st.sig("kept", 2)
        block = st.block()

        @block.sync
        def _(e):
            if affine:
                e.dma_start(gb[:, :], k.ins[affine]).then_inc(loaded, 16)

        @block.vector
        def _(e):
            v = nc.vector
            for s in (devd, var, nrm):
                s.seed(e)
            v.memset(xt[D:D + 1, :], 1.0).then_inc(const, 1)
            v.memset(epsc[:, :], EPS).then_inc(const, 1)
            with e.Fori(0, NT) as i:
                own.n = 0
                own.turn(i, 6)
                x = [k.resid[:, bass.ds((2 * i + a) * G * D, G * D)].rearrange("p (g d) -> p g d", g=G) for a in PAIR]
                for a in PAIR:
                    v.tensor_reduce(mean[a][:, :], x[a], axis=AX.X, op=ALU.add).then_inc(*own.up())
                k.wait("vector", e, *own.done())
                for a in PAIR:
                    v.tensor_scalar(mean[a][:, :], mean[a][:, :], 1.0 / D, None, ALU.mult).then_inc(*own.up())
                k.wait("vector", e, *own.done())
                for a in PAIR:
                    v.tensor_tensor(dev[a][:, :, :], x[a], spread(mean[a][:, :], 2, D), ALU.subtract).then_inc(*devd.up())
                for a in PAIR:
                    k.wait("vector", e, *sqd.now(i, a))
                    v.tensor_reduce(ss[a][:, :], sq[a][:, :, :], axis=AX.X, op=ALU.add).then_inc(*var.up())
                for a in PAIR:
                    k.wait("vector", e, *rtd.now(i, a))
                    v.reciprocal(inv[a][:, :], root[a][:, :]).then_inc(*own.up())
                    k.wait("vector", e, *own.done())
                    k.wait("vector", e, *trd.prev(i, a))
                    v.tensor_tensor(xn[a][:, :, :], dev[a][:, :, :], spread(inv[a][:, :], 2, D), ALU.mult).then_inc(*nrm.up())
                own.end()

        @block.scalar
        def _(e):
            for s in (sqd, rtd, kept):
                s.seed(e)
            e.wait_ge(const, 2)
            if affine:
                e.wait_ge(loaded, 16)
            with e.Fori(0, NT) as i:
                for a in PAIR:
                    k.wait("scalar", e, *devd.now(i, a))
                    e.activation(sq[a][:, :, :], dev[a][:, :, :], ACT.Square).then_inc(*sqd.up())
                for a in PAIR:
                    k.wait("scalar", e, *var.now(i, a))
                    e.activation(root[a][:, :], ss[a][:, :], ACT.Sqrt, bias=epsc[:, 0:1], scale=1.0 / D).then_inc(*rtd.up())
                for a in PAIR:
                    k.wait("scalar", e, *trd.now(i, a))
                    dst = xt[0:D, bass.ds((2 * i + a) * G * C, G * C)].rearrange("p (g c) -> p g c", g=G)
                    if affine:
                        e.activation(dst, pt[a][:, :, :], ACT.Identity, bias=gb[:, 1:2], scale=gb[:, 0:1]).then_inc(*kept.up())
                    else:
                        e.activation(dst, pt[a][:, :, :], ACT.Copy).then_inc(*kept.up())

        @block.tensor
        def _(e):
            trd.seed(e)
            with e.Fori(0, NT) as i:
                for a in PAIR:
                    k.wait("tensor", e, *nrm.now(i, a))
                    k.wait("tensor", e, *kept.prev(i, a))
                    for g in range(G):
                        m = nc.tensor.transpose(pt[a][:, g, :], xn[a][:, g, :], k.ident[:, :])
                    m.then_inc(*trd.up())


def odd_attention(k, xt):
    nc = k.nc
    DA = DH + 1
    with Stage(k, "oddattn") as st:
        wq, wk, wv = st.sb("wq", [D + 1, HEADS * DH]), st.sb("wk", [D + 1, HEADS * DH]), st.sb("wv", [D + 1, HEADS * DH])
        wo, bo, ones = st.sb("wo", [128, 2, D]), st.sb("bo", [1, D]), st.sb("ones", [1, C])
        mask = st.sb("mask", [C, C])
        xb = st.sb("xb", [D + 1, C])
        qz, kt, va = st.sb("qz", [128, 2, 4, C]), st.sb("kt", [128, 2, C]), st.sb("va", [C, HEADS, DA])
        s, mx, p, pt_ = st.sb("s", [C, HEADS, C]), st.sb("mx", [C, HEADS]), st.sb("p", [C, HEADS, C]), st.sb("pt_", [C, HEADS, C])
        rz, zn, zt = st.sb("rz", [C, HEADS]), st.sb("zn", [C, HEADS, DH]), st.sb("zt", [128, 2, C])
        pqk, pv, pS = st.ps("pqk", [128, 4, C]), st.ps("pv", [C, 512]), st.ps("pS", [C, HEADS, C])
        pT, pz, pzt = st.ps("pT", [C, HEADS, C]), st.ps("pz", [C, 512]), st.ps("pzt", [128, 512])
        loaded, const = st.sem("attn_weights_loaded"), st.sem("attn_constants")
        xc, qkv, qkk, vk = st.sig("x_copied", 1), st.sig("qkv_done", 1), st.sig("qk_kept", 5), st.sig("v_kept", 1)
        sc, masked, maxed = st.sig("scores_done", 1), st.sig("scores_masked", 1), st.sig("row_maxima", 1)
        sh, ex = st.sig("scores_shifted", 1), st.sig("exps_done", 1)
        tr, ta, tb, zd = (st.sig("probs_transposed", 1), st.sig("probs_kept_low", 1), st.sig("probs_kept_high", 1),
                          st.sig("mixed", 1))
        inverted, zn_s, ztd = st.sig("sums_inverted", 1), st.sig("mix_normed", 1), st.sig("mix_transposed", 1)
        ztk, od, rd = st.sig("mix_kept", 1), st.sig("out_done", 1), st.sig("resid_done", 1)
        block = st.block()

        @block.sync
        def _(e):
            for t, n in ((wq, "a_wq"), (wk, "a_wk"), (wv, "a_wv"), (wo, "a_wo"), (bo, "a_bo")):
                e.dma_start(t[:], k.ins[n]).then_inc(loaded, 16)

        @block.gpsimd
        def _(e):
            e.memset(mask[:, :], 0.0).then_inc(const, 1)
            e.memset(qz[:, :, :, :], 0.0).then_inc(const, 1)
            e.memset(va[:, :, :], 1.0).then_inc(const, 1)
            e.memset(ones[:, :], 1.0).then_inc(const, 1)
            e.wait_ge(const, 4)
            e.affine_select(out=mask[:, :], in_=mask[:, :], compare_op=ALU.is_ge, fill=-BIG, base=0,
                            pattern=[[-1, C]], channel_multiplier=1).then_inc(const, 1)
            e.wait_ge(const, 5)
            e.affine_select(out=mask[:, 0:C:2], in_=mask[:, 0:C:2], compare_op=ALU.is_equal, fill=-BIG, base=0,
                            pattern=[[-2, C // 2]], channel_multiplier=1).then_inc(const, 1)

        @block.vector
        def _(e):
            v = nc.vector
            for g in (tb, inverted, zn_s, rd):
                g.seed(e)
            e.wait_ge(const, 6)

            def copy_x(b):
                v.tensor_copy(xb[:, :], xt[0:D + 1, bass.ds(b * C, C)]).then_inc(*xc.up())

            def keep_v():
                v.tensor_copy(va[:, :, 0:DH], pv[:, 0:HEADS * DH].rearrange("p (h d) -> p h d", h=HEADS)).then_inc(*vk.up())

            def mask_scores():
                v.scalar_tensor_tensor(s[:, :, :], pS[:, :, :], float(DH) ** -0.5, spread(mask[:, :], 1, HEADS),
                                       ALU.mult, ALU.add).then_inc(*masked.up())

            def shift_scores(masked_now, maxed_now):
                k.wait("vector", e, *masked_now)
                v.tensor_reduce(mx[:, :], s[:, :, :], axis=AX.X, op=ALU.max).then_inc(*maxed.up())
                k.wait("vector", e, *maxed_now)
                v.tensor_tensor(s[:, :, :], s[:, :, :], spread(mx[:, :], 2, C), ALU.subtract).then_inc(*sh.up())

            def turn(i, more):
                if more:
                    k.wait("vector", e, *qkv.prev(i))
                    copy_x(i + 1)
                k.wait("vector", e, *tr.now(i))
                k.wait("vector", e, *zd.prev(i))
                v.tensor_copy(pt_[:, 4:8, :], pT[:, 4:8, :]).then_inc(*tb.up())
                if more:
                    k.wait("vector", e, *sc.now(i))
                    k.wait("vector", e, *ex.prev(i))
                    mask_scores()
                k.wait("vector", e, *zd.now(i))
                z = pz[:, 0:HEADS * DA].rearrange("p (h d) -> p h d", h=HEADS)
                v.reciprocal(rz[:, :], z[:, :, DH]).then_inc(*inverted.up())
                k.wait("vector", e, *inverted.now(i))
                k.wait("vector", e, *ztd.prev(i))
                v.tensor_tensor(zn[:, :, :], z[:, :, 0:DH], spread(rz[:, :], 2, DH), ALU.mult).then_inc(*zn_s.up())
                if more:
                    shift_scores(masked.now(i), maxed.now(i))
                    k.wait("vector", e, *qkv.now(i))
                    keep_v()
                k.wait("vector", e, *od.now(i))
                r = k.resid[:, bass.ds(i * D, D)]
                v.tensor_tensor(r, r, pzt[:, 256:256 + D], ALU.add).then_inc(*rd.up())
            copy_x(0)
            e.wait_ge(*qkv.prev(0))
            keep_v()
            e.wait_ge(*sc.prev(0))
            mask_scores()
            shift_scores(masked.prev(0), maxed.prev(0))
            with e.Fori(0, NB - 1) as i:
                turn(i, True)
            turn(NB - 1, False)

        @block.scalar
        def _(e):
            for g in (ta, ztk):
                g.seed(e)
            e.wait_ge(const, 6)

            def keep_qk():
                for j in range(4):
                    r = slice(32 * j, 32 * j + 32)
                    e.activation(qz[r, :, j, :], pqk[r, 0:2, :], ACT.Copy).then_inc(*qkk.up())
                e.activation(kt[:, :, :], pqk[:, 2:4, :], ACT.Copy).then_inc(*qkk.up())

            def exps():
                e.activation(p[:, :, :], s[:, :, :], ACT.Exp).then_inc(*ex.up())

            def turn(i, more):
                if more:
                    k.wait("scalar", e, *qkv.now(i))
                    k.wait("scalar", e, *sc.prev(i))
                    keep_qk()
                k.wait("scalar", e, *tr.now(i))
                k.wait("scalar", e, *zd.prev(i))
                e.activation(pt_[:, 0:4, :], pT[:, 0:4, :], ACT.Copy).then_inc(*ta.up())
                k.wait("scalar", e, *ztd.now(i))
                k.wait("scalar", e, *od.prev(i))
                e.activation(zt[:, :, :], pzt[:, 0:256].rearrange("p (a c) -> p a c", a=2), ACT.Copy).then_inc(*ztk.up())
                if more:
                    k.wait("scalar", e, *sh.now(i))
                    exps()
            e.wait_ge(*qkv.prev(0))
            keep_qk()
            e.wait_ge(*sh.prev(0))
            exps()
            with e.Fori(0, NB - 1) as i:
                turn(i, True)
            turn(NB - 1, False)

        @block.tensor
        def _(e):
            t = nc.tensor
            for g in (tr, zd, ztd, od):
                g.seed(e)
            e.wait_ge(loaded, 80)
            e.wait_ge(const, 6)

            def project():
                for n, w in ((0, wq), (2, wk)):
                    for g in range(2):
                        t.matmul(pqk[:, n + g, :], w[:, g * 128:(g + 1) * 128], xb[:, :], start=True, stop=True)
                t.matmul(pv[:, 0:256], xb[:, :], wv[:, :], start=True, stop=True).then_inc(*qkv.up())

            def scores():
                for h in range(HEADS):
                    m = t.matmul(pS[:, h, :], qz[:, h // 4, h % 4, :], kt[:, h // 4, :], start=True, stop=True)
                m.then_inc(*sc.up())

            def turn(i, more):
                if more:
                    k.wait("tensor", e, *xc.now(i))
                    k.wait("tensor", e, *qkk.prev(i))
                    k.wait("tensor", e, *vk.prev(i))
                    project()
                k.wait("tensor", e, *ex.prev(i))
                k.wait("tensor", e, *ta.prev(i))
                k.wait("tensor", e, *tb.prev(i))
                for h in range(HEADS):
                    m = t.transpose(pT[:, h, :], p[:, h, :], k.ident[:, :])
                m.then_inc(*tr.up())
                if more:
                    k.wait("tensor", e, *qkk.now(i))
                    k.wait("tensor", e, *masked.prev(i))
                    scores()
                k.wait("tensor", e, *ta.now(i))
                k.wait("tensor", e, *tb.now(i))
                k.wait("tensor", e, *vk.prev(i))
                k.wait("tensor", e, *zn_s.prev(i))
                for h in range(HEADS):
                    m = t.matmul(pz[:, h * DA:(h + 1) * DA], pt_[:, h, :], va[:, h, :], start=True, stop=True)
                m.then_inc(*zd.up())
                k.wait("tensor", e, *zn_s.now(i))
                k.wait("tensor", e, *rd.prev(i))
                zf = zn[:, :, :].rearrange("p h d -> p (h d)")
                for g in range(2):
                    m = t.transpose(pzt[:, g * C:(g + 1) * C], zf[:, g * 128:(g + 1) * 128], k.ident[:, :])
                m.then_inc(*ztd.up())
                k.wait("tensor", e, *ztk.now(i))
                for g in range(2):
                    t.matmul(pzt[:, 256:256 + D], zt[:, g, :], wo[:, g, :], start=g == 0, stop=False)
                t.matmul(pzt[:, 256:256 + D], ones[:, :], bo[:, :], start=False, stop=True).then_inc(*od.up())
            e.wait_ge(*xc.prev(0))
            project()
            e.wait_ge(*qkk.prev(0))
            scores()
            with e.Fori(0, NB - 1) as i:
                turn(i, True)
            turn(NB - 1, False)




RUNS = ((0, 1, 16), (1, 1, 8), (2, 1, 5), (3, 1, 4), (4, 1, 3), (5, 3, 2), (8, 8, 1))
NCAND = sum(n * m for _, n, m in RUNS)
RING = 8


def key_memory(k, xt):
    nc = k.nc
    DV = D + 1
    with Stage(k, "pkm") as st:
        wpk, keys = st.sb("wpk", [32, 16, D]), st.sb("keys", [32, 16, NKEY])
        wsim = st.sb("wsim", [D, 16, NKEY])
        wq, wo = st.sb("wq", [D, HEADS * D]), st.sb("wo", [128, 4, D])
        mask = st.sb("mask", [C, C])
        hoff, iot = st.sb("hoff", [C, HEADS, TOPK]), st.sb("iot", [C, NCAND])
        xb = st.sb("xb", [D, C])
        sim, rest = st.sb("sim", [C, 16, NKEY]), st.sb("rest", [C, 16, NKEY])
        val, idx = st.sb("val", [C, 16, TOPK]), st.sb("idx", [C, 16, TOPK], U32)
        idf = st.sb("idf", [C, 16, TOPK])
        cand, crest, cidx = st.sb("cand", [C, HEADS, NCAND]), st.sb("crest", [C, HEADS, NCAND]), st.sb("cidx", [C, HEADS, NCAND])
        best, pos, posf = st.sb("best", [C, HEADS, TOPK]), st.sb("pos", [C, HEADS, TOPK], U32), st.sb("posf", [C, HEADS, TOPK])
        hit = st.sb("hit", [C, 4, TOPK, NCAND])
        rowf, row = st.sb("rowf", [C, HEADS, TOPK]), st.sb("row", [C, HEADS * TOPK], U32)
        shifted, wnew, wcur = st.sb("shifted", [C, HEADS, TOPK]), st.sb("wnew", [C, HEADS, TOPK]), st.sb("wcur", [C, HEADS, TOPK])
        tot, rtot = st.sb("tot", [C, HEADS]), st.sb("rtot", [C, HEADS])
        ring = [[st.sb(f"ring{r}", [C, TOPK, 2 * D])] for r in range(RING)]
        ring = [r[0] for r in ring]
        kk, vv = st.sb("kk", [C, HEADS, D]), st.sb("vv", [C, HEADS, DV])
        qz, kt = st.sb("qz", [128, HEADS, C]), st.sb("kt", [128, 4, C])
        s, mx, p, pt_ = st.sb("s", [C, HEADS, C]), st.sb("mx", [C, HEADS]), st.sb("p", [C, HEADS, C]), st.sb("pt_", [C, HEADS, C])
        rz, zn, zt = st.sb("rz", [C, HEADS]), st.sb("zn", [C, HEADS, D]), st.sb("zt", [128, 4, C])
        pq, psim, pk = st.ps("pq", [128, 4, C]), st.ps("psim", [128, 16, NKEY]), st.ps("pk", [128, 4, C])
        pS, pT = st.ps("pS", [C, HEADS, C]), st.ps("pT", [C, HEADS, C])
        loaded, const, prep = st.sem("weights_loaded"), st.sem("constants"), st.sem("key_product")
        own = st.steps("vector_steps")
        xc, simd, simk = st.sig("x_copied", 1), st.sig("similarities_done", 1), st.sig("similarities_kept", 1)
        wsh, wex = st.sig("best_shifted", 1), st.sig("best_exps", 1)
        rows = st.sig("rows_chosen", 2)
        got = [st.sig(f"rows_gathered{r}", HEADS // RING, 256, seeded=False) for r in range(RING)]
        used = st.sig("rows_used", HEADS)
        qd, qk = st.sig("q_done", 1), st.sig("q_kept", 2)
        kd, kkept = st.sig("k_transposed", 1), st.sig("k_kept", 1)
        sc, sh, ex, tr = st.sig("scores_done", 1), st.sig("scores_shifted", 1), st.sig("exps_done", 1), st.sig("probs_transposed", 1)
        ta, tb, zd, zns = st.sig("probs_kept_low", 1), st.sig("probs_kept_high", 1), st.sig("mixed", 1), st.sig("mix_normed", 1)
        ztd, ztk, od, rd = st.sig("mix_transposed", 1), st.sig("mix_kept", 1), st.sig("out_done", 1), st.sig("resid_done", 1)
        block = st.block()

        @block.sync
        def _(e):
            for t, n in ((wpk, "k_wpk"), (keys, "k_keys"), (wq, "k_wq"), (wo, "k_wo")):
                e.dma_start(t[:], k.ins[n]).then_inc(loaded, 16)

        @block.gpsimd
        def _(e):
            e.memset(mask[:, :], 0.0).then_inc(const, 1)
            e.memset(qz[:, :, :], 0.0).then_inc(const, 1)
            e.memset(vv[:, :, :], 1.0).then_inc(const, 1)
            e.iota(hoff[:, :, :], [[NKV, HEADS], [0, TOPK]], base=0, channel_multiplier=0,
                   allow_small_or_imprecise_dtypes=True).then_inc(const, 1)
            e.iota(iot[:, :], [[1, NCAND]], base=0, channel_multiplier=0,
                   allow_small_or_imprecise_dtypes=True).then_inc(const, 1)
            e.wait_ge(const, 5)
            e.affine_select(out=mask[:, :], in_=mask[:, :], compare_op=ALU.is_ge, fill=-BIG, base=0,
                            pattern=[[-1, C]], channel_multiplier=1).then_inc(const, 1)
            with e.Fori(0, NB) as i:
                for h in range(HEADS):
                    if h % (HEADS // 2) == 0:
                        k.wait("gpsimd", e, *rows.now(i, h // (HEADS // 2)))
                    k.wait("gpsimd", e, *(used.now(i, h - RING) if h >= RING else used.prev(i, h + HEADS - RING)))
                    for j in range(TOPK):
                        e.indirect_dma_start(ring[h % RING][:, j, :], None, k.ins["k_table"],
                                             bass.IndirectOffsetOnAxis(ap=row[:, h * TOPK + j:h * TOPK + j + 1], axis=0)
                                             ).then_inc(got[h % RING].sem, 16)

        @block.vector
        def _(e):
            v = nc.vector
            for g in (xc, wsh, rows, used, kkept, sh, tb, zns, rd):
                g.seed(e)
            e.wait_ge(prep, 1)
            v.tensor_copy(wsim[:, :, :], psim[0:D, :, :]).then_inc(prep, 1)
            e.wait_ge(const, 6)

            def settle():
                k.wait("vector", e, *own.done())

            def top16(vals, spots, x, y, n, m):
                for a in range(n):
                    v.max(vals[:, a, 0:8], x[:, a, :]).then_inc(*own.up())
                settle()
                for a in range(n):
                    v.max_index(spots[:, a, 0:8], vals[:, a, 0:8], x[:, a, :]).then_inc(*own.up())
                    v.match_replace(y[:, a, :], vals[:, a, 0:8], x[:, a, :], -BIG).then_inc(*own.up())
                settle()
                for a in range(n):
                    v.max(vals[:, a, 8:16], y[:, a, :]).then_inc(*own.up())
                settle()
                for a in range(n):
                    v.max_index(spots[:, a, 8:16], vals[:, a, 8:16], y[:, a, :]).then_inc(*own.up())

            def search(i):
                k.wait("vector", e, *simd.prev(i))
                v.tensor_copy(xb[:, :], xt[0:D, bass.ds(i * C, C)]).then_inc(*xc.up())
                k.wait("vector", e, *simk.now(i))
                top16(val, idx, sim, rest, 16, NKEY)
                settle()
                v.tensor_copy(idf[:, :, :], idx[:, :, :]).then_inc(*own.up())
                settle()
                v.scalar_tensor_tensor(idf[:, HEADS:, :], idf[:, HEADS:, :], float(NKEY), hoff[:, :, :],
                                       ALU.mult, ALU.add).then_inc(*own.up())
                settle()
                o = 0
                for a, n, m in RUNS:
                    for to, at in ((cand, val), (cidx, idf)):
                        v.tensor_tensor(to[:, :, o:o + n * m].rearrange("p h (a b) -> p h a b", a=n),
                                        spread(at[:, 0:HEADS, a:a + n], 3, m),
                                        spread(at[:, HEADS:, 0:m], 2, n), ALU.add).then_inc(*own.up())
                    o += n * m
                settle()
                top16(best, pos, cand, crest, HEADS, NCAND)
                settle()
                k.wait("vector", e, *wex.prev(i))
                v.tensor_tensor(shifted[:, :, :], best[:, :, :], spread(best[:, :, 0], 2, TOPK), ALU.subtract).then_inc(*wsh.up())
                v.tensor_copy(posf[:, :, :], pos[:, :, :]).then_inc(*own.up())
                settle()
                for a in (0, 4):
                    v.tensor_tensor(hit[:, :, :, :], spread(posf[:, a:a + 4, :], 3, NCAND),
                                    spread(spread(iot[:, :], 1, TOPK), 1, 4), ALU.is_equal).then_inc(*own.up())
                    settle()
                    v.tensor_tensor(hit[:, :, :, :], hit[:, :, :, :], spread(cidx[:, a:a + 4, :], 2, TOPK), ALU.mult).then_inc(*own.up())
                    settle()
                    v.tensor_reduce(rowf[:, a:a + 4, :], hit[:, :, :, :], axis=AX.X, op=ALU.add).then_inc(*own.up())
                    settle()
                k.wait("vector", e, *wex.now(i))
                v.tensor_reduce(tot[:, :], wnew[:, :, :], axis=AX.X, op=ALU.add).then_inc(*own.up())
                settle()
                v.reciprocal(rtot[:, :], tot[:, :]).then_inc(*own.up())
                settle()
                v.tensor_tensor(wnew[:, :, :], wnew[:, :, :], spread(rtot[:, :], 2, TOPK), ALU.mult).then_inc(*own.up())
                settle()

            def choose(half):
                n = HEADS // 2
                v.tensor_copy(row[:, half * n * TOPK:(half + 1) * n * TOPK],
                              rowf[:, half * n:(half + 1) * n, :].rearrange("p h j -> p (h j)")).then_inc(*rows.up())

            def mix(i, h):
                r = ring[h % RING]
                k.wait("vector", e, *got[h % RING].now(i, h // RING))
                if h % (HEADS // 2) == HEADS // 2 - 1 and k.more:
                    choose(h // (HEADS // 2))
                v.tensor_tensor(r[:, :, :], r[:, :, :], spread(wcur[:, h, :], 2, 2 * D), ALU.mult).then_inc(*own.up())
                settle()
                if h == 0:
                    k.wait("vector", e, *kd.prev(i))
                    k.wait("vector", e, *zd.prev(i))
                v.tensor_reduce(kk[:, h, :], r[:, :, 0:D].rearrange("p j d -> p d j"), axis=AX.X, op=ALU.add).then_inc(*own.up())
                v.tensor_reduce(vv[:, h, 0:D], r[:, :, D:].rearrange("p j d -> p d j"), axis=AX.X, op=ALU.add).then_inc(*used.up())

            def attend(i):
                k.wait("vector", e, *kd.now(i))
                v.tensor_copy(kt[:, :, :], pk[:, :, :]).then_inc(*kkept.up())
                k.wait("vector", e, *sc.now(i))
                v.tensor_tensor(s[:, :, :], pS[:, :, :], spread(mask[:, :], 1, HEADS), ALU.add).then_inc(*own.up())
                settle()
                v.tensor_reduce(mx[:, :], s[:, :, :], axis=AX.X, op=ALU.max).then_inc(*own.up())
                settle()
                v.tensor_tensor(s[:, :, :], s[:, :, :], spread(mx[:, :], 2, C), ALU.subtract).then_inc(*sh.up())
                k.wait("vector", e, *tr.now(i))
                v.tensor_copy(pt_[:, 4:8, :], pT[:, 4:8, :]).then_inc(*tb.up())
                k.wait("vector", e, *zd.now(i))
                z = [pS[:, 4 * a:4 * a + 4, :].rearrange("p h c -> p (h c)")[:, 0:4 * DV].rearrange("p (h d) -> p h d", h=4)
                     for a in range(2)]
                for a in range(2):
                    v.reciprocal(rz[:, 4 * a:4 * a + 4], z[a][:, :, D]).then_inc(*own.up())
                settle()
                v.tensor_tensor(zn[:, 0:4, :], z[0][:, :, 0:D], spread(rz[:, 0:4], 2, D), ALU.mult).then_inc(*own.up())
                v.tensor_tensor(zn[:, 4:8, :], z[1][:, :, 0:D], spread(rz[:, 4:8], 2, D), ALU.mult).then_inc(*zns.up())
                k.wait("vector", e, *od.now(i))
                r = k.resid[:, bass.ds(i * D, D)]
                v.tensor_tensor(r, r, pk[:, 0, 0:D], ALU.add).then_inc(*rd.up())

            def turn(i, more):
                k.more = more
                if more:
                    search(i + 1)
                for h in range(HEADS):
                    mix(i, h)
                if more:
                    v.tensor_copy(wcur[:, :, :], wnew[:, :, :]).then_inc(*own.up())
                attend(i)

            search(0)
            choose(0)
            choose(1)
            v.tensor_copy(wcur[:, :, :], wnew[:, :, :]).then_inc(*own.up())
            own.turn(0, 0)
            first = own.n
            with e.Fori(0, NB - 1) as i:
                own.n = first
                own.turn(i, PER_PKM)
                turn(i, True)
                own.end()
            own.leave(NB - 1)
            turn(NB - 1, False)

        @block.scalar
        def _(e):
            for g in (simk, wex, qk, ex, ta, ztk):
                g.seed(e)
            e.wait_ge(const, 6)

            def search(i):
                k.wait("scalar", e, *simd.now(i))
                k.wait("scalar", e, *wsh.prev(i))
                e.activation(sim[:, :, :], psim[:, :, :], ACT.Copy).then_inc(*simk.up())
                k.wait("scalar", e, *wsh.now(i))
                e.activation(wnew[:, :, :], shifted[:, :, :], ACT.Exp).then_inc(*wex.up())

            def attend(i):
                k.wait("scalar", e, *qd.now(i))
                e.activation(qz[0:D, 0:HEADS:2, :], pq[0:D, :, :], ACT.Copy, scale=float(D) ** -0.5).then_inc(*qk.up())
                e.activation(qz[D:, 1:HEADS:2, :], pq[D:, :, :], ACT.Copy, scale=float(D) ** -0.5).then_inc(*qk.up())
                k.wait("scalar", e, *sh.now(i))
                k.wait("scalar", e, *tr.prev(i))
                e.activation(p[:, :, :], s[:, :, :], ACT.Exp).then_inc(*ex.up())
                k.wait("scalar", e, *tr.now(i))
                k.wait("scalar", e, *zd.prev(i))
                e.activation(pt_[:, 0:4, :], pT[:, 0:4, :], ACT.Copy).then_inc(*ta.up())
                k.wait("scalar", e, *ztd.now(i))
                e.activation(zt[:, :, :], pq[:, :, :], ACT.Copy).then_inc(*ztk.up())
            search(0)
            with e.Fori(0, NB - 1) as i:
                search(i + 1)
                attend(i)
            attend(NB - 1)

        @block.tensor
        def _(e):
            t = nc.tensor
            for g in (simd, qd, kd, sc, tr, zd, ztd, od):
                g.seed(e)
            e.wait_ge(loaded, 64)
            for n in range(16):
                m = t.matmul(psim[0:D, n, :], wpk[:, n, :], keys[:, n, :], start=True, stop=True)
            m.then_inc(prep, 1)
            e.wait_ge(prep, 2)
            e.wait_ge(const, 6)

            def search(i):
                k.wait("tensor", e, *xc.now(i))
                k.wait("tensor", e, *simk.prev(i))
                w = wsim[:, :, :].rearrange("p n k -> p (n k)")
                o = psim[:, :, :].rearrange("p n k -> p (n k)")
                for a in range(2):
                    m = t.matmul(o[:, a * 512:(a + 1) * 512], xb[:, :], w[:, a * 512:(a + 1) * 512], start=True, stop=True)
                m.then_inc(*simd.up())

            def attend(i):
                k.wait("tensor", e, *ztk.prev(i))
                for a in range(4):
                    m = t.matmul(pq[:, a, :], wq[:, a * 128:(a + 1) * 128], xt[0:D, bass.ds(i * C, C)], start=True, stop=True)
                m.then_inc(*qd.up())
                k.wait("tensor", e, *used.now(i))
                k.wait("tensor", e, *rd.prev(i))
                kf = kk[:, :, :].rearrange("p h d -> p (h d)")
                for a in range(4):
                    m = t.transpose(pk[:, a, :], kf[:, a * 128:(a + 1) * 128], k.ident[:, :])
                m.then_inc(*kd.up())
                k.wait("tensor", e, *kkept.now(i))
                k.wait("tensor", e, *qk.now(i))
                for h in range(HEADS):
                    m = t.matmul(pS[:, h, :], qz[:, h, :], kt[:, h // 2, :], start=True, stop=True)
                m.then_inc(*sc.up())
                k.wait("tensor", e, *ex.now(i))
                for h in range(HEADS):
                    m = t.transpose(pT[:, h, :], p[:, h, :], k.ident[:, :])
                m.then_inc(*tr.up())
                k.wait("tensor", e, *ta.now(i))
                k.wait("tensor", e, *tb.now(i))
                for h in range(HEADS):
                    o = pS[:, 4 * (h // 4):4 * (h // 4) + 4, :].rearrange("p h c -> p (h c)")
                    m = t.matmul(o[:, (h % 4) * DV:(h % 4 + 1) * DV], pt_[:, h, :], vv[:, h, :], start=True, stop=True)
                m.then_inc(*zd.up())
                k.wait("tensor", e, *zns.now(i))
                zf = zn[:, :, :].rearrange("p h d -> p (h d)")
                for a in range(4):
                    m = t.transpose(pq[:, a, :], zf[:, a * 128:(a + 1) * 128], k.ident[:, :])
                m.then_inc(*ztd.up())
                k.wait("tensor", e, *ztk.now(i))
                for a in range(4):
                    m = t.matmul(pk[:, 0, 0:D], zt[:, a, :], wo[:, a, :], start=a == 0, stop=a == 3)
                m.then_inc(*od.up())
            search(0)
            with e.Fori(0, NB - 1) as i:
                search(i + 1)
                attend(i)
            attend(NB - 1)


PER_PKM = 168


SC = 16
LR = 0.1
GATES = 3


def gated_features(k, xt, fp, gates):
    nc = k.nc
    W = 3 * D + GATES
    with Stage(k, "gated") as st:
        wf, xb = st.sb("wf", [D, W]), st.sb("xb", [D, 2 * C])
        pf = st.ps("pf", [C, 2, W])
        sq, n2 = st.sb("sq", [C, NB, D]), st.sb("n2", [C, 2, NB])
        loaded = st.sem("weights_loaded")
        own, aown = st.steps("vector_steps"), st.steps("scalar_steps")
        xc, fd, fk = st.sig("x_copied", 1), st.sig("features_done", 1), st.sig("features_kept", 1)
        block = st.block()

        @block.sync
        def _(e):
            e.dma_start(wf[:, :], k.ins["t_wf"]).then_inc(loaded, 16)

        @block.tensor
        def _(e):
            fd.seed(e)
            e.wait_ge(loaded, 16)
            with e.Fori(0, NB // 2) as i:
                k.wait("tensor", e, *xc.now(i))
                k.wait("tensor", e, *fk.prev(i))
                for g in range(2):
                    m = nc.tensor.matmul(pf[:, g, :], xb[:, g * C:(g + 1) * C], wf[:, :], start=True, stop=True)
                m.then_inc(*fd.up())

        @block.scalar
        def _(e):
            fk.seed(e)
            with e.Fori(0, NB // 2) as i:
                k.wait("scalar", e, *fd.now(i))
                e.activation(fp[:, bass.ds(2 * i, 2), :], pf[:, :, :], ACT.Copy).then_inc(*fk.up())
            e.wait_ge(*fk.now(NB // 2 - 1))
            e.activation(fp[:, :, 0:3 * D], fp[:, :, 0:3 * D], ACT.Silu).then_inc(*aown.up())
            e.activation(gates[:, :, :], fp[:, :, 3 * D:], ACT.Sigmoid).then_inc(*aown.up())
            e.wait_ge(own.sem, NORM_AT)
            e.activation(n2[:, :, :], n2[:, :, :], ACT.Sqrt).then_inc(*aown.up())

        @block.vector
        def _(e):
            v = nc.vector
            xc.seed(e)
            with e.Fori(0, NB // 2) as i:
                k.wait("vector", e, *fd.prev(i))
                v.tensor_copy(xb[:, :], xt[0:D, bass.ds(i * 2 * C, 2 * C)]).then_inc(*xc.up())
            e.wait_ge(aown.sem, 2)
            for a in range(2):
                x = fp[:, :, a * D:(a + 1) * D]
                v.tensor_tensor(sq[:, :, :], x, x, ALU.mult).then_inc(*own.up())
                e.wait_ge(*own.done())
                v.tensor_reduce(n2[:, a, :], sq[:, :, :], axis=AX.X, op=ALU.add).then_inc(*own.up())
                e.wait_ge(*own.done())
            assert own.n == NORM_AT
            v.tensor_scalar(gates[:, :, 1], gates[:, :, 1], LR, None, ALU.mult).then_inc(*own.up())
            e.wait_ge(aown.sem, 3)
            v.tensor_scalar(n2[:, :, :], n2[:, :, :], 1e-12, None, ALU.max).then_inc(*own.up())
            e.wait_ge(*own.done())
            v.reciprocal(n2[:, :, :], n2[:, :, :]).then_inc(*own.up())
            e.wait_ge(*own.done())
            for a in range(2):
                x = fp[:, :, a * D:(a + 1) * D]
                v.tensor_tensor(x, x, spread(n2[:, a, :], 2, D), ALU.mult).then_inc(*own.up())
            e.wait_ge(*own.done())


NORM_AT = 4


def load_sum(k, e, v, a, b, loaded, own):
    e.wait_ge(*loaded)
    v.tensor_tensor(a, a, b, ALU.add).then_inc(*own.up())
    e.wait_ge(*own.done())


def scan_weights(k, fp, gates, dram, ccol):
    nc = k.nc
    with Stage(k, "weights") as st:
        a0, a1 = st.sb("a0", [D, HID]), st.sb("a1", [D, HID])
        ones, zero, one = st.sb("ones", [C, C]), st.sb("zero", [C, C]), st.sb("one", [1, 1])
        qk, gt = st.sb("qk", [C, 2, D]), st.sb("gt", [C, GATES])
        qkt = st.sb("qkt", [D, 2, C])
        diag, own_g = st.sb("diag", [C, 2, C]), st.sb("own_g", [C, C])
        m2, oma, u, cr = st.sb("m2", [C, C]), st.sb("oma", [C, C]), st.sb("u", [C, C + 1]), st.sb("cr", [C, C + 1])
        cc, uq, w1, wr = st.sb("cc", [C, 2]), st.sb("uq", [C, C]), st.sb("w1", [C, C]), st.sb("wr", [C, 2, C])
        kq = st.sb("kq", [C, 2, HID])
        pt, pb, pg = st.ps("pt", [D, 2, C]), st.ps("pb", [C, 2, C]), st.ps("pg", [C, 2, C])
        pa, pc, pw = st.ps("pa", [C, 2, HID]), st.ps("pc", [C, 2]), st.ps("pw", [C, 2, C])
        loaded, const = st.sem("weights_loaded"), st.sem("constants")
        own = st.steps("vector_steps")
        xc, trd, trk, dg = st.sig("qk_copied", 1), st.sig("qk_transposed", 1), st.sig("qk_kept", 1), st.sig("diagonals", 1)
        bd, sd, gd, wd = st.sig("rows_spread", 1), st.sig("scanned", 1), st.sig("grams_done", 1), st.sig("weighted", 4)
        cd, cck, wtd, wtk = st.sig("c_turned", 1), st.sig("c_kept", 2), st.sig("weights_turned", 1), st.sig("weights_kept", 1)
        kak, stored = st.sig("first_terms_kept", 2), st.sig("stored", 7, 16)
        vdone = st.sem("v_stored")
        block = st.block()

        @block.sync
        def _(e):
            e.dma_start(a0[:, :], k.ins["t_w0"]).then_inc(loaded, 16)
            e.dma_start(a1[:, :], k.ins["t_p0"]).then_inc(loaded, 16)
            e.dma_start(dram["v"].rearrange("b t d -> t b d"), fp[:, :, 2 * D:3 * D]).then_inc(vdone, 16)
            stored.seed(e)
            with e.Fori(0, NB) as i:
                def row(t):
                    return t[bass.ds(i, 1)]
                k.wait("sync", e, *kak.now(i))
                e.dma_start(row(dram["ka"]).rearrange("o t h -> (o t) h"), kq[:, 0, :]).then_inc(*stored.up())
                e.dma_start(row(dram["qa"]).rearrange("o t h -> (o t) h"), kq[:, 1, :]).then_inc(*stored.up())
                k.wait("sync", e, *wtk.now(i))
                e.dma_start(row(dram["w"]).rearrange("o t h -> (o t) h"), wr[:, :, :].rearrange("p a s -> p (a s)")).then_inc(*stored.up())
                e.dma_start(row(dram["uq"])[:, :, 0, :].rearrange("o s t -> (o s) t"), uq[:, :]).then_inc(*stored.up())
                e.dma_start(row(dram["uq"])[:, :, 1, :].rearrange("o s t -> (o s) t"), u[:, 1:C + 1]).then_inc(*stored.up())
                e.dma_start(row(dram["c"]), cr[0:1, :]).then_inc(*stored.up())
                e.dma_start(row(dram["w1t"]).rearrange("o s t -> (o s) t"), w1[:, :]).then_inc(*stored.up())
            e.wait_ge(*stored.now(NB - 1))
            e.wait_ge(vdone, 16)

        @block.gpsimd
        def _(e):
            e.memset(ones[:, :], 1.0).then_inc(const, 1)
            e.memset(zero[:, :], 0.0).then_inc(const, 1)
            e.memset(one[:, :], 1.0).then_inc(const, 1)
            e.memset(u[:, 0:1], 0.0).then_inc(const, 1)
            e.memset(cr[:, 0:1], 1.0).then_inc(const, 1)

        @block.vector
        def _(e):
            v = nc.vector
            for s in (xc, dg, sd, wd, cck):
                s.seed(e)
            load_sum(k, e, v, a0[:, :], a1[:, :], (loaded, 32), own)
            e.sem_inc(const, 1)
            e.wait_ge(const, 6)
            first = own.n
            with e.Fori(0, NB) as i:
                own.n = first
                own.turn(i, 4)
                k.wait("vector", e, *bd.prev(i))
                v.tensor_copy(gt[:, :], gates[:, bass.ds(i, 1), :].rearrange("p o g -> p (o g)")).then_inc(*own.up())
                v.tensor_copy(qk[:, :, :], fp[:, bass.ds(i, 1), 0:2 * D].rearrange("p o (a d) -> p (o a) d", a=2)).then_inc(*xc.up())
                k.wait("vector", e, *own.done())
                v.tensor_scalar(own_g[:, :], k.ident[:, :], gt[:, 1:2], -2.0, ALU.mult, ALU.mult).then_inc(*own.up())
                v.tensor_scalar(diag[:, 0, :], k.ident[:, :], gt[:, 2:3], None, ALU.mult).then_inc(*own.up())
                v.tensor_scalar(diag[:, 1, :], k.ident[:, :], gt[:, 0:1], None, ALU.mult).then_inc(*dg.up())
                k.wait("vector", e, *own.done())
                k.wait("vector", e, *bd.now(i))
                v.tensor_scalar(oma[:, :], pb[:, 1, :], -1.0, 1.0, ALU.mult, ALU.add).then_inc(*own.up())
                v.tensor_tensor_scan(m2[:, :], pb[:, 0, :], own_g[:, :], 0.0, ALU.mult, ALU.add).then_inc(*sd.up())
                k.wait("vector", e, *own.done())
                k.wait("vector", e, *sd.now(i))
                k.wait("vector", e, *stored.prev(i))
                v.tensor_tensor_scan(u[:, 1:C + 1], oma[:, :], m2[:, :], 0.0, ALU.mult, ALU.add).then_inc(*wd.up())
                v.tensor_tensor_scan(cr[:, 1:C + 1], oma[:, :], zero[:, :], 1.0, ALU.mult, ALU.add).then_inc(*wd.up())
                k.wait("vector", e, *wd.now(i, 1))
                k.wait("vector", e, *gd.now(i))
                v.tensor_tensor(uq[:, :], pg[:, 0, :], u[:, 1:C + 1], ALU.mult).then_inc(*wd.up())
                v.tensor_tensor(w1[:, :], pg[:, 1, :], u[:, 0:C], ALU.mult).then_inc(*wd.up())
                k.wait("vector", e, *cd.now(i))
                k.wait("vector", e, *kak.prev(i))
                v.tensor_copy(cc[:, :], pc[:, :]).then_inc(*cck.up())
                v.tensor_copy(ccol[:, bass.ds(i, 1)], pc[:, 1:2]).then_inc(*cck.up())
                own.end()
            e.wait_ge(*cck.now(NB - 1))

        @block.scalar
        def _(e):
            for s in (trk, wtk, kak):
                s.seed(e)
            with e.Fori(0, NB) as i:
                k.wait("scalar", e, *trd.now(i))
                k.wait("scalar", e, *gd.prev(i))
                e.activation(qkt[:, :, :], pt[:, :, :], ACT.Copy).then_inc(*trk.up())
                k.wait("scalar", e, *cck.now(i))
                k.wait("scalar", e, *stored.prev(i))
                for a in range(2):
                    e.activation(kq[:, a, :], pa[:, a, :], ACT.Copy, scale=cc[:, a:a + 1]).then_inc(*kak.up())
                k.wait("scalar", e, *wtd.now(i))
                e.activation(wr[:, :, :], pw[:, :, :], ACT.Copy).then_inc(*wtk.up())

        @block.tensor
        def _(e):
            t = nc.tensor
            for s in (trd, bd, gd, cd, wtd):
                s.seed(e)
            e.wait_ge(const, 6)
            with e.Fori(0, NB) as i:
                k.wait("tensor", e, *xc.now(i))
                k.wait("tensor", e, *trk.prev(i))
                for a in range(2):
                    m = t.transpose(pt[:, a, :], qk[:, a, :], k.ident[:, :])
                m.then_inc(*trd.up())
                k.wait("tensor", e, *dg.now(i))
                k.wait("tensor", e, *sd.prev(i))
                t.matmul(pb[:, :, :], ones[:, :], diag[:, :, :], start=True, stop=True).then_inc(*bd.up())
                k.wait("tensor", e, *trk.now(i))
                k.wait("tensor", e, *wd.prev(i))
                k.wait("tensor", e, *kak.prev(i))
                t.matmul(pa[:, 0, :], qkt[:, 1, :], a0[:, :], start=True, stop=True)
                t.matmul(pa[:, 1, :], qkt[:, 0, :], a0[:, :], start=True, stop=True)
                t.matmul(pg[:, :, :], qkt[:, 1, :], qkt[:, :, :], start=True, stop=True).then_inc(*gd.up())
                k.wait("tensor", e, *wd.now(i, 1))
                k.wait("tensor", e, *cck.prev(i))
                t.matmul(pc[:, 0:1], cr[0:1, 0:C], one[:, :], start=True, stop=True)
                t.matmul(pc[:, 1:2], cr[0:1, 1:C + 1], one[:, :], start=True, stop=True).then_inc(*cd.up())
                k.wait("tensor", e, *wd.now(i))
                k.wait("tensor", e, *wtk.prev(i))
                t.transpose(pw[:, 0, :], w1[:, :], k.ident[:, :])
                t.transpose(pw[:, 1, :], u[:, 0:C], k.ident[:, :]).then_inc(*wtd.up())


COST = {"v": 2.2, "g": 4.4, "s": 4.2, "sum_v": 2.2, "sum_t": 3.5, "sum_s": 5.5}


def share_dots(blocks):
    best = None
    for made in range(1, blocks + 1):
        for sums in range(0, made):
            t = max(COST["v"] * made + COST["sum_v"] * (blocks - sums), COST["g"] * (blocks - made) + COST["sum_v"],
                    COST["v"] + COST["sum_s"] * sums)
            if best is None or t < best[0]:
                best = t, made, sums
    return best[1:]


def share_mix(blocks):
    best = None
    for s in range(0, blocks):
        for g in range(0, blocks - s):
            v = blocks - s - g
            if v < 1:
                continue
            made = sorted([(COST["v"] * (n + 1), "v") for n in range(v)] + [(COST["s"] * (n + 1), "s") for n in range(s)]
                          + [(COST["g"] * (n + 1), "g") for n in range(g)])
            tv, tt, plan = COST["v"] * v, 0.0, []
            for ready, who in made:
                a, b = max(tv, ready) + COST["sum_v"], max(tt, ready) + COST["sum_t"]
                if b <= a:
                    tt = b
                    plan.append((who, "t"))
                else:
                    tv = a
                    plan.append((who, "v"))
            if best is None or max(tv, tt) < best[0]:
                best = max(tv, tt), plan
    return best[1]


class ChunkSignal:

    def __init__(self, st, name, per):
        self.sem = st.sem(name)
        self.base, total = [], 0
        for c in range(C // SC):
            self.base.append(total)
            total += SC * per(c)
        self.per = per

    def up(self):
        return self.sem, 1

    def now(self, c, it, j):
        assert 0 <= j < self.per(c), (c, j)
        return self.sem, it * self.per(c) + (self.base[c] + j + 1)


def scan(k, dram):
    nc = k.nc
    HH, DD, NC = HID // 2, D // 2, C // SC
    BG = 16
    DOTS = [share_dots(c + 1) for c in range(NC)]
    MIX = [share_mix(c + 1) for c in range(NC)]
    THIN = [SC * (c + 1) - SC * ((c + 1) // 3) for c in range(NC)]
    made_by = lambda c, who: [b for b, (w, _) in enumerate(MIX[c]) if w == who]
    summed_by = lambda c, who: [b for b, (_, w) in enumerate(MIX[c]) if w == who]
    with Stage(k, "scan") as st:
        hh, ee = st.sb("hh", [128, C, HH]), st.sb("ee", [128, C, DD])
        gc = st.sb("gc", [128, SC, HH])
        wc, ka, vc = st.sb("wc", [128, SC, 2, C]), st.sb("ka", [128, SC, HH]), st.sb("vc", [128, SC, DD])
        cp = st.sb("cp", [128, C + 1])
        prod = st.sb("prod", [128, NC, SC * HH])
        part = st.sb("part", [128, NC, HH])
        acc, pre, sg, h, ds = [st.sb(n, [128, HH]) for n in ("acc", "pre", "sg", "h", "ds")]
        gr, w = st.sb("gr", [128, C]), st.sb("w", [128, C])
        er, eacc = st.sb("er", [128, DD]), st.sb("eacc", [128, DD])
        ht, et = st.sb("ht", [128, 128]), st.sb("et", [DD, 128])
        b0, c0 = st.sb("b0", [128, 2, D]), st.sb("c0", [DD, 2, HID])
        flat = prod[:, :, :].rearrange("p b n -> p (b n)")
        b1 = flat[:, 0:2 * D].rearrange("p (a d) -> p a d", a=2)
        c1 = flat[0:DD, 2 * D:2 * D + 2 * HID].rearrange("p (a h) -> p a h", a=2)
        old = [flat[:, a * 4096:(a + 1) * 4096].rearrange("p (b h) -> p b h", b=BG) for a in range(2)]
        oldw = [flat[:, 8192 + a * 256:8192 + (a + 1) * 256].rearrange("p (b t) -> p b t", b=BG) for a in range(2)]
        said = [flat[0:SC, 10240 + 2048 * a:10240 + 2048 * (a + 1)].rearrange("p (b h) -> p b h", b=8) for a in range(2)]
        olds = flat[:, 14336:14336 + SC * HH].rearrange("p (t h) -> p t h", t=SC)
        pair = st.sb("pair", [128, 128])
        pht, ppb = st.ps("pht", [128, 128]), st.ps("ppb", [128, DD])
        pgr, pmx = st.ps("pgr", [128, 2, C]), st.ps("pmx", [128, 512])
        pet, pdb = st.ps("pet", [DD, 128]), st.ps("pdb", [128, HH])
        pold = st.ps("pold", [SC, 2, 2, HID])
        loaded, cleared, const = st.sem("weights_loaded"), st.sem("cleared"), st.sem("constants")
        chunk, over, kept = st.sem("chunk_loaded"), st.sem("chunk_over"), st.sem("histories_stored")
        gstored = st.sem("gradients_stored")
        oldl, oldd = [st.sem(f"older_loaded{a}") for a in range(2)], st.sem("older_products")
        olde, olds_ld = st.sem("older_kept"), st.sem("older_reloaded")
        olds_st = [st.sem(f"older_stored{a}") for a in range(2)]
        own = st.steps("vector_steps")
        pr, sgd, hd = st.sig("pre_done", 1), st.sig("sigmoid_done", 1), st.sig("hidden_done", 1)
        htd, htk, pbd = st.sig("hidden_turned", 1), st.sig("hidden_kept", 1), st.sig("first_prediction_done", 1)
        grd, prd = st.sig("gram_halves", 2), st.sig("gram_sums", 2)
        wd = st.sig("coefficients_done", 2)
        ed, etd, etk, dbd = st.sig("error_done", 1), st.sig("error_turned", 1), st.sig("error_kept", 1), st.sig("first_backward_done", 1)
        gdone = st.sig("gradient_done", 1)
        mxd = st.sig("rows_summed", 1)
        adots = st.sig("scalar_dots_done", 1)
        vdot = ChunkSignal(st, "vector_dot_products", lambda c: max(DOTS[c][1], 1))
        vmix = ChunkSignal(st, "vector_mix_products", lambda c: len(made_by(c, "v")))
        smix = ChunkSignal(st, "scalar_mix_products", lambda c: max(len(made_by(c, "s")), 1))
        gdot = ChunkSignal(st, "gpsimd_dot_products", lambda c: max(c + 1 - DOTS[c][0], 1))
        gmix = ChunkSignal(st, "gpsimd_mix_products", lambda c: max(len(made_by(c, "g")), 1))
        gthin = ChunkSignal(st, "gpsimd_thin_products", lambda c: 2)
        block = st.block()
        blk = lambda b: prod[:, b, :].rearrange("p (s w) -> p s w", s=SC)
        hist = lambda b: hh[:, b * SC:(b + 1) * SC, :]
        coef = lambda b: spread(w[:, b * SC:(b + 1) * SC], 2, HH)
        thin = lambda a, b: flat[:, a * DD:b * DD].rearrange("p (s w) -> p s w", s=b - a)
        one = lambda t, j: t[:, bass.ds(j, 1), :].rearrange("p o w -> p (o w)")

        def own_steps(c):
            made, sums = DOTS[c]
            mine, rest = len(summed_by(c, "v")), bool(summed_by(c, "t"))
            return 13 + made - sums + c - sums + mine + rest + (mine + rest > 1)

        def store_old(e, c, q):
            for a in range(2):
                g = ((c - 1) * (NB // BG) + q) * 2 + a
                e.wait_ge(olde, 4 * (g + 1))
                b = q * BG + 8 * a
                e.dma_start(dram["po"][b:b + 8, :, :].rearrange("b t h -> t b h"), said[a][:, :, :]).then_inc(olds_st[a], 16)

        def gap(e, c, *missing):
            for s, n in missing:
                if n:
                    e.sem_inc(s.sem, n * SC)

        def older(e, c):
            for q in range(NB // BG):
                for j in range(8):
                    g = ((c - 1) * (NB // BG) + q) * 8 + j
                    e.wait_ge(oldd, g + 1)
                    if g >= 8 and j % 4 == 0:
                        e.wait_ge(olds_st[j // 4], 16 * (g // 8))
                    e.activation(said[j // 4][:, 2 * (j % 4):2 * (j % 4) + 2, :], pold[:, g % 2, :, :], ACT.Copy).then_inc(olde, 1)

        @block.sync
        def _(e):
            for t, n in ((b0, "t_w1"), (b1, "t_p1"), (c0, "t_w1t"), (c1, "t_p1t")):
                e.dma_start(t[:, :, :], k.ins[n]).then_inc(loaded, 16)
            for a in range(2):
                e.dma_start(cp[64 * a:64 * a + 64, :], dram["c"]).then_inc(loaded, 16)
            for c in range(NC + 1):
                s = slice(c * SC, (c + 1) * SC)
                if c:
                    e.wait_ge(over, c)
                    for a in range(2):
                        e.dma_start(dram["g"][:, (c - 1) * SC:c * SC, a * HH:(a + 1) * HH],
                                    gc[64 * a:64 * a + 64, :, :]).then_inc(gstored, 16)
                if c < NC:
                    for a in range(2):
                        r = slice(64 * a, 64 * a + 64)
                        e.dma_start(wc[r, :, :, :].rearrange("p t a s -> p t (a s)"), dram["w"][:, s, :]).then_inc(chunk, 16)
                        e.dma_start(ka[r, :, :], dram["ka"][:, s, a * HH:(a + 1) * HH]).then_inc(chunk, 16)
                        e.dma_start(vc[r, :, :], dram["v"][:, s, a * DD:(a + 1) * DD]).then_inc(chunk, 16)
                if 0 < c < NC:
                    n = c * SC
                    e.wait_ge(gstored, 32 * c)
                    for q in range(NB // BG):
                        g = (c - 1) * (NB // BG) + q
                        if q >= 2:
                            e.wait_ge(oldd, 8 * (g - 1))
                        b = slice(q * BG, (q + 1) * BG)
                        e.dma_start(old[q % 2][0:n, :, :], dram["g"][b, 0:n, :].rearrange("b s h -> s b h")).then_inc(oldl[q % 2], 16)
                        e.dma_start(oldw[q % 2][0:n, :, :], dram["w1t"][b, 0:n, s].rearrange("b s t -> s b t")).then_inc(oldl[q % 2], 16)
                        if q:
                            store_old(e, c, q - 1)
                    store_old(e, c, NB // BG - 1)
                    for a in range(2):
                        e.wait_ge(olds_st[a], 16 * (NB // BG) * c)
                    for a in range(2):
                        e.dma_start(olds[64 * a:64 * a + 64, :, :], dram["po"][:, :, a * HH:(a + 1) * HH]).then_inc(olds_ld, 16)
            for a in range(2):
                r = slice(64 * a, 64 * a + 64)
                e.dma_start(dram["h"][:, :, a * HH:(a + 1) * HH], hh[r, :, :]).then_inc(kept, 16)
                e.dma_start(dram["e"][:, :, a * DD:(a + 1) * DD], ee[r, :, :]).then_inc(kept, 16)
            e.wait_ge(kept, 64)
            e.wait_ge(gstored, 32 * NC)

        @block.gpsimd
        def _(e):
            e.memset(gc[:, :, :], 0.0).then_inc(cleared, 1)
            e.memset(ee[:, :, :], 0.0).then_inc(cleared, 1)
            e.memset(hh[:, :, :], 0.0).then_inc(cleared, 1)
            e.memset(gr[:, :], 0.0).then_inc(cleared, 1)
            e.wait_ge(cleared, 4)
            for c in range(NC):
                n, x = SC * (c + 1), THIN[c]
                busy = c + 1 > DOTS[c][0] or made_by(c, "g") or x < n
                if not busy:
                    gap(e, c, (gdot, 1), (gmix, 1), (gthin, 2))
                    continue
                with e.Fori(0, SC) as it:
                    i = it + c * SC
                    k.wait("gpsimd", e, *hd.now(i))
                    for j, b in enumerate(range(DOTS[c][0], c + 1)):
                        e.tensor_tensor(blk(b), hist(b), spread(h[:, :], 1, SC), ALU.mult).then_inc(*gdot.up())
                    if x < n:
                        k.wait("gpsimd", e, *wd.now(i, 0))
                        e.tensor_tensor(thin(x, n), ee[:, x:n, :], spread(w[:, x:n], 2, DD), ALU.mult).then_inc(*gthin.up())
                        k.wait("gpsimd", e, *ed.now(i))
                        e.tensor_tensor(thin(x, n), ee[:, x:n, :], spread(er[:, :], 1, n - x), ALU.mult).then_inc(*gthin.up())
                    k.wait("gpsimd", e, *wd.now(i, 1))
                    for b in made_by(c, "g"):
                        e.tensor_tensor(blk(b), hist(b), coef(b), ALU.mult).then_inc(*gmix.up())
                gap(e, c, (gdot, max(c + 1 - DOTS[c][0], 1) - (c + 1 - DOTS[c][0])),
                    (gmix, max(len(made_by(c, "g")), 1) - len(made_by(c, "g"))), (gthin, 0 if x < n else 2))

        @block.vector
        def _(e):
            v = nc.vector
            for s in (pr, hd, grd, wd, ed, gdone):
                s.seed(e)

            def settle():
                k.wait("vector", e, *own.done())
            for a in range(2):
                for b in range(2):
                    v.tensor_copy(pair[64 * a:64 * a + 64, 64 * b:64 * b + 64],
                                  k.ident[64 * a:64 * a + 64, 64 * a:64 * a + 64]).then_inc(const, 1)
            e.wait_ge(loaded, 96)
            v.tensor_tensor(b0[:, :, :], b0[:, :, :], b1, ALU.add).then_inc(const, 1)
            v.tensor_tensor(c0[:, :, :], c0[:, :, :], c1, ALU.add).then_inc(const, 1)
            e.wait_ge(const, 6)
            e.wait_ge(cleared, 4)

            def dots(c, it, i):
                made, sums = DOTS[c]
                for b in range(made):
                    v.tensor_tensor(blk(b), hist(b), spread(h[:, :], 1, SC), ALU.mult).then_inc(
                        *(vdot.up() if b < sums else own.up()))
                settle()
                for b in range(sums, c + 1):
                    if b >= made:
                        k.wait("vector", e, *gdot.now(c, it, b - made))
                    v.tensor_reduce(gr[:, b * SC:(b + 1) * SC], blk(b), axis=AX.X, op=ALU.add).then_inc(
                        *(grd.up() if b == c else own.up()))

            def mix(c, it, i):
                for b in made_by(c, "v"):
                    v.tensor_tensor(blk(b), hist(b), coef(b), ALU.mult).then_inc(*vmix.up())
                sums, first = summed_by(c, "v"), True
                rest = summed_by(c, "t")
                for j, b in enumerate(sums):
                    who = MIX[c][b][0]
                    s = {"v": vmix, "s": smix, "g": gmix}[who]
                    k.wait("vector", e, *s.now(c, it, made_by(c, who).index(b)))
                    out = acc[:, :] if len(sums) == 1 and not rest else part[:, j, :]
                    v.tensor_reduce(out, blk(b).rearrange("p s w -> p w s"), axis=AX.X, op=ALU.add).then_inc(*own.up())
                if rest:
                    k.wait("vector", e, *mxd.now(i))
                    out = part[:, len(sums), :] if sums else acc[:, :]
                    v.tensor_reduce(out, pmx[:, :].rearrange("p (j w) -> p w j", j=4), axis=AX.X, op=ALU.add).then_inc(*own.up())
                pieces = len(sums) + bool(rest)
                settle()
                if pieces > 1:
                    v.tensor_reduce(acc[:, :], part[:, 0:pieces, :].rearrange("p b w -> p w b"), axis=AX.X, op=ALU.add).then_inc(*own.up())
                    settle()

            for c in range(NC):
                n, x = SC * (c + 1), THIN[c]
                e.wait_ge(chunk, 96 * (c + 1))
                if c:
                    own.leave(SC)
                    e.wait_ge(olds_ld, 32 * c)
                    v.tensor_tensor(ka[:, :, :], ka[:, :, :], olds, ALU.add).then_inc(*own.up())
                    settle()
                    e.wait_ge(gstored, 32 * c)
                    v.memset(gc[:, :, :], 0.0).then_inc(*own.up())
                    settle()
                first = own.n
                with e.Fori(0, SC) as it:
                    i = it + c * SC
                    own.n = first
                    own.turn(it, own_steps(c))
                    row = lambda a, m0, m1: wc[:, bass.ds(it, 1), a, m0:m1].rearrange("p o s -> p (o s)")
                    v.tensor_tensor(blk(0), gc[:, :, :], spread(row(0, n - SC, n), 2, HH), ALU.mult).then_inc(*own.up())
                    settle()
                    v.tensor_reduce(acc[:, :], blk(0).rearrange("p s w -> p w s"), axis=AX.X, op=ALU.add).then_inc(*own.up())
                    settle()
                    v.tensor_tensor(pre[:, :], acc[:, :], one(ka, it), ALU.add).then_inc(*pr.up())
                    k.wait("vector", e, *sgd.now(i))
                    k.wait("vector", e, *pr.now(i))
                    v.tensor_tensor(h[:, :], pre[:, :], sg[:, :], ALU.mult).then_inc(*hd.up())
                    k.wait("vector", e, *hd.now(i))
                    dots(c, it, i)
                    v.tensor_tensor(ds[:, :], h[:, :], sg[:, :], ALU.mult).then_inc(*own.up())
                    settle()
                    v.tensor_tensor(ds[:, :], h[:, :], ds[:, :], ALU.subtract).then_inc(*own.up())
                    settle()
                    v.tensor_tensor(ds[:, :], ds[:, :], sg[:, :], ALU.add).then_inc(*own.up())
                    k.wait("vector", e, *prd.now(i, 0))
                    v.tensor_tensor(w[:, 0:n], pgr[:, 0, 0:n], row(1, 0, n), ALU.mult).then_inc(*wd.up())
                    k.wait("vector", e, *wd.now(i, 0))
                    v.tensor_tensor(thin(0, x), ee[:, 0:x, :], spread(w[:, 0:x], 2, DD), ALU.mult).then_inc(*own.up())
                    settle()
                    if x < n:
                        k.wait("vector", e, *gthin.now(c, it, 0))
                    v.tensor_reduce(eacc[:, :], thin(0, n).rearrange("p s w -> p w s"), axis=AX.X, op=ALU.add).then_inc(*own.up())
                    settle()
                    k.wait("vector", e, *pbd.now(i))
                    v.scalar_tensor_tensor(eacc[:, :], ppb[:, :], cp[:, bass.ds(i, 1)], eacc[:, :], ALU.mult, ALU.add).then_inc(*own.up())
                    settle()
                    v.tensor_tensor(eacc[:, :], eacc[:, :], one(vc, it), ALU.subtract).then_inc(*own.up())
                    settle()
                    v.tensor_scalar(er[:, :], eacc[:, :], 2.0 / D, None, ALU.mult).then_inc(*ed.up())
                    k.wait("vector", e, *ed.now(i))
                    v.tensor_tensor(thin(0, x), ee[:, 0:x, :], spread(er[:, :], 1, x), ALU.mult).then_inc(*own.up())
                    settle()
                    if x < n:
                        k.wait("vector", e, *gthin.now(c, it, 1))
                    v.tensor_reduce(gr[:, 0:n], thin(0, n), axis=AX.X, op=ALU.add).then_inc(*grd.up())
                    k.wait("vector", e, *prd.now(i, 1))
                    v.tensor_tensor(w[:, 0:n], pgr[:, 1, 0:n], row(1, 0, n), ALU.mult).then_inc(*wd.up())
                    k.wait("vector", e, *wd.now(i, 1))
                    mix(c, it, i)
                    k.wait("vector", e, *dbd.now(i))
                    v.scalar_tensor_tensor(acc[:, :], pdb[:, :], cp[:, bass.ds(i, 1)], acc[:, :], ALU.mult, ALU.add).then_inc(*own.up())
                    settle()
                    v.tensor_copy(one(hh, i), h[:, :]).then_inc(*own.up())
                    v.tensor_copy(one(ee, i), er[:, :]).then_inc(*own.up())
                    v.tensor_tensor(one(gc, it), acc[:, :], ds[:, :], ALU.mult).then_inc(*gdone.up())
                    k.wait("vector", e, *gdone.now(i))
                    own.end()
                gap(e, c, (vdot, max(DOTS[c][1], 1) - DOTS[c][1]))
                e.sem_inc(over, 1)

        @block.scalar
        def _(e):
            for s in (sgd, htk, etk, adots):
                s.seed(e)
            for c in range(NC):
                if c:
                    older(e, c)
                made, sums = DOTS[c]
                with e.Fori(0, SC) as it:
                    i = it + c * SC
                    k.wait("scalar", e, *pr.now(i))
                    e.activation(sg[:, :], pre[:, :], ACT.Sigmoid).then_inc(*sgd.up())
                    k.wait("scalar", e, *htd.now(i))
                    e.activation(ht[:, :], pht[:, :], ACT.Copy).then_inc(*htk.up())
                    for b in range(sums):
                        k.wait("scalar", e, *vdot.now(c, it, b))
                        for s in range(SC):
                            m = e.activation(blk(b)[:, s, :], blk(b)[:, s, :], ACT.Copy,
                                             accum_out=gr[:, b * SC + s:b * SC + s + 1])
                            if s == SC - 1 and b == sums - 1:
                                m.then_inc(*adots.up())
                    if not sums:
                        e.sem_inc(adots.sem, 1)
                    k.wait("scalar", e, *etd.now(i))
                    e.activation(et[:, :], pet[:, :], ACT.Copy).then_inc(*etk.up())
                    if made_by(c, "s"):
                        k.wait("scalar", e, *wd.now(i, 1))
                    for b in made_by(c, "s"):
                        for s in range(SC):
                            m = e.activation(blk(b)[:, s, :], hist(b)[:, s, :], ACT.Copy, scale=w[:, b * SC + s:b * SC + s + 1])
                        m.then_inc(*smix.up())
                gap(e, c, (smix, max(len(made_by(c, "s")), 1) - len(made_by(c, "s"))))

        @block.tensor
        def _(e):
            t = nc.tensor
            for s in (htd, pbd, prd, etd, dbd, mxd):
                s.seed(e)
            e.wait_ge(const, 6)
            for c in range(NC):
                for q in range(NB // BG if c else 0):
                    g = (c - 1) * (NB // BG) + q
                    e.wait_ge(oldl[q % 2], 32 * (g // 2 + 1))
                    for j in range(8):
                        if g * 8 + j >= 2:
                            e.wait_ge(olde, g * 8 + j - 1)
                        for b in range(2):
                            m = t.matmul(pold[:, (g * 8 + j) % 2, b, :], oldw[q % 2][0:c * SC, 2 * j + b, :],
                                         old[q % 2][0:c * SC, 2 * j + b, :], start=True, stop=True)
                        m.then_inc(oldd, 1)
                made, sums = DOTS[c]
                with e.Fori(0, SC) as it:
                    i = it + c * SC
                    k.wait("tensor", e, *hd.now(i))
                    t.transpose(pht[:, :], h[:, :], k.ident[:, :]).then_inc(*htd.up())
                    k.wait("tensor", e, *htk.now(i))
                    for to in range(2):
                        for a in range(2):
                            m = t.matmul(ppb[64 * to:64 * to + 64, :], ht[:, 64 * a:64 * a + 64],
                                         b0[:, a, DD * to:DD * to + DD], start=a == 0, stop=a == 1)
                    m.then_inc(*pbd.up())
                    k.wait("tensor", e, *grd.now(i, 0))
                    k.wait("tensor", e, *adots.now(i))
                    t.matmul(pgr[:, 0, :], pair[:, :], gr[:, :], start=True, stop=True).then_inc(*prd.up())
                    k.wait("tensor", e, *ed.now(i))
                    t.transpose(pet[:, :], er[:, :], k.ident[:, :]).then_inc(*etd.up())
                    k.wait("tensor", e, *etk.now(i))
                    for to in range(2):
                        for a in range(2):
                            m = t.matmul(pdb[64 * to:64 * to + 64, :], et[:, 64 * a:64 * a + 64],
                                         c0[:, a, HH * to:HH * to + HH], start=a == 0, stop=a == 1)
                    m.then_inc(*dbd.up())
                    k.wait("tensor", e, *grd.now(i, 1))
                    t.matmul(pgr[:, 1, :], pair[:, :], gr[:, :], start=True, stop=True).then_inc(*prd.up())
                    rest = summed_by(c, "t")
                    for b in rest:
                        who = MIX[c][b][0]
                        s = {"v": vmix, "s": smix, "g": gmix}[who]
                        k.wait("tensor", e, *s.now(c, it, made_by(c, who).index(b)))
                        for j in range(4):
                            m = t.matmul(pmx[:, :], k.ident[:, :], prod[:, b, j * 512:(j + 1) * 512],
                                         start=b == rest[0] and j == 0, stop=b == rest[-1] and j == 3)
                    if rest:
                        m.then_inc(*mxd.up())
                    else:
                        e.sem_inc(mxd.sem, 1)


def scan_outputs(k, dram, ccol):
    nc = k.nc
    PAIR = range(2)
    with Stage(k, "answers") as st:
        two = lambda name, shape: [st.sb(f"{name}{a}", shape) for a in PAIR]
        gb, hb, eb = two("gb", [C, HID]), two("hb", [C, HID]), two("eb", [C, D])
        uq, qa = two("uq", [C, 2, C]), two("qa", [C, HID])
        pre, hq, tt, w = two("pre", [C, HID]), two("hq", [C, HID]), two("tt", [128, 4, C]), two("w", [C, C])
        y = two("y", [C, D])
        b0, b1 = st.sb("b0", [128, 2, D]), st.sb("b1", [128, 2, D])
        pp, ptt, pg, po = [[st.ps(f"{n}{a}", [C, 512]) for a in PAIR] for n in ("pp", "ptt", "pg", "po")]
        loaded = st.sem("weights_loaded")
        own = st.steps("vector_steps")
        ld = [st.sig(f"batch_loaded{a}", 5, 16) for a in PAIR]
        ppd, prd, hqd = st.sig("history_term", 2), st.sig("pre_done", 2), st.sig("hidden_done", 2)
        trd, trk, gd, wd = st.sig("turned", 2), st.sig("turned_kept", 2), st.sig("gram_done", 2), st.sig("weighted", 2)
        od, rd = st.sig("out_done", 2), st.sig("resid_done", 2)
        block = st.block()

        @block.sync
        def _(e):
            for t, n in ((b0, "t_w1"), (b1, "t_p1")):
                e.dma_start(t[:], k.ins[n]).then_inc(loaded, 16)
            for a in PAIR:
                ld[a].seed(e)
            with e.Fori(0, NB // 2) as i:
                for a in PAIR:
                    batch = bass.ds(2 * i + a, 1)
                    k.wait("sync", e, *rd.prev(i, a))
                    for t, n in ((gb, "g"), (hb, "h"), (eb, "e"), (qa, "qa")):
                        e.dma_start(t[a][:, :], dram[n][batch, :, :].rearrange("o s w -> (o s) w")).then_inc(*ld[a].up())
                    e.dma_start(uq[a][:, :, :], dram["uq"][batch, :, :, :].rearrange("o s a t -> (o s) a t")).then_inc(*ld[a].up())

        @block.tensor
        def _(e):
            t = nc.tensor
            for s in (ppd, trd, gd, od):
                s.seed(e)
            e.wait_ge(own.sem, 1)
            with e.Fori(0, NB // 2) as i:
                for a in PAIR:
                    k.wait("tensor", e, *ld[a].now(i))
                    t.matmul(pp[a][:, 0:HID], uq[a][:, 0, :], gb[a][:, :], start=True, stop=True).then_inc(*ppd.up())
                for a in PAIR:
                    k.wait("tensor", e, *hqd.now(i, a))
                    for n, x in enumerate((hb, hb, hq, hq)):
                        m = t.transpose(ptt[a][:, n * C:(n + 1) * C], x[a][:, (n % 2) * 128:(n % 2 + 1) * 128], k.ident[:, :])
                    m.then_inc(*trd.up())
                for a in PAIR:
                    k.wait("tensor", e, *trk.now(i, a))
                    for n in range(2):
                        m = t.matmul(pg[a][:, 0:C], tt[a][:, n, :], tt[a][:, 2 + n, :], start=n == 0, stop=n == 1)
                    m.then_inc(*gd.up())
                    k.wait("tensor", e, *rd.prev(i, a))
                    for n in range(2):
                        t.matmul(po[a][:, D:2 * D], tt[a][:, 2 + n, :], b0[:, n, :], start=n == 0, stop=n == 1)
                for a in PAIR:
                    k.wait("tensor", e, *wd.now(i, a))
                    t.matmul(po[a][:, 0:D], w[a][:, :], eb[a][:, :], start=True, stop=True).then_inc(*od.up())

        @block.scalar
        def _(e):
            for s in (hqd, trk):
                s.seed(e)
            with e.Fori(0, NB // 2) as i:
                for a in PAIR:
                    k.wait("scalar", e, *prd.now(i, a))
                    e.activation(hq[a][:, :], pre[a][:, :], ACT.Silu).then_inc(*hqd.up())
                for a in PAIR:
                    k.wait("scalar", e, *trd.now(i, a))
                    e.activation(tt[a][:, :, :], ptt[a][:, :].rearrange("p (n c) -> p n c", n=4), ACT.Copy).then_inc(*trk.up())

        @block.vector
        def _(e):
            v = nc.vector
            for s in (prd, wd, rd):
                s.seed(e)
            load_sum(k, e, v, b0[:, :, :], b1[:, :, :], (loaded, 32), own)
            first = own.n
            with e.Fori(0, NB // 2) as i:
                own.n = first
                own.turn(i, 2)
                for a in PAIR:
                    k.wait("vector", e, *ppd.now(i, a))
                    v.tensor_tensor(pre[a][:, :], pp[a][:, 0:HID], qa[a][:, :], ALU.add).then_inc(*prd.up())
                for a in PAIR:
                    k.wait("vector", e, *gd.now(i, a))
                    v.tensor_tensor(w[a][:, :], pg[a][:, 0:C], uq[a][:, 1, :], ALU.mult).then_inc(*wd.up())
                for a in PAIR:
                    k.wait("vector", e, *od.now(i, a))
                    r = k.resid[:, bass.ds((2 * i + a) * D, D)]
                    v.scalar_tensor_tensor(y[a][:, :], po[a][:, D:2 * D], ccol[:, bass.ds(2 * i + a, 1)], r,
                                           ALU.mult, ALU.add).then_inc(*own.up())
                    k.wait("vector", e, *own.done())
                    v.tensor_tensor(r, y[a][:, :], po[a][:, 0:D], ALU.add).then_inc(*rd.up())
                own.end()


def experts(k, xt):
    nc = k.nc
    G, NG = 4, NB // 4
    with Stage(k, "experts") as st:
        wr, w1, w2 = st.sb("wr", [D + 1, EXPERTS]), st.sb("w1", [D + 1, EXPERTS, DFF]), st.sb("w2", [DFF, EXPERTS, D])
        b2 = st.sb("b2", [C, EXPERTS, D])
        iot = st.sb("iot", [C, EXPERTS])
        xs = st.sb("xs", [D + 1, G * C])
        lg, top, place, pf = st.sb("lg", [C, G, 8]), st.sb("top", [C, G, 8]), st.sb("place", [C, G, 8], U32), st.sb("pf", [C, G, 8])
        gap, e2, share = st.sb("gap", [C, G]), st.sb("e2", [C, G]), st.sb("share", [C, G, 2])
        one_hot, wf = st.sb("one_hot", [C, G, 2, 8]), st.sb("wf", [C, G, 8])
        hb = st.sb("hb", [DFF, 2, G * C])
        prod, y = st.sb("prod", [C, 2, EXPERTS, D]), st.sb("y", [C, G, D])
        py, ph, pl = st.ps("py", [C, G, EXPERTS * D]), st.ps("ph", [DFF, 2, G * C]), st.ps("pl", [C, G, 8])
        loaded, const = st.sem("weights_loaded"), st.sem("constants")
        own = st.steps("vector_steps")
        xc, ld, gp, ex2 = st.sig("x_copied", 1), st.sig("logits_done", 1), st.sig("gap_done", 1), st.sig("gap_exp", 1)
        lk = st.sig("logits_kept", 1)
        hd, gl, rd = st.sig("hidden_done", EXPERTS), st.sig("gelu_done", EXPERTS), st.sig("resid_done", 1)
        yu = st.sig("answers_used", G)
        used = st.sig("hidden_used", EXPERTS)
        block = st.block()

        @block.sync
        def _(e):
            for t, n in ((wr, "m_wr"), (w1, "m_w1"), (w2, "m_w2")):
                e.dma_start(t[:], k.ins[n]).then_inc(loaded, 16)
            e.dma_start(b2[:, :, :].rearrange("p x d -> p (x d)"), k.ins["m_b2"].to_broadcast([C, EXPERTS * D])).then_inc(loaded, 16)

        @block.gpsimd
        def _(e):
            e.iota(iot[:, :], [[1, EXPERTS]], base=0, channel_multiplier=0,
                   allow_small_or_imprecise_dtypes=True).then_inc(const, 1)

        @block.tensor
        def _(e):
            t = nc.tensor
            for s in (ld, hd, used):
                s.seed(e)
            e.wait_ge(loaded, 64)
            e.wait_ge(const, 1)
            with e.Fori(0, NG) as i:
                def hidden(x):
                    k.wait("tensor", e, *(gl.now(i, x - 2) if x >= 2 else gl.prev(i, x + EXPERTS - 2)))
                    t.matmul(ph[:, x % 2, :], w1[:, x, :], xt[:, bass.ds(i * G * C, G * C)], start=True, stop=True).then_inc(*hd.up())
                hidden(0)
                hidden(1)
                k.wait("tensor", e, *xc.now(i))
                k.wait("tensor", e, *lk.prev(i))
                for g in range(G):
                    m = t.matmul(pl[:, g, :], xs[:, g * C:(g + 1) * C], wr[:, :], start=True, stop=True)
                m.then_inc(*ld.up())
                for g in range(G):
                    k.wait("tensor", e, *yu.prev(i, g))
                for x in range(EXPERTS):
                    if 1 < x + 1 < EXPERTS:
                        hidden(x + 1)
                    k.wait("tensor", e, *gl.now(i, x))
                    for g in range(G):
                        m = t.matmul(py[:, g, x * D:(x + 1) * D], hb[:, x % 2, g * C:(g + 1) * C], w2[:, x, :],
                                     start=True, stop=True)
                    m.then_inc(*used.up())

        @block.scalar
        def _(e):
            for s in (ex2, gl):
                s.seed(e)
            with e.Fori(0, NG) as i:
                for x in range(EXPERTS):
                    k.wait("scalar", e, *hd.now(i, x))
                    k.wait("scalar", e, *(used.now(i, x - 2) if x >= 2 else used.prev(i, x + EXPERTS - 2)))
                    e.activation(hb[:, x % 2, :], ph[:, x % 2, :], ACT.Gelu).then_inc(*gl.up())
                    if x == EXPERTS // 2:
                        k.wait("scalar", e, *gp.now(i))
                        e.activation(e2[:, :], gap[:, :], ACT.Exp).then_inc(*ex2.up())

        @block.vector
        def _(e):
            v = nc.vector
            for s in (xc, lk, gp, yu, rd):
                s.seed(e)
            e.wait_ge(const, 1)
            e.wait_ge(loaded, 64)

            def settle():
                k.wait("vector", e, *own.done())
            with e.Fori(0, NG) as i:
                own.n = 0
                own.turn(i, PER_EXPERTS)
                k.wait("vector", e, *ld.prev(i))
                v.tensor_copy(xs[:, :], xt[:, bass.ds(i * G * C, G * C)]).then_inc(*xc.up())
                k.wait("vector", e, *ld.now(i))
                v.tensor_copy(lg[:, :, :], pl[:, :, :]).then_inc(*lk.up())
                k.wait("vector", e, *lk.now(i))
                for g in range(G):
                    v.max(top[:, g, :], lg[:, g, :]).then_inc(*own.up())
                settle()
                for g in range(G):
                    v.max_index(place[:, g, :], top[:, g, :], lg[:, g, :]).then_inc(*own.up())
                v.tensor_tensor(gap[:, :], top[:, :, 1], top[:, :, 0], ALU.subtract).then_inc(*gp.up())
                settle()
                v.tensor_copy(pf[:, :, :], place[:, :, :]).then_inc(*own.up())
                settle()
                v.tensor_tensor(one_hot[:, :, :, :], spread(pf[:, :, 0:2], 3, 8),
                                spread(spread(iot[:, :], 1, 2), 1, G), ALU.is_equal).then_inc(*own.up())
                k.wait("vector", e, *ex2.now(i))
                v.tensor_scalar(share[:, :, 0], e2[:, :], 1.0, None, ALU.add).then_inc(*own.up())
                settle()
                v.reciprocal(share[:, :, 0], share[:, :, 0]).then_inc(*own.up())
                settle()
                v.tensor_tensor(share[:, :, 1], share[:, :, 0], e2[:, :], ALU.mult).then_inc(*own.up())
                settle()
                v.tensor_tensor(one_hot[:, :, :, :], one_hot[:, :, :, :], spread(share[:, :, :], 3, 8), ALU.mult).then_inc(*own.up())
                settle()
                v.tensor_tensor(wf[:, :, :], one_hot[:, :, 0, :], one_hot[:, :, 1, :], ALU.add).then_inc(*own.up())
                settle()
                k.wait("vector", e, *used.now(i))
                for g in range(G):
                    v.tensor_tensor(prod[:, g % 2, :, :], py[:, g, :].rearrange("p (x d) -> p x d", x=EXPERTS),
                                    b2[:, :, :], ALU.add).then_inc(*yu.up())
                    k.wait("vector", e, *yu.now(i, g))
                    v.tensor_tensor(prod[:, g % 2, :, :], prod[:, g % 2, :, :], spread(wf[:, g, :], 2, D), ALU.mult).then_inc(*own.up())
                    settle()
                    v.tensor_reduce(y[:, g, :], prod[:, g % 2, :, :].rearrange("p x d -> p d x"), axis=AX.X, op=ALU.add).then_inc(*own.up())
                settle()
                r = k.resid[:, bass.ds(i * G * D, G * D)]
                v.tensor_tensor(r, r, y[:, :, :].rearrange("p g d -> p (g d)"), ALU.add).then_inc(*rd.up())
                own.end()


PER_EXPERTS = 23


def store(k):
    nc = k.nc
    with Stage(k, "store") as st:
        stored = st.sem("out_stored")
        block = st.block()

        @block.sync
        def _(e):
            e.dma_start(k.out.rearrange("b s d -> s b d"), k.resid[:, :].rearrange("s (b d) -> s b d", b=NB)).then_inc(stored, 16)
            e.wait_ge(stored, 16)


def build(nc, ins, out):
    with ExitStack() as ctx:
        k = Core(nc, ctx, ins, out)
        make_constants(k)
        with ExitStack() as t:
            feats = t.enter_context(nc.sbuf_tensor("feats", [C, NB * LEN3], F32))
            lrow = t.enter_context(nc.sbuf_tensor("lrow", [1, NB * LEN3], F32))
            conv_stack(k, feats)
            importance(k, feats, lrow)
            pool_frames(k, feats, lrow)
        with ExitStack() as t:
            xt = t.enter_context(nc.sbuf_tensor("xt", [D + 1, NB * C], F32))
            norm_transpose(k, "norm1", xt)
            odd_attention(k, xt)
        with ExitStack() as t:
            xt = t.enter_context(nc.sbuf_tensor("xt2", [D + 1, NB * C], F32))
            norm_transpose(k, "norm2", xt)
            key_memory(k, xt)
        ccol = ctx.enter_context(nc.sbuf_tensor("ccol", [C, NB], F32))
        shapes = {"v": (NB, C, D), "ka": (NB, C, HID), "qa": (NB, C, HID), "w": (NB, C, 2 * C), "uq": (NB, C, 2, C),
                  "c": (NB, C + 1), "w1t": (NB, C, C), "po": (NB, SC, HID), "g": (NB, C, HID), "h": (NB, C, HID), "e": (NB, C, D)}
        dram = {n: nc.dram_tensor(f"history_{n}", s, F32, kind="Internal").ap() for n, s in shapes.items()}
        with ExitStack() as t:
            fp = t.enter_context(nc.sbuf_tensor("fp", [C, NB, 3 * D + GATES], F32))
            gates = t.enter_context(nc.sbuf_tensor("gates", [C, NB, GATES], F32))
            with ExitStack() as u:
                xt = u.enter_context(nc.sbuf_tensor("xt3", [D + 1, NB * C], F32))
                norm_transpose(k, "norm3", xt)
                gated_features(k, xt, fp, gates)
            scan_weights(k, fp, gates, dram, ccol)
        scan(k, dram)
        scan_outputs(k, dram, ccol)
        with ExitStack() as t:
            xt = t.enter_context(nc.sbuf_tensor("xt4", [D + 1, NB * C], F32))
            norm_transpose(k, "norm4", xt, "m_affine")
            experts(k, xt)
        store(k)


def laid_out(a):
    import numpy as np
    t = lambda n: np.asarray(a["L0_tok_" + n])
    x = np.pad(np.asarray(a["x"])[:, 0, :], ((0, 0), (3, 4)), mode="reflect")
    o = {"x": x[:, :5 * (LEN0 + 1)].reshape(NB, LEN0 + 1, 5).transpose(0, 2, 1)}
    o["conv0"] = t("conv0_w")[:, 0, :].T
    for n in (1, 2, 3):
        o[f"conv{n}"] = t(f"conv{n}_w").transpose(1, 2, 0)
    o["conv_b"] = np.stack([t(f"conv{n}_b") for n in range(4)], 1)
    o["norm_g"] = np.stack([t(f"n{n}_w") for n in range(5)], 1)
    o["norm_b"] = np.stack([t(f"n{n}_b") for n in range(5)], 1)
    o["mlp_w1"] = t("mlp_w1")
    o["mlp_w2"] = t("mlp_w2").reshape(4, C, DMLP).transpose(1, 0, 2)
    o["mlp_w3"] = t("mlp_w3").reshape(4, C).T
    o["mlp_b1"] = t("mlp_b1").reshape(4, C).T
    o["mlp_b2"] = t("mlp_b2").reshape(4, C).T
    o["mlp_b3"] = t("mlp_b3").reshape(1, 1)
    b = lambda n: np.asarray(a["L0_attn_" + n])
    for n in "QKV":
        w = b("W_" + n).transpose(1, 0, 2).reshape(D, HEADS * DH)
        o["a_w" + n.lower()] = np.concatenate([w, b("b_" + n).reshape(1, -1)], 0)
    o["a_wo"] = b("W_O").reshape(2, 128, D).transpose(1, 0, 2)
    o["a_bo"] = b("b_O").reshape(1, D)
    f = lambda n: np.asarray(a["L0_ffn_" + n])
    o["k_wpk"] = f("Wq_pk").T.reshape(16, 32, D).transpose(1, 0, 2)
    o["k_keys"] = f("pk_keys").transpose(3, 0, 2, 1).reshape(32, 16, NKEY)
    o["k_wq"] = f("Wq")
    o["k_wo"] = f("Wo").reshape(4, 128, D).transpose(1, 0, 2)
    o["k_table"] = np.concatenate([f("keys_table"), f("values_table")], 1)
    g = lambda n: np.asarray(a["L1_attn_" + n])
    o["t_wf"] = g("W_fused").T
    o["t_w0"], o["t_p0"] = g("W0"), g("P0")
    for n, w in (("w1", g("W1")), ("p1", g("P1"))):
        o["t_" + n] = w.reshape(2, 128, D).transpose(1, 0, 2)
        o["t_" + n + "t"] = w.T.reshape(2, D // 2, HID).transpose(1, 0, 2)
    h = lambda n: np.asarray(a["L1_ffn_" + n])
    o["m_affine"] = np.stack([h("gamma"), h("beta")], 1)
    o["m_wr"] = np.concatenate([h("Wr"), h("br").reshape(1, EXPERTS)], 0)
    o["m_w1"] = np.concatenate([h("W1").transpose(1, 0, 2), h("b1").reshape(1, EXPERTS, DFF)], 0)
    o["m_w2"] = h("W2").transpose(1, 0, 2)
    o["m_b2"] = h("b2").reshape(1, EXPERTS * D)
    return {n: np.ascontiguousarray(v) for n, v in o.items()}


def kernel(**inputs):
    import concourse.bacc as _bacc
    from concourse import mybir as _mybir
    from concourse.bass_utils import run_bass_kernel_spmd as _run

    nc = _bacc.Bacc("TRN2", target_bir_lowering=False, num_devices=1)
    arrays = laid_out(inputs)
    ins = {n: nc.dram_tensor(n, v.shape, _mybir.dt.from_np(v.dtype), kind="ExternalInput").ap()
           for n, v in arrays.items()}
    out = nc.dram_tensor("out", (NB, C, D), _mybir.dt.float32, kind="ExternalOutput").ap()
    build(nc, ins, out)
    r = _run(nc, [arrays], core_ids=[0])
    return r.results[0]["out"]
```
